# Optimizing a Trainium2 kernel written in Bass

```python
import numpy as np
import jax
import jax.numpy as jnp

def _softmax(x, axis=-1):
    return jax.nn.softmax(x, axis=axis)

def _gelu(x):
    return jax.nn.gelu(x, approximate=True)

def _silu(x):
    return jax.nn.silu(x)

def _sigmoid(x):
    return jax.nn.sigmoid(x)

def _layernorm(x, axis=-1, eps=1e-05):
    m = jnp.mean(x, axis=axis, keepdims=True)
    v = jnp.var(x, axis=axis, keepdims=True)
    return (x - m) / jnp.sqrt(v + eps)

def _scatter_add(tgt, idx, src, axis=0):
    return tgt.at[idx].add(src)

def _segment_sum(src, seg, n):
    return jax.ops.segment_sum(src, seg, n)
kernel_name = 'mk_prb_d1_jaxref_r8_21e11b'

def setup_inputs(seed: int=0):
    np.random.seed(seed)
    _w = jnp.asarray

    def _L0_attn_setup():
        import jax, jax.numpy as jnp
        import numpy as np
        HID, H, B, T = (128, 16, 4, 256)
        D = HID // H
        BETA_MIN, BETA_MAX, EPS = (0.8, 0.999, 1e-06)

        def _rope_cache(T, D):
            inv_freq = 1.0 / 10000.0 ** (jnp.arange(0, D, 2, dtype=jnp.float32) / D)
            t = jnp.arange(T, dtype=jnp.float32)
            freqs = t[:, None] * inv_freq[None, :]
            emb = jnp.concatenate([freqs, freqs], axis=-1)
            return (jnp.cos(emb)[None, :, None, :], jnp.sin(emb)[None, :, None, :])

        def _apply_rope(u, cos, sin):
            u1, u2 = jnp.split(u, 2, axis=-1)
            rot = jnp.concatenate([-u2, u1], axis=-1)
            return u * cos + rot * sin

        def _phi(u):
            return jax.nn.elu(u) + 1.0
        key = jax.random.key(seed)
        ks = jax.random.split(key, 8)
        s = 1.0 / np.sqrt(HID)
        x = jax.random.normal(ks[0], (B, T, HID), dtype=jnp.float32)
        Wq = jax.random.normal(ks[1], (HID, HID), dtype=jnp.float32) * s
        Wk = jax.random.normal(ks[2], (HID, HID), dtype=jnp.float32) * s
        Wv = jax.random.normal(ks[3], (HID, HID), dtype=jnp.float32) * s
        Wb = jax.random.normal(ks[4], (H, HID), dtype=jnp.float32) * s
        bb = jnp.full((H,), float(np.log(0.95 / 0.05)), dtype=jnp.float32)
        Wo = jax.random.normal(ks[5], (HID, HID), dtype=jnp.float32) * s
        bo = jnp.zeros((HID,), dtype=jnp.float32)
        scale = jnp.ones((HID,), dtype=jnp.float32)
        return {'x': x, 'Wq': Wq, 'Wk': Wk, 'Wv': Wv, 'Wb': Wb, 'bb': bb, 'Wo': Wo, 'bo': bo, 'scale': scale}
    _L0_attn_in = _L0_attn_setup()

    def _L0_ffn_setup():
        import jax, jax.numpy as jnp
        import numpy as np
        D = 128
        HQ = 16
        HKV = 4
        G = HQ // HKV
        K = 64
        V = 64
        E = 8
        TOPK = 2
        HID = 256
        CAP_FRAC = 0.125
        EPS = 1e-06

        def _rmsnorm(x, g):
            return x * jax.lax.rsqrt(jnp.mean(x * x, axis=-1, keepdims=True) + EPS) * g

        def _rotary_tables(t, dim):
            thetas = 10000.0 ** (-np.arange(0, dim, 2, dtype=np.float32) / dim)
            ticks = np.outer(np.arange(t, dtype=np.float32), thetas)
            ticks = np.tile(ticks, (1, 2))[None, :, None, :]
            return (jnp.asarray(np.cos(ticks)), jnp.asarray(np.sin(ticks)))

        def _neg_half(x):
            x1, x2 = jnp.split(x, 2, axis=-1)
            return jnp.concatenate([-x2, x1], axis=-1)

        def _attention(x, wq, wk, wv, wo):
            b, t, _ = x.shape
            q = (x @ wq).reshape(b, t, HQ, K)
            k = (x @ wk).reshape(b, t, HKV, K)
            v = (x @ wv).reshape(b, t, HKV, V)
            cos, sin = _rotary_tables(t, K)
            q = q * cos + _neg_half(q) * sin
            k = k * cos + _neg_half(k) * sin
            qg = q.reshape(b, t, G, HKV, K)
            scores = jnp.einsum('btghk,bThk->bghtT', qg, k)
            mask = jnp.tril(jnp.ones((t, t), bool))
            scores = jnp.where(mask, scores, -jnp.inf) / np.float32(np.sqrt(K))
            p = jax.nn.softmax(scores, axis=-1)
            out = jnp.einsum('bghtT,bThv->btghv', p, v).reshape(b, t, HQ * V)
            return out @ wo

        def _moe(x, router_w, router_b, w1, w2, w3):
            b, t, d = x.shape
            n = b * t
            xf = x.reshape(n, d)
            logits = xf @ router_w + router_b
            vals, idx = jax.lax.top_k(logits, TOPK)
            scores = jax.nn.softmax(vals, axis=-1)
            cap = int(np.floor(n * CAP_FRAC))
            oh = jax.nn.one_hot(idx, E, dtype=jnp.float32)
            pos = jnp.cumsum(jnp.cumsum(oh, axis=0), axis=1).astype(jnp.int32)
            emask = oh * (pos < cap)
            tmask = jnp.sum(emask, axis=-1)
            assign = jnp.einsum('tke,e->tk', emask, jnp.arange(E, dtype=jnp.float32)).astype(jnp.int32)
            m = jnp.max(assign, axis=-1)

            def ff(w1e, w2e, w3e):
                h = jax.nn.gelu(xf @ w2e * (xf @ w1e), approximate=False)
                return h @ w3e
            y_all = jax.vmap(ff)(w1, w2, w3)
            y = y_all[m, jnp.arange(n)]
            slot = jnp.where(tmask[..., None] > 0, y[:, None, :], xf[:, None, :])
            out = jnp.einsum('tkD,tk->tD', slot, scores)
            return out.reshape(b, t, d)
        key = jax.random.key(seed)
        ks = jax.random.split(key, 10)
        w = lambda k, shape: jax.random.normal(k, shape, jnp.float32) * 0.02
        return {'x': jax.random.normal(ks[0], (4, 64, D), jnp.float32), 'g1': jnp.ones((D,), jnp.float32), 'g2': jnp.ones((D,), jnp.float32), 'wq': w(ks[1], (D, HQ * K)), 'wk': w(ks[2], (D, HKV * K)), 'wv': w(ks[3], (D, HKV * V)), 'wo': w(ks[4], (HQ * V, D)), 'router_w': w(ks[5], (D, E)), 'router_b': jnp.zeros((E,), jnp.float32), 'w1': w(ks[6], (E, D, HID)), 'w2': w(ks[7], (E, D, HID)), 'w3': w(ks[8], (E, HID, D))}
    _L0_ffn_in = _L0_ffn_setup()
    _d = {'L0_attn_x': _L0_attn_in['x'], 'L0_attn_Wq': _L0_attn_in['Wq'], 'L0_attn_Wk': _L0_attn_in['Wk'], 'L0_attn_Wv': _L0_attn_in['Wv'], 'L0_attn_Wb': _L0_attn_in['Wb'], 'L0_attn_bb': _L0_attn_in['bb'], 'L0_attn_Wo': _L0_attn_in['Wo'], 'L0_attn_bo': _L0_attn_in['bo'], 'L0_attn_scale': _L0_attn_in['scale'], 'L0_ffn_g1': _L0_ffn_in['g1'], 'L0_ffn_g2': _L0_ffn_in['g2'], 'L0_ffn_wq': _L0_ffn_in['wq'], 'L0_ffn_wk': _L0_ffn_in['wk'], 'L0_ffn_wv': _L0_ffn_in['wv'], 'L0_ffn_wo': _L0_ffn_in['wo'], 'L0_ffn_router_w': _L0_ffn_in['router_w'], 'L0_ffn_router_b': _L0_ffn_in['router_b'], 'L0_ffn_w1': _L0_ffn_in['w1'], 'L0_ffn_w2': _L0_ffn_in['w2'], 'L0_ffn_w3': _L0_ffn_in['w3']}
    _x0 = _d['L0_attn_x']
    _d['L0_attn_x'] = jax.random.normal(jax.random.fold_in(jax.random.key(seed), 1), (8, 512, 128), dtype=_x0.dtype)
    del _x0
    return _d

def reference(L0_attn_x, L0_attn_Wq, L0_attn_Wk, L0_attn_Wv, L0_attn_Wb, L0_attn_bb, L0_attn_Wo, L0_attn_bo, L0_attn_scale, L0_ffn_g1, L0_ffn_g2, L0_ffn_wq, L0_ffn_wk, L0_ffn_wv, L0_ffn_wo, L0_ffn_router_w, L0_ffn_router_b, L0_ffn_w1, L0_ffn_w2, L0_ffn_w3):

    def _L0_attn_ref(x, Wq, Wk, Wv, Wb, bb, Wo, bo, scale):
        import jax, jax.numpy as jnp
        import numpy as np
        HID, H, B, T = (128, 16, 4, 256)
        D = HID // H
        BETA_MIN, BETA_MAX, EPS = (0.8, 0.999, 1e-06)

        def _rope_cache(T, D):
            inv_freq = 1.0 / 10000.0 ** (jnp.arange(0, D, 2, dtype=jnp.float32) / D)
            t = jnp.arange(T, dtype=jnp.float32)
            freqs = t[:, None] * inv_freq[None, :]
            emb = jnp.concatenate([freqs, freqs], axis=-1)
            return (jnp.cos(emb)[None, :, None, :], jnp.sin(emb)[None, :, None, :])

        def _apply_rope(u, cos, sin):
            u1, u2 = jnp.split(u, 2, axis=-1)
            rot = jnp.concatenate([-u2, u1], axis=-1)
            return u * cos + rot * sin

        def _phi(u):
            return jax.nn.elu(u) + 1.0
        Bx, Tx, hid = x.shape
        q = (x @ Wq.T).reshape(Bx, Tx, H, D)
        k = (x @ Wk.T).reshape(Bx, Tx, H, D)
        v = (x @ Wv.T).reshape(Bx, Tx, H, D)
        beta = jax.nn.sigmoid(x @ Wb.T + bb)
        beta = jnp.clip(beta, BETA_MIN, BETA_MAX).astype(jnp.float32)
        cos, sin = _rope_cache(Tx, D)
        phi_q = _phi(_apply_rope(q, cos, sin)).astype(jnp.float32)
        phi_k = _phi(_apply_rope(k, cos, sin)).astype(jnp.float32)
        v32 = v.astype(jnp.float32)
        pq = jnp.swapaxes(phi_q, 0, 1)
        pk = jnp.swapaxes(phi_k, 0, 1)
        vv = jnp.swapaxes(v32, 0, 1)
        bt = jnp.swapaxes(beta, 0, 1)

        def step(carry, inp):
            S, z = carry
            pqt, pkt, vt, b = inp
            S = b[..., None, None] * S + pkt[..., :, None] * vt[..., None, :]
            z = b[..., None] * z + pkt
            num = jnp.einsum('bhd,bhde->bhe', pqt, S)
            den = jnp.einsum('bhd,bhd->bh', pqt, z) + EPS
            return ((S, z), num / den[..., None])
        S0 = jnp.zeros((Bx, H, D, D), jnp.float32)
        z0 = jnp.zeros((Bx, H, D), jnp.float32)
        _, outs = jax.lax.scan(step, (S0, z0), (pq, pk, vv, bt))
        attn = jnp.swapaxes(outs, 0, 1).reshape(Bx, Tx, hid).astype(x.dtype)
        y = attn @ Wo.T + bo
        h = x + y
        rms = jnp.sqrt(jnp.mean(h * h, axis=-1, keepdims=True) + EPS)
        return h / rms * scale

    def _L0_ffn_ref(x, g1, g2, wq, wk, wv, wo, router_w, router_b, w1, w2, w3):
        import jax, jax.numpy as jnp
        import numpy as np
        D = 128
        HQ = 16
        HKV = 4
        G = HQ // HKV
        K = 64
        V = 64
        E = 8
        TOPK = 2
        HID = 256
        CAP_FRAC = 0.125
        EPS = 1e-06

        def _rmsnorm(x, g):
            return x * jax.lax.rsqrt(jnp.mean(x * x, axis=-1, keepdims=True) + EPS) * g

        def _rotary_tables(t, dim):
            thetas = 10000.0 ** (-np.arange(0, dim, 2, dtype=np.float32) / dim)
            ticks = np.outer(np.arange(t, dtype=np.float32), thetas)
            ticks = np.tile(ticks, (1, 2))[None, :, None, :]
            return (jnp.asarray(np.cos(ticks)), jnp.asarray(np.sin(ticks)))

        def _neg_half(x):
            x1, x2 = jnp.split(x, 2, axis=-1)
            return jnp.concatenate([-x2, x1], axis=-1)

        def _attention(x, wq, wk, wv, wo):
            b, t, _ = x.shape
            q = (x @ wq).reshape(b, t, HQ, K)
            k = (x @ wk).reshape(b, t, HKV, K)
            v = (x @ wv).reshape(b, t, HKV, V)
            cos, sin = _rotary_tables(t, K)
            q = q * cos + _neg_half(q) * sin
            k = k * cos + _neg_half(k) * sin
            qg = q.reshape(b, t, G, HKV, K)
            scores = jnp.einsum('btghk,bThk->bghtT', qg, k)
            mask = jnp.tril(jnp.ones((t, t), bool))
            scores = jnp.where(mask, scores, -jnp.inf) / np.float32(np.sqrt(K))
            p = jax.nn.softmax(scores, axis=-1)
            out = jnp.einsum('bghtT,bThv->btghv', p, v).reshape(b, t, HQ * V)
            return out @ wo

        def _moe(x, router_w, router_b, w1, w2, w3):
            b, t, d = x.shape
            n = b * t
            xf = x.reshape(n, d)
            logits = xf @ router_w + router_b
            vals, idx = jax.lax.top_k(logits, TOPK)
            scores = jax.nn.softmax(vals, axis=-1)
            cap = int(np.floor(n * CAP_FRAC))
            oh = jax.nn.one_hot(idx, E, dtype=jnp.float32)
            pos = jnp.cumsum(jnp.cumsum(oh, axis=0), axis=1).astype(jnp.int32)
            emask = oh * (pos < cap)
            tmask = jnp.sum(emask, axis=-1)
            assign = jnp.einsum('tke,e->tk', emask, jnp.arange(E, dtype=jnp.float32)).astype(jnp.int32)
            m = jnp.max(assign, axis=-1)

            def ff(w1e, w2e, w3e):
                h = jax.nn.gelu(xf @ w2e * (xf @ w1e), approximate=False)
                return h @ w3e
            y_all = jax.vmap(ff)(w1, w2, w3)
            y = y_all[m, jnp.arange(n)]
            slot = jnp.where(tmask[..., None] > 0, y[:, None, :], xf[:, None, :])
            out = jnp.einsum('tkD,tk->tD', slot, scores)
            return out.reshape(b, t, d)
        h = x + _attention(_rmsnorm(x, g1), wq, wk, wv, wo)
        return h + _moe(_rmsnorm(h, g2), router_w, router_b, w1, w2, w3)
    x = L0_attn_x
    xn = _layernorm(x, axis=-1)
    x = x + _L0_attn_ref(xn, L0_attn_Wq, L0_attn_Wk, L0_attn_Wv, L0_attn_Wb, L0_attn_bb, L0_attn_Wo, L0_attn_bo, L0_attn_scale) + _L0_ffn_ref(xn, L0_ffn_g1, L0_ffn_g2, L0_ffn_wq, L0_ffn_wk, L0_ffn_wv, L0_ffn_wo, L0_ffn_router_w, L0_ffn_router_b, L0_ffn_w1, L0_ffn_w2, L0_ffn_w3)
    return x

_drawn_inputs = setup_inputs


def setup_inputs(seed=0):
    import zlib

    import numpy as np

    out = dict(_drawn_inputs(seed))
    spreads = {'L0_attn_bb': (2.944438934326172, 0.6),
     'L0_attn_bo': (0.0, 0.27),
     'L0_attn_scale': (1.0, 0.2),
     'L0_ffn_g1': (1.0, 0.6),
     'L0_ffn_g2': (1.0, 0.2),
     'L0_ffn_router_b': (0.0, 0.1)}
    factors = {'L0_attn_Wq': 5.974,
     'L0_attn_Wk': 3.225,
     'L0_attn_Wb': 7.74,
     'L0_ffn_wq': 8.0,
     'L0_ffn_wk': 8.0,
     'L0_ffn_wv': 3.63,
     'L0_ffn_wo': 4.138,
     'L0_ffn_w1': 8.0,
     'L0_ffn_w2': 8.0,
     'L0_ffn_w3': 8.0}
    for name, (base, spread) in spreads.items():
        noise = np.random.default_rng([zlib.crc32(name.encode()), seed]).standard_normal(out[name].shape)
        drawn = base * np.exp(spread * noise) if base else spread * noise
        out[name] = jnp.asarray(drawn.astype(out[name].dtype))
    for name, factor in factors.items():
        out[name] = (out[name] * factor).astype(out[name].dtype)
    return out
```

```python
import concourse.bass as bass
from concourse import mybir
from contextlib import ExitStack

F32 = mybir.dt.float32
F32R = mybir.dt.float32r
U32 = mybir.dt.uint32
ALU = mybir.AluOpType
ACT = mybir.ActivationFunctionType
AX = mybir.AxisListType

B, T, D = 8, 512, 128
P = 128
NT = T // P
LH, LD = 16, 8
LV = LD + 1
HQ, HKV, HD = 16, 4, 64
G = HQ // HKV
E, HID = 8, 256
CAP = (B * T) // 8
EPS = 1e-6
LN_EPS = 1e-5

CONST = [("ident", P), ("mask_qk", P), ("mask_kq", P), ("upto", P), ("ones", P), ("quad", G),
         ("diag", LH * LV), ("iota", E), ("less", E),
         ("cos_l", T), ("sin_l", T), ("cos_s", T), ("sin_s", T)]
COFF = {}
_at = 0
for _n, _w in CONST:
    COFF[_n] = (_at, _w)
    _at += _w
NCONST = _at
ROWS = [("bb", LH), ("bo", D), ("scale", D), ("g2", D), ("router_b", E)]
ROFF = {}
_at = 0
for _n, _w in ROWS:
    ROFF[_n] = (_at, _w)
    _at += _w
NROWS = _at


def attention_kernel(nc, x, w_lin, w_lout, w_att, w_out, w_up, w_down, w_router, g1, rows, consts, out):
    ctx = ExitStack()
    with ctx:
        def sb(name, shape, dt=F32):
            return ctx.enter_context(nc.sbuf_tensor(name, shape, dt))

        def sem(name):
            return ctx.enter_context(nc.semaphore(name))

        c_all = sb("c_all", [P, NCONST])
        rows_sb = sb("rows_sb", [P, NROWS])
        g1_sb = sb("g1_sb", [P, 1])
        wlout = sb("wlout", [P, D])
        wout = sb("wout", [P, HQ * HD // P, D])
        wup = sb("wup", [P, E, 2 * HID])
        wdown = sb("wdown", [P, E, 2, D])
        wrt = sb("wrt", [P, E])

        def const(name):
            a, w = COFF[name]
            return c_all[:, a:a + w]

        def row(name):
            a, w = ROFF[name]
            return rows_sb[:, a:a + w]

        cr = sb("cr", [P, 3 * P], F32R)
        ident_r, mask_qk_r, mask_kq_r = cr[:, 0:P], cr[:, P:2 * P], cr[:, 2 * P:3 * P]

        def pick_row(n, r):
            return ident_r[0:n, r:r + 1].to_broadcast([n, P])

        NW = 2 * HQ * HD + 4 * HKV * HD + HKV * HD
        watt_h = sb("watt_h", [P, NW], F32R)
        watt_l = sb("watt_l", [P, NW], F32R)
        wlin_h = sb("wlin_h", [P, 5 * D + LH], F32R)
        wlin_l = sb("wlin_l", [P, 5 * D + LH], F32R)

        xt = sb("xt", [P, NT, D])
        xn = sb("xn", [P, NT, D])
        xg = sb("xg", [P, NT, D])
        sq = sb("sq", [P, NT, D])
        st = sb("st", [P, 10, NT])
        xn_h = sb("xn_h", [P, T], F32R)
        xn_l = sb("xn_l", [P, T], F32R)
        xg_h = sb("xg_h", [P, T], F32R)
        xg_l = sb("xg_l", [P, T], F32R)
        ql = sb("ql", [P, T])
        kl = sb("kl", [P, T])
        dec = sb("dec", [P, 2, T])
        zb = sb("zb", [P, 4, NT, LH])
        qm = sb("qm", [P, 2, G, P])
        v9 = sb("v9", [P, NT, LH, LV])
        kt = sb("kt", [P, D])
        state = sb("state", [P, LH * LV])
        stt = sb("stt", [P, LH * LV])
        rden_l = sb("rden_l", [P, LH])
        kh = sb("kh", [P, HKV, T], F32R)
        klo = sb("klo", [P, HKV, T], F32R)
        qs = sb("qs", [P, HQ, T], F32R)
        v1 = sb("v1", [P, NT, HKV, HD + 2])
        negm = sb("negm", [P, 2, NT, G])
        half = sb("half", [P, NT])
        negmT = sb("negmT", [G, 2, T], F32R)
        NPT = P * (NT * (NT + 1) // 2)
        pt = sb("pt", [P, 2, NPT])
        rden = sb("rden", [P, 2, NT])
        osb = sb("osb", [P, NT, HQ * HD])
        stage = osb[:, :, :].rearrange("p n e -> p (n e)")
        watt, wlin = stage[:, 0:NW], stage[:, NW:NW + 5 * D + LH]

        def part(ap, i, shape):
            a = ap[:, 2 * T * i:2 * T * (i + 1)]
            return a.rearrange("p (a b) -> p a b", a=shape[0])

        r_a, r_b, rot = (part(stage, i, (2, T)) for i in range(3))
        xgt = stage[:, 6 * T:7 * T]
        xm, hc, hp, hg = (part(stage, i, (2, T)) for i in range(4))
        area = pt[:, :, :].rearrange("p a n -> p (a n)")
        r_m, r_e = (part(area, i, (2, T)) for i in range(2))
        oT = area[:, 0:16 * P].rearrange("p (a c t) -> p a c t", a=2, c=8)
        bet = [a.rearrange("p (n h d) -> p n h d", n=NT, h=LH) for a in (stage[:, 7 * T:8 * T], area[:, 4 * T:5 * T])]
        am = area[:, 0:LH * P].rearrange("p (h t) -> p h t", h=LH)
        h1 = sb("h1", [P, NT, D])
        xf = xg
        xfT = sb("xfT", [P, T])
        lg = sb("lg", [P, 2, NT, E])
        mx = sb("mx", [P, 2, NT])
        mi = sb("mi", [P, NT])
        eq = sb("eq", [P, NT, E])
        oh = sb("oh", [P, NT, 2, E])
        ohc = sb("ohc", [P, NT, 2, E])
        carry = sb("carry", [P, 2, E])
        pos = sb("pos", [P, NT, 2, E])
        em = sb("em", [P, NT, 2, E])
        emi = sb("emi", [P, NT, 2, E])
        tk = sb("tk", [P, 10, NT, 2])
        pick = sb("pick", [P, NT, E])
        pickT = sb("pickT", [E, T], F32R)
        ob = sb("ob", [P, NT, D])
        tmp = sb("tmp", [P, NT, D])
        yl = sb("yl", [P, NT, D])
        at_l, atT = tmp, xfT

        bank = [ctx.enter_context(nc.psum_tensor(f"bank{i}", [P, 512], F32)) for i in range(8)]

        s_load = sem("s_load")
        s_x = sem("s_x")
        s_keep = sem("s_keep")
        s_out = sem("s_out")
        s_wsplit = sem("s_wsplit")
        s_const = sem("s_const")
        s_var = sem("s_var")
        s_rstd = sem("s_rstd")
        s_norm = sem("s_norm")
        s_pd = sem("s_pd")
        s_pdfree = sem("s_pdfree")
        s_pa = sem("s_pa")
        s_pafree = sem("s_pafree")
        s_hi = sem("s_hi")
        s_lo = sem("s_lo")
        s_elu = sem("s_elu")
        s_eluexp = sem("s_eluexp")
        s_full = sem("s_full")
        s_lin = sem("s_lin")
        s_qm = sem("s_qm")
        s_beta = sem("s_beta")
        s_zb = sem("s_zb")
        s_zbe = sem("s_zbe")
        s_sc = sem("s_sc")
        s_mx = sem("s_mx")
        s_mt = sem("s_mt")
        s_mtc = sem("s_mtc")
        s_ex = sem("s_ex")
        s_p = sem("s_p")
        s_pv = sem("s_pv")
        s_o = sem("s_o")
        s_ot = sem("s_ot")
        s_otc = sem("s_otc")
        s_kt = sem("s_kt")
        s_ktc = sem("s_ktc")
        s_as = sem("s_as")
        s_am = sem("s_am")
        s_ao = sem("s_ao")
        s_aod = sem("s_aod")
        s_su = sem("s_su")
        s_st = sem("s_st")
        s_at = sem("s_at")
        s_atc = sem("s_atc")
        s_y = sem("s_y")
        s_xf = sem("s_xf")
        s_xft = sem("s_xft")
        s_xftc = sem("s_xftc")
        s_lg = sem("s_lg")
        s_dif = sem("s_dif")
        s_dexp = sem("s_dexp")
        s_oh = sem("s_oh")
        s_pos = sem("s_pos")
        s_pick = sem("s_pick")
        s_pkt = sem("s_pkt")
        s_pktc = sem("s_pktc")
        s_pb = sem("s_pb")
        s_xm = sem("s_xm")
        s_up = sem("s_up")
        s_hc = sem("s_hc")
        s_hp = sem("s_hp")
        s_hg = sem("s_hg")
        s_dn = sem("s_dn")
        s_chain = sem("s_chain")
        s_ob = sem("s_ob")
        s_pe_end = sem("s_pe_end")
        s_act_end = sem("s_act_end")
        s_dve_end = sem("s_dve_end")
        s_pool_end = sem("s_pool_end")

        s_half = sem("s_half")
        s_setup = sem("s_setup")
        s_yl = sem("s_yl")

        block = ctx.enter_context(nc.Block())
        xv = x.rearrange("b (n p) d -> b p n d", p=P)
        ov = out.rearrange("b (n p) d -> b p n d", p=P)
        NLOAD = 10
        ND = 33
        NFULL = 1 + HKV + HQ // 2
        NSPLIT = NFULL + 1
        CHAIN = 91

        WQ, WQX, WK, WKX, WV = 0, 1024, 2048, 2560, 3072

        def bcast(ap, n):
            return ap.unsqueeze(2).to_broadcast([ap.shape[0], ap.shape[1], n])

        def end_of_batch_before(eng, b):
            eng.wait_ge(s_pe_end, b + 1)
            eng.wait_ge(s_act_end, b + 1)
            eng.wait_ge(s_dve_end, b + 1)

        POFF = [sum(T - P * i for i in range(j)) for j in range(NT)]
        PIECES = [[0], [1], [2, 3]]

        @block.sync
        def _(sp):
            sp.dma_start(xt[:, :, :], xv[0]).then_inc(s_x, 16)
            sp.dma_start(ob[:, :, :], xv[0]).then_inc(s_keep, 16)
            sp.dma_start(c_all[:, :], consts).then_inc(s_load, 16)
            sp.dma_start(rows_sb[:, :], rows).then_inc(s_load, 16)
            sp.dma_start(g1_sb[:, :], g1).then_inc(s_load, 16)
            sp.dma_start(wlin[:, :], w_lin).then_inc(s_load, 16)
            sp.dma_start(watt[:, :], w_att).then_inc(s_load, 16)
            sp.dma_start(wlout[:, :], w_lout).then_inc(s_load, 16)
            sp.dma_start(wout[:, :, :], w_out.rearrange("(c p) n -> p c n", p=P)).then_inc(s_load, 16)
            sp.dma_start(wup[:, :, :], w_up).then_inc(s_load, 16)
            sp.dma_start(wdown[:, :, :, :], w_down.rearrange("e (c p) n -> p e c n", p=P)).then_inc(s_load, 16)
            sp.dma_start(wrt[:, :], w_router).then_inc(s_load, 16)
            with sp.Fori(1, B) as b:
                sp.wait_ge(s_norm, 2 * b)
                sp.dma_start(xt[:, :, :], xv[b]).then_inc(s_x, 16)
                sp.wait_ge(s_ob, b)
                sp.dma_start(ov[b - 1], ob[:, :, :]).then_inc(s_out, 16)
                sp.wait_ge(s_out, 16 * b)
                sp.dma_start(ob[:, :, :], xv[b]).then_inc(s_keep, 16)
            sp.wait_ge(s_ob, B)
            sp.dma_start(ov[B - 1], ob[:, :, :]).then_inc(s_out, 16)
            sp.wait_ge(s_out, 16 * B)

        ROOTS = [(2, 3), (4, 5), (6, 7), (8, 9)]

        @block.gpsimd
        def _(pool):
            nc.gpsimd.memset(half[:, :], -0.5).then_inc(s_half, 1)
            pool.wait_ge(s_half, 1)
            with pool.Fori(0, B) as b:
                for r, (i, o) in enumerate(ROOTS):
                    pool.wait_ge(s_var, b * 4 + r + 1)
                    nc.gpsimd.tensor_tensor(st[:, o, :], st[:, i, :], half[:, :], ALU.pow).then_inc(s_rstd, 1)

        @block.tensor
        def _(pe):
            pe.wait_ge(s_const, 1)
            pe.wait_ge(s_wsplit, 1)
            pe.wait_ge(s_load, 16 * NLOAD)
            pe.nop().then_inc(s_pe_end, 1)

            def split_product(out_, lh, ll, rh, rl):
                nc.tensor.matmul(out_, lh, rh, start=True, stop=False)
                nc.tensor.matmul(out_, lh, rl, start=False, stop=False)
                return nc.tensor.matmul(out_, ll, rh, start=False, stop=True)

            with pe.Fori(0, B) as b:
                end_of_batch_before(pe, b)
                nd = [0]

                def to_dve():
                    i = nd[0]
                    nd[0] += 1
                    if i >= 7:
                        pe.wait_ge(s_pdfree, b * (ND - 3) + i - 6)
                    elif i >= 4:
                        pe.wait_ge((s_lo, s_full, s_zb)[i - 4], b * (NSPLIT, NFULL, 1)[i - 4] + 1)
                    return bank[i % 4]

                def tile(ap, n):
                    return ap[:, n * P:(n + 1) * P]

                bk = to_dve()
                pe.wait_ge(s_norm, b * 2 + 1)
                for n in range(NT):
                    last = nc.tensor.transpose(tile(bk, n), xn[:, n, :], const("ident"))
                last.then_inc(s_pd, 1)
                bk = to_dve()
                pe.wait_ge(s_norm, b * 2 + 2)
                for n in range(NT):
                    last = nc.tensor.transpose(tile(bk, n), xg[:, n, :], const("ident"))
                last.then_inc(s_pd, 1)
                bk = to_dve()
                pe.wait_ge(s_lo, b * NSPLIT + 1)
                for n in range(NT):
                    last = split_product(bk[:, n * LH:(n + 1) * LH], tile(xn_h, n), tile(xn_l, n),
                                         wlin_h[:, 5 * D:], wlin_l[:, 5 * D:])
                last.then_inc(s_pd, 1)
                for i in range(4):
                    bk = to_dve()
                    w = slice(i * D, (i + 1) * D)
                    split_product(bk[:, :], wlin_h[:, w], wlin_l[:, w], xn_h[:, :], xn_l[:, :])\
                        .then_inc(s_pd, 1)
                for n in range(NT):
                    last = split_product(tile(bank[4], n), tile(xn_h, n), tile(xn_l, n),
                                         wlin_h[:, 4 * D:5 * D], wlin_l[:, 4 * D:5 * D])
                last.then_inc(s_pa, 1)
                pe.wait_ge(s_lo, b * NSPLIT + 2)
                for i in range(2):
                    if i == 1:
                        pe.wait_ge(s_pafree, b * 3 + 1)
                    bk = bank[5 - i]
                    for k in range(2):
                        n = 2 * i + k
                        last = split_product(bk[:, k * 256:(k + 1) * 256], tile(xg_h, n), tile(xg_l, n),
                                             watt_h[:, WV:WV + 256], watt_l[:, WV:WV + 256])
                    last.then_inc(s_pa, 1)
                for a, ax, k in [(WK, WKX, HKV), (WQ, WQX, HQ // 2)]:
                    for i in range(k):
                        for o in (a + i * P, ax + i * P):
                            bk = to_dve()
                            split_product(bk[:, :], watt_h[:, o:o + P], watt_l[:, o:o + P],
                                          xg_h[:, :], xg_l[:, :]).then_inc(s_pd, 1)
                pe.wait_ge(s_beta, b + 1)
                for i in range(2):
                    bk = to_dve()
                    for n in range(NT):
                        last = nc.tensor.matmul(tile(bk, n), bet[i][:, n, :, :].rearrange("p h d -> p (h d)"), const("ident"),
                                                start=True, stop=True)
                    last.then_inc(s_pd, 1)
                assert nd[0] == ND

                def max_scores(h, g):
                    n = h * G + g
                    for qt in range(NT):
                        u = n * NT + qt
                        if u >= 2:
                            pe.wait_ge(s_mx, b * 64 + u - 1)
                        bk = bank[u % 2]
                        w = (qt + 1) * P
                        nc.tensor.matmul(bk[:, 0:w], tile(qs[:, n, :], qt), kh[:, h, 0:w], start=True, stop=False)
                        nc.tensor.matmul(bk[:, w - P:w], ident_r, mask_qk_r, start=False, stop=True)\
                            .then_inc(s_sc, 1)

                def turn_max(h):
                    pe.wait_ge(s_mx, b * 64 + 16 * (h + 1))
                    if h >= 1:
                        pe.wait_ge(s_mtc, b * HKV + h)
                    for qt in range(NT):
                        last = nc.tensor.transpose(bank[7][0:G, qt * P:(qt + 1) * P], negm[:, h % 2, qt, :],
                                                   const("ident"))
                    last.then_inc(s_mt, 1)

                def exp_scores(h, g):
                    n = h * G + g
                    for i, js in enumerate(PIECES):
                        c = n * 3 + i
                        if c >= 3:
                            pe.wait_ge(s_p, b * 48 + c - 2)
                        for j in js:
                            o = POFF[j] - POFF[js[0]]
                            w = T - P * j
                            dst = bank[2 + i][:, o:o + w]
                            nc.tensor.matmul(dst, tile(kh[:, h, :], j), qs[:, n, j * P:], start=True, stop=False)
                            nc.tensor.matmul(dst, tile(klo[:, h, :], j), qs[:, n, j * P:], start=False, stop=False)
                            nc.tensor.matmul(dst, pick_row(G, g), negmT[:, h % 2, j * P:], start=False, stop=False)
                            last = nc.tensor.matmul(bank[2 + i][:, o:o + P], ident_r, mask_kq_r,
                                                    start=False, stop=True)
                        last.then_inc(s_ex, 1)

                def head_out(n):
                    h = n // G
                    pe.wait_ge(s_p, b * 48 + 3 * (n + 1))
                    if n >= 2:
                        pe.wait_ge(s_o, b * HQ + n - 1)
                    for qt in range(NT):
                        for j in range(qt + 1):
                            o = POFF[j] + (qt - j) * P
                            last = nc.tensor.matmul(bank[5 + n % 2][:, qt * (HD + 1):(qt + 1) * (HD + 1)],
                                                    pt[:, n % 2, o:o + P], v1[:, j, h, 0:HD + 1],
                                                    start=(j == 0), stop=(j == qt))
                    last.then_inc(s_pv, 1)

                pe.wait_ge(s_lo, b * NSPLIT + NSPLIT)
                pe.wait_ge(s_pdfree, (b + 1) * (ND - 3))
                pe.wait_ge(s_pafree, b * 3 + 3)
                for g in range(G):
                    max_scores(0, g)
                turn_max(0)
                for h in range(HKV):
                    pe.wait_ge(s_mtc, b * HKV + h + 1)
                    for g in range(G):
                        if h + 1 < HKV:
                            max_scores(h + 1, g)
                        exp_scores(h, g)
                        if h * G + g >= 1:
                            head_out(h * G + g - 1)
                    if h + 1 < HKV:
                        turn_max(h + 1)
                head_out(HQ - 1)
                for qt in range(NT):
                    if qt == 0:
                        pe.wait_ge(s_o, b * HQ + HQ)
                    for i in range(2):
                        u = qt * 2 + i
                        if u >= 2:
                            pe.wait_ge(s_otc, b * 8 + u - 1)
                        for c in range(4):
                            o = (i * 4 + c) * P
                            last = nc.tensor.transpose(tile(bank[u % 2], c), osb[:, qt, o:o + P], const("ident"))
                        last.then_inc(s_ot, 1)
                    pe.wait_ge(s_otc, b * 8 + 2 * (qt + 1))
                    for c in range(8):
                        last = nc.tensor.matmul(tile(bank[3], qt), oT[:, qt % 2, c, :], wout[:, c, :],
                                                start=(c == 0), stop=(c == 7))
                last.then_inc(s_y, 1)
                pe.wait_ge(s_lin, b + 1)
                for c in range(NT):
                    if c >= 1:
                        pe.wait_ge(s_ktc, b * NT + c)
                    nc.tensor.transpose(bank[5][:, 0:P], tile(kl, c), const("ident")).then_inc(s_kt, 1)
                    pe.wait_ge(s_qm, b * NT + c + 1)
                    for q in range(4):
                        u = c * 4 + q
                        if u >= 2:
                            pe.wait_ge(s_am, b * 16 + u - 1)
                        r = slice(32 * q, 32 * q + 32)
                        nc.tensor.matmul(bank[6 + u % 2][:, :], kl[r, c * P:(c + 1) * P],
                                         qm[r, c % 2, :, :].rearrange("p g t -> p (g t)"),
                                         start=True, stop=True).then_inc(s_as, 1)
                    pe.wait_ge(s_st, b * (NT + 1) + c + 1)
                    nc.tensor.matmul(bank[0][:, 0:LH * LV], tile(ql, c), state[:, :], start=True, stop=False,
                                     skip_group_check=True)
                    pe.wait_ge(s_am, b * 16 + 4 * (c + 1))
                    for hd in range(LH):
                        last = nc.tensor.matmul(bank[0][:, hd * LV:(hd + 1) * LV], am[:, hd, :],
                                                v9[:, c, hd, :], start=False, stop=True, skip_group_check=True)
                    last.then_inc(s_ao, 1)
                    pe.wait_ge(s_ktc, b * NT + c + 1)
                    nc.tensor.matmul(bank[1][:, 0:LH * LV], kt[:, :], v9[:, c, :, :].rearrange("p h e -> p (h e)"),
                                     start=True, stop=True).then_inc(s_su, 1)
                    pe.wait_ge(s_aod, b * NT + c + 1)
                for n in range(NT):
                    last = nc.tensor.transpose(tile(bank[2], n), at_l[:, n, :], const("ident"))
                last.then_inc(s_at, 1)
                pe.wait_ge(s_atc, b + 1)
                for n in range(NT):
                    last = nc.tensor.matmul(tile(bank[4], n), tile(atT, n), wlout[:, :], start=True, stop=True)
                last.then_inc(s_y, 1)
                pe.wait_ge(s_xf, b + 1)
                for n in range(NT):
                    last = nc.tensor.transpose(tile(bank[0], n), xf[:, n, :], const("ident"))
                last.then_inc(s_xft, 1)
                pe.wait_ge(s_xftc, b + 1)
                pe.wait_ge(s_st, (b + 1) * (NT + 1))
                for n in range(NT):
                    last = nc.tensor.matmul(bank[1][:, n * E:(n + 1) * E], tile(xfT, n), wrt[:, :],
                                            start=True, stop=True)
                last.then_inc(s_lg, 1)
                pe.wait_ge(s_oh, b + 1)
                for n in range(NT):
                    dst = bank[2][:, n * 2 * E:(n + 1) * 2 * E]
                    nc.tensor.matmul(dst, const("upto"), oh[:, n, :, :].rearrange("p k e -> p (k e)"),
                                     start=True, stop=False)
                    last = nc.tensor.matmul(dst, const("ones"), ohc[:, n, :, :].rearrange("p k e -> p (k e)"),
                                            start=False, stop=True)
                last.then_inc(s_pos, 1)
                pe.wait_ge(s_pick, b + 1)
                for n in range(NT):
                    last = nc.tensor.transpose(bank[3][0:E, n * P:(n + 1) * P], pick[:, n, :], const("ident"))
                last.then_inc(s_pkt, 1)

                def spread(e):
                    if e >= 2:
                        pe.wait_ge(s_xm, b * E + e - 1)
                    nc.tensor.matmul(bank[4 + e % 2][:, :], pick_row(E, e), pickT[:, :], start=True, stop=True)\
                        .then_inc(s_pb, 1)

                def up(v):
                    e, c = v // 2, v % 2
                    pe.wait_ge(s_xm, b * E + e + 1)
                    if v >= 2:
                        pe.wait_ge(s_hp, b * 16 + v - 1)
                    for i in range(2):
                        o = i * HID + c * P
                        last = nc.tensor.matmul(bank[v % 2 * 2 + i][:, :], wup[:, e, o:o + P], xm[:, e % 2, :],
                                                start=True, stop=True)
                    last.then_inc(s_up, 1)

                def down(v):
                    e, c = v // 2, v % 2
                    pe.wait_ge(s_hg, b * 16 + v + 1)
                    for n in range(NT):
                        last = nc.tensor.matmul(tile(bank[6], n), tile(hg[:, v % 2, :], n), wdown[:, e, c, :],
                                                start=(v == 0 and n == 0), stop=(v == 15), skip_group_check=True)
                    last.then_inc(s_dn, 1)

                pe.wait_ge(s_pktc, b + 1)
                pe.wait_ge(s_yl, b + 1)
                spread(0)
                for v in range(2 * E):
                    if v % 2 == 0 and v // 2 + 1 < E:
                        spread(v // 2 + 1)
                    up(v)
                    if v >= 1:
                        down(v - 1)
                down(2 * E - 1)
                pe.nop().then_inc(s_pe_end, 1)

        @block.scalar
        def _(act):
            act.wait_ge(s_load, 16 * NLOAD)
            nc.scalar.activation(watt_h[:, :], watt[:, :], ACT.Copy)
            nc.scalar.activation(wlin_h[:, :], wlin[:, :], ACT.Copy).then_inc(s_wsplit, 1)
            act.nop().then_inc(s_act_end, 1)
            with act.Fori(0, B) as b:
                end_of_batch_before(act, b)
                act.wait_ge(s_pd, b * ND + 1)
                nc.scalar.activation(xn_h[:, :], bank[0][:, :], ACT.Copy).then_inc(s_hi, 1)
                act.wait_ge(s_full, b * NFULL + 1)
                nc.scalar.activation(xg_h[:, :], xgt[:, :], ACT.Copy).then_inc(s_hi, 1)
                act.wait_ge(s_zb, b + 1)
                nc.scalar.activation(zb[:, 1], zb[:, 0], ACT.Exp, scale=-1.0).then_inc(s_zbe, 1)
                act.wait_ge(s_pa, b * 3 + 1)
                nc.scalar.activation(v9[:, :, :, 0:LD],
                                     bank[4][:, :].rearrange("p (n h d) -> p n h d", n=NT, h=LH), ACT.Copy)\
                    .then_inc(s_pafree, 1)
                for i in range(2):
                    act.wait_ge(s_elu, b * 2 + i + 1)
                    nc.scalar.activation(r_e[:, i, :], r_m[:, i, :], ACT.Exp).then_inc(s_eluexp, 1)
                for i in range(2):
                    act.wait_ge(s_pa, b * 3 + 2 + i)
                    nc.scalar.activation(v1[:, 2 * i:2 * i + 2, :, 0:HD],
                                         bank[5 - i][:, :].rearrange("p (n h d) -> p n h d", n=2, h=HKV), ACT.Copy)\
                        .then_inc(s_pafree, 1)
                for h in range(HKV):
                    act.wait_ge(s_full, b * NFULL + 2 + h)
                    nc.scalar.activation(kh[:, h, :], rot[:, h % 2, :], ACT.Copy).then_inc(s_hi, 1)
                for i in range(HQ // 2):
                    act.wait_ge(s_full, b * NFULL + 2 + HKV + i)
                    nc.scalar.activation(qs[0:HD, 2 * i, :], rot[0:HD, i % 2, :], ACT.Copy)
                    nc.scalar.activation(qs[HD:P, 2 * i + 1, :], rot[HD:P, i % 2, :], ACT.Copy).then_inc(s_hi, 1)

                def copy_max(h):
                    act.wait_ge(s_mt, b * HKV + h + 1)
                    nc.scalar.activation(negmT[:, h % 2, :], bank[7][0:G, :], ACT.Copy).then_inc(s_mtc, 1)

                copy_max(0)
                for n in range(HQ):
                    if n >= 2:
                        act.wait_ge(s_pv, b * HQ + n - 1)
                    for i, js in enumerate(PIECES):
                        act.wait_ge(s_ex, b * 48 + n * 3 + i + 1)
                        o = POFF[js[0]]
                        w = sum(T - P * j for j in js)
                        nc.scalar.activation(pt[:, n % 2, o:o + w], bank[2 + i][:, 0:w], ACT.Exp,
                                             scale=HD ** -0.5).then_inc(s_p, 1)
                    if n % G == G - 1 and n // G + 1 < HKV:
                        copy_max(n // G + 1)
                for u in range(8):
                    act.wait_ge(s_ot, b * 8 + u + 1)
                    nc.scalar.activation(oT[:, (u // 2) % 2, (u % 2) * 4:(u % 2) * 4 + 4, :],
                                         bank[u % 2][:, :].rearrange("p (c t) -> p c t", c=4), ACT.Copy)\
                        .then_inc(s_otc, 1)
                for c in range(NT):
                    act.wait_ge(s_kt, b * NT + c + 1)
                    if c >= 1:
                        act.wait_ge(s_su, b * NT + c)
                    nc.scalar.activation(kt[:, :], bank[5][:, 0:P], ACT.Copy).then_inc(s_ktc, 1)
                act.wait_ge(s_at, b + 1)
                nc.scalar.activation(atT[:, :], bank[2][:, :], ACT.Copy).then_inc(s_atc, 1)
                act.wait_ge(s_xft, b + 1)
                nc.scalar.activation(xfT[:, :], bank[0][:, :], ACT.Copy).then_inc(s_xftc, 1)
                act.wait_ge(s_dif, b + 1)
                nc.scalar.activation(tk[:, 0, :, 1], tk[:, 0, :, 0], ACT.Exp).then_inc(s_dexp, 1)
                act.wait_ge(s_pkt, b + 1)
                nc.scalar.activation(pickT[:, :], bank[3][0:E, :], ACT.Copy).then_inc(s_pktc, 1)

                def copy_factor(v):
                    act.wait_ge(s_up, b * 16 + v + 1)
                    if v >= 2:
                        act.wait_ge(s_hp, b * 16 + v - 1)
                    nc.scalar.activation(hc[:, v % 2, :], bank[v % 2 * 2][:, :], ACT.Copy).then_inc(s_hc, 1)

                copy_factor(0)
                for v in range(2 * E):
                    if v + 1 < 2 * E:
                        copy_factor(v + 1)
                    act.wait_ge(s_hp, b * 16 + v + 1)
                    if v >= 2:
                        act.wait_ge(s_dn, b * 16 + v - 1)
                    nc.scalar.activation(hg[:, v % 2, :], hp[:, v % 2, :], ACT.Gelu).then_inc(s_hg, 1)
                act.nop().then_inc(s_act_end, 1)

        @block.vector
        def _(dve):
            v = nc.vector
            links = [0]

            def setup(ins):
                links[0] += 1
                ins.then_inc(s_setup, 1)
                dve.wait_ge(s_setup, links[0])

            dve.wait_ge(s_load, 16 * NLOAD)
            v.memset(v9[:, :, :, LD:LV], 1.0)
            v.memset(v1[:, :, :, HD:HD + 2], 1.0)
            v.memset(carry[:, :, :], 0.0)
            setup(v.tensor_copy(cr[:, :], c_all[:, 0:3 * P]))
            dve.wait_ge(s_wsplit, 1)
            v.tensor_tensor(watt_l[:, :], watt[:, :], watt_h[:, :], ALU.subtract)
            v.tensor_tensor(wlin_l[:, :], wlin[:, :], wlin_h[:, :], ALU.subtract).then_inc(s_const, 1)
            v.nop().then_inc(s_dve_end, 1)
            with dve.Fori(0, B) as b:
                count = [0]

                def link(ins):
                    count[0] += 1
                    ins.then_inc(s_chain, 1)
                    dve.wait_ge(s_chain, b * CHAIN + count[0])

                def mean_square(src, r, eps):
                    i = ROOTS[r][0]
                    link(v.tensor_tensor(sq[:, :, :], src, src, ALU.mult))
                    link(v.tensor_reduce(st[:, 0, :], sq[:, :, :], AX.X, ALU.add))
                    v.tensor_scalar(st[:, i, :], st[:, 0, :], 1.0 / D, eps, ALU.mult, ALU.add).then_inc(s_var, 1)

                def root(r):
                    dve.wait_ge(s_rstd, b * 4 + r + 1)
                    return bcast(st[:, ROOTS[r][1], :], D)

                end_of_batch_before(dve, b)
                dve.wait_ge(s_x, 16 * b + 16)
                link(v.tensor_reduce(st[:, 0, :], xt[:, :, :], AX.X, ALU.add))
                link(v.tensor_scalar(st[:, 1, :], st[:, 0, :], 1.0 / D, None, ALU.mult))
                link(v.tensor_tensor(xn[:, :, :], xt[:, :, :], bcast(st[:, 1, :], D), ALU.subtract))
                mean_square(xn[:, :, :], 0, LN_EPS)
                v.tensor_tensor(xn[:, :, :], xn[:, :, :], root(0), ALU.mult).then_inc(s_norm, 1)
                dve.wait_ge(s_norm, b * 2 + 1)
                mean_square(xn[:, :, :], 1, EPS)
                v.tensor_tensor(xg[:, :, :], xn[:, :, :], root(1), ALU.mult).then_inc(s_norm, 1)
                nd = [0]
                nf = [0]

                def filled():
                    i = nd[0]
                    nd[0] += 1
                    dve.wait_ge(s_pd, b * ND + i + 1)
                    return bank[i % 4]

                def low(k):
                    dve.wait_ge(s_hi, b * NSPLIT + k + 1)

                bk = filled()
                low(0)
                v.tensor_tensor(xn_l[:, :], bk[:, :], xn_h[:, :], ALU.subtract).then_inc(s_lo, 1)
                bk = filled()
                v.tensor_scalar(xgt[:, :], bk[:, :], g1_sb[:, :], None, ALU.mult).then_inc(s_full, 1)
                dve.wait_ge(s_full, b * NFULL + 1)
                low(1)
                v.tensor_tensor(xg_l[:, :], xgt[:, :], xg_h[:, :], ALU.subtract).then_inc(s_lo, 1)
                bk = filled()
                v.tensor_tensor(zb[:, 0], bk[:, 0:NT * LH].rearrange("p (n h) -> p n h", n=NT),
                                row("bb").unsqueeze(1).to_broadcast([P, NT, LH]), ALU.add).then_inc(s_zb, 1)
                for i, dst in enumerate((ql, kl)):
                    bk = filled()
                    v.tensor_tensor(r_a[:, i, :], bk[:, :], const("cos_l"), ALU.mult).then_inc(s_pdfree, 1)
                    bk = filled()
                    v.tensor_tensor(r_b[:, i, :], bk[:, :], const("sin_l"), ALU.mult).then_inc(s_pdfree, 1)
                    dve.wait_ge(s_pdfree, b * (ND - 3) + nd[0] - 3)
                    link(v.tensor_tensor(r_a[:, i, :], r_a[:, i, :], r_b[:, i, :], ALU.add))
                    v.tensor_scalar(r_m[:, i, :], r_a[:, i, :], 0.0, None, ALU.min).then_inc(s_elu, 1)
                dve.wait_ge(s_zbe, b + 1)
                link(v.tensor_scalar(zb[:, 2], zb[:, 1], 1.0, None, ALU.add))
                link(v.reciprocal(zb[:, 3], zb[:, 2]))
                link(v.tensor_scalar(zb[:, 0], zb[:, 3], 0.8, 0.999, ALU.max, ALU.min))
                link(v.reciprocal(zb[:, 1], zb[:, 0]))
                for i in range(2):
                    last = v.tensor_copy(bet[i], zb[:, i].unsqueeze(3).to_broadcast([P, NT, LH, LD]))
                last.then_inc(s_beta, 1)
                for i, dst in enumerate((ql, kl)):
                    dve.wait_ge(s_eluexp, b * 2 + i + 1)
                    link(v.scalar_tensor_tensor(dst[:, :], r_a[:, i, :], 0.0, r_e[:, i, :], ALU.max, ALU.add))

                def rotated(i):
                    bk = filled()
                    v.tensor_tensor(rot[:, i % 2, :], bk[:, :], const("cos_s"), ALU.mult).then_inc(s_pdfree, 1)
                    bk = filled()
                    v.tensor_tensor(r_b[:, i % 2, :], bk[:, :], const("sin_s"), ALU.mult).then_inc(s_pdfree, 1)
                    dve.wait_ge(s_pdfree, b * (ND - 3) + nd[0] - 3)
                    v.tensor_tensor(rot[:, i % 2, :], rot[:, i % 2, :], r_b[:, i % 2, :], ALU.add)\
                        .then_inc(s_full, 1)

                def key_low(h):
                    low(2 + h)
                    v.tensor_tensor(klo[:, h, :], rot[:, h % 2, :], kh[:, h, :], ALU.subtract).then_inc(s_lo, 1)

                def query_low(i):
                    low(2 + HKV + i)
                    v.tensor_tensor(qs[HD:P, 2 * i, :], rot[0:HD, i % 2, :], qs[0:HD, 2 * i, :], ALU.subtract)
                    v.tensor_tensor(qs[0:HD, 2 * i + 1, :], rot[HD:P, i % 2, :], qs[HD:P, 2 * i + 1, :],
                                    ALU.subtract).then_inc(s_lo, 1)

                for h in range(HKV):
                    if h >= 2:
                        dve.wait_ge(s_lo, b * NSPLIT + 2 + h - 1)
                    rotated(h)
                    if h >= 1:
                        key_low(h - 1)
                key_low(HKV - 1)
                dve.wait_ge(s_lo, b * NSPLIT + 2 + HKV)
                for i in range(HQ // 2):
                    rotated(i)
                    if i >= 1:
                        query_low(i - 1)
                        dve.wait_ge(s_lo, b * NSPLIT + 2 + HKV + i)
                query_low(HQ // 2 - 1)
                for i in range(2):
                    bk = filled()
                    for c in range(NT):
                        t = slice(c * P, (c + 1) * P)
                        last = v.tensor_tensor_scan(dec[:, i, t], bk[:, t], const("ones"), 1.0,
                                                    ALU.mult, ALU.mult)
                    last.then_inc(s_pdfree, 1)
                dve.wait_ge(s_pdfree, (b + 1) * (ND - 3))
                link(v.tensor_tensor(ql[:, :], ql[:, :], dec[:, 0, :], ALU.mult))
                v.tensor_tensor(kl[:, :], kl[:, :], dec[:, 1, :], ALU.mult).then_inc(s_lin, 1)

                def spread_queries(c):
                    if c >= 2:
                        dve.wait_ge(s_as, b * 16 + 4 * (c - 1))
                    for g in range(G):
                        last = v.tensor_scalar(qm[:, c % 2, g, :], ql[:, c * P:(c + 1) * P],
                                               const("quad")[:, g:g + 1], None, ALU.mult)
                    last.then_inc(s_qm, 1)

                v.memset(state[:, :], 0.0).then_inc(s_st, 1)

                def take_max(h, g):
                    n = h * G + g
                    if g == 0 and h >= 2:
                        dve.wait_ge(s_mt, b * HKV + h - 1)
                    for qt in range(NT):
                        u = n * NT + qt
                        dve.wait_ge(s_sc, b * 64 + u + 1)
                        v.tensor_reduce(negm[:, h % 2, qt, g:g + 1], bank[u % 2][:, 0:(qt + 1) * P], AX.X, ALU.max,
                                        negate=True).then_inc(s_mx, 1)

                def normalise(n):
                    dve.wait_ge(s_pv, b * HQ + n + 1)
                    acc = bank[5 + n % 2][:, 0:NT * (HD + 1)].rearrange("p (q e) -> p q e", q=NT)
                    link(v.reciprocal(rden[:, n % 2, :], acc[:, :, HD:HD + 1].rearrange("p q e -> p (q e)")))
                    v.tensor_tensor(osb[:, :, n * HD:(n + 1) * HD], acc[:, :, 0:HD], bcast(rden[:, n % 2, :], HD),
                                    ALU.mult).then_inc(s_o, 1)

                for g in range(G):
                    take_max(0, g)
                for h in range(HKV):
                    for g in range(G):
                        if h + 1 < HKV:
                            take_max(h + 1, g)
                        if h * G + g >= 1:
                            normalise(h * G + g - 1)
                normalise(HQ - 1)
                dve.wait_ge(s_y, b * 2 + 1)
                link(v.tensor_tensor(h1[:, :, :], xn[:, :, :], bank[3][:, :].rearrange("p (n d) -> p n d", n=NT),
                                     ALU.add))
                mean_square(h1[:, :, :], 2, EPS)
                link(v.tensor_tensor(tmp[:, :, :], h1[:, :, :], root(2), ALU.mult))
                v.tensor_tensor(xf[:, :, :], tmp[:, :, :], row("g2").unsqueeze(1).to_broadcast([P, NT, D]), ALU.mult)\
                    .then_inc(s_xf, 1)
                spread_queries(0)
                for c in range(NT):
                    if c + 1 < NT:
                        spread_queries(c + 1)
                    if c >= 1:
                        dve.wait_ge(s_ao, b * NT + c)
                    for q in range(4):
                        u = c * 4 + q
                        dve.wait_ge(s_as, b * 16 + u + 1)
                        v.tensor_tensor(am[:, 4 * q:4 * q + 4, :], bank[6 + u % 2][:, :].rearrange("p (g t) -> p g t", g=4),
                                        const("upto").unsqueeze(1).to_broadcast([P, G, P]), ALU.mult)\
                            .then_inc(s_am, 1)
                    dve.wait_ge(s_ao, b * NT + c + 1)
                    acc = bank[0][:, 0:LH * LV].rearrange("p (h e) -> p h e", h=LH)
                    link(v.tensor_scalar(rden_l[:, :], acc[:, :, LD:LV].rearrange("p h e -> p (h e)"), EPS, None, ALU.add))
                    link(v.reciprocal(rden_l[:, :], rden_l[:, :]))
                    v.tensor_tensor(at_l[:, c, :].rearrange("p (h d) -> p h d", h=LH), acc[:, :, 0:LD],
                                    bcast(rden_l[:, :], LD), ALU.mult).then_inc(s_aod, 1)
                    dve.wait_ge(s_su, b * NT + c + 1)
                    link(v.tensor_tensor(stt[:, :], bank[1][:, 0:LH * LV], const("diag"), ALU.mult))
                    link(v.tensor_tensor(stt[:, :], stt[:, :], state[:, :], ALU.add))
                    v.tensor_scalar(state[:, :], stt[:, :], dec[:, 0, (c + 1) * P - 1:(c + 1) * P], None, ALU.mult)\
                        .then_inc(s_st, 1)
                dve.wait_ge(s_y, b * 2 + 2)
                link(v.tensor_tensor(tmp[:, :, :], xn[:, :, :], bank[4][:, :].rearrange("p (n d) -> p n d", n=NT), ALU.add))
                link(v.tensor_tensor(yl[:, :, :], tmp[:, :, :], row("bo").unsqueeze(1).to_broadcast([P, NT, D]), ALU.add))
                mean_square(yl[:, :, :], 3, EPS)
                link(v.tensor_tensor(tmp[:, :, :], yl[:, :, :], root(3), ALU.mult))
                v.tensor_tensor(yl[:, :, :], tmp[:, :, :], row("scale").unsqueeze(1).to_broadcast([P, NT, D]), ALU.mult)\
                    .then_inc(s_yl, 1)
                dve.wait_ge(s_lg, b + 1)
                link(v.tensor_tensor(lg[:, 0], bank[1][:, 0:NT * E].rearrange("p (n e) -> p n e", n=NT),
                                     row("router_b").unsqueeze(1).to_broadcast([P, NT, E]), ALU.add))
                less = const("less").unsqueeze(1).to_broadcast([P, NT, E])
                iota = const("iota").unsqueeze(1).to_broadcast([P, NT, E])
                for k in range(2):
                    link(v.tensor_reduce(mx[:, k, :], lg[:, k], AX.X, ALU.max))
                    link(v.tensor_tensor(eq[:, :, :], lg[:, k], bcast(mx[:, k, :], E), ALU.is_equal))
                    link(v.tensor_tensor(eq[:, :, :], eq[:, :, :], less, ALU.mult))
                    link(v.tensor_reduce(mi[:, :], eq[:, :, :], AX.X, ALU.min))
                    link(v.tensor_tensor(oh[:, :, k, :], less, bcast(mi[:, :], E), ALU.is_equal))
                    if k == 0:
                        link(v.scalar_tensor_tensor(lg[:, 1], oh[:, :, 0, :], -3.0e38, lg[:, 0], ALU.mult, ALU.add))
                v.tensor_copy(ohc[:, 0], carry[:, :, :])
                for n in range(1, NT):
                    link(v.tensor_tensor(ohc[:, n], ohc[:, n - 1], oh[:, n - 1], ALU.add)) if n > 1 else \
                        link(v.tensor_tensor(ohc[:, 1], carry[:, :, :], oh[:, 0], ALU.add))
                v.tensor_tensor(carry[:, :, :], ohc[:, NT - 1], oh[:, NT - 1], ALU.add).then_inc(s_oh, 1)
                v.tensor_tensor(tk[:, 0, :, 0], mx[:, 1, :], mx[:, 0, :], ALU.subtract).then_inc(s_dif, 1)
                dve.wait_ge(s_pos, b + 1)
                cnt = bank[2][:, 0:NT * 2 * E].rearrange("p (n k e) -> p n k e", n=NT, k=2)
                link(v.tensor_copy(pos[:, :, 0, :], cnt[:, :, 0, :]))
                link(v.tensor_tensor(pos[:, :, 1, :], cnt[:, :, 1, :], pos[:, :, 0, :], ALU.add))
                link(v.scalar_tensor_tensor(em[:, :, :, :].rearrange("p n k e -> p (n k e)"),
                                            pos[:, :, :, :].rearrange("p n k e -> p (n k e)"), float(CAP),
                                            oh[:, :, :, :].rearrange("p n k e -> p (n k e)"), ALU.is_lt, ALU.mult))
                fit = tk[:, 1]
                link(v.tensor_reduce(fit, em[:, :, :, :], AX.X, ALU.add))
                for k in range(2):
                    last = v.tensor_tensor(emi[:, :, k, :], em[:, :, k, :], iota, ALU.mult)
                link(last)
                link(v.tensor_reduce(tk[:, 2], emi[:, :, :, :], AX.X, ALU.add))
                v.tensor_tensor(tk[:, 3, :, 0], tk[:, 2, :, 0], tk[:, 2, :, 1], ALU.max)
                link(v.tensor_tensor(tk[:, 3, :, 1], fit[:, :, 0], fit[:, :, 1], ALU.max))
                link(v.tensor_tensor(pick[:, :, :], iota, tk[:, 3, :, 0:1].to_broadcast([P, NT, E]), ALU.is_equal))
                v.tensor_tensor(pick[:, :, :], pick[:, :, :], tk[:, 3, :, 1:2].to_broadcast([P, NT, E]), ALU.mult)\
                    .then_inc(s_pick, 1)
                dve.wait_ge(s_dexp, b + 1)
                link(v.tensor_scalar(tk[:, 5, :, 0], tk[:, 0, :, 1], 1.0, None, ALU.add))
                link(v.reciprocal(tk[:, 6, :, 0], tk[:, 5, :, 0]))
                link(v.tensor_tensor(tk[:, 6, :, 1], tk[:, 6, :, 0], tk[:, 0, :, 1], ALU.mult))
                link(v.tensor_tensor(tk[:, 7], tk[:, 6], fit, ALU.mult))
                link(v.tensor_tensor(tk[:, 8], tk[:, 6], tk[:, 7], ALU.subtract))
                v.tensor_tensor(tk[:, 9, :, 0], tk[:, 7, :, 0], tk[:, 7, :, 1], ALU.add)
                link(v.tensor_tensor(tk[:, 9, :, 1], tk[:, 8, :, 0], tk[:, 8, :, 1], ALU.add))
                def mask_input(e):
                    dve.wait_ge(s_pb, b * E + e + 1)
                    if e >= 2:
                        dve.wait_ge(s_up, b * 16 + 2 * (e - 1))
                    if e == 0:
                        dve.wait_ge(s_xftc, b + 1)
                    v.tensor_tensor(xm[:, e % 2, :], xfT[:, :], bank[4 + e % 2][:, :], ALU.mult).then_inc(s_xm, 1)

                mask_input(0)
                for u in range(2 * E):
                    if u % 2 == 0 and u // 2 + 1 < E:
                        mask_input(u // 2 + 1)
                    dve.wait_ge(s_hc, b * 16 + u + 1)
                    if u >= 2:
                        dve.wait_ge(s_hg, b * 16 + u - 1)
                    v.tensor_tensor(hp[:, u % 2, :], bank[u % 2 * 2 + 1][:, :], hc[:, u % 2, :], ALU.mult)\
                        .then_inc(s_hp, 1)
                link(v.tensor_tensor(tmp[:, :, :], xf[:, :, :], tk[:, 9, :, 1:2].to_broadcast([P, NT, D]), ALU.mult))
                link(v.tensor_tensor(tmp[:, :, :], tmp[:, :, :], h1[:, :, :], ALU.add))
                link(v.tensor_tensor(tmp[:, :, :], tmp[:, :, :], yl[:, :, :], ALU.add))
                dve.wait_ge(s_keep, 16 * b + 16)
                link(v.tensor_tensor(tmp[:, :, :], tmp[:, :, :], ob[:, :, :], ALU.add))
                dve.wait_ge(s_dn, b * 16 + 16)
                link(v.tensor_tensor(sq[:, :, :], bank[6][:, :].rearrange("p (n d) -> p n d", n=NT),
                                     tk[:, 9, :, 0:1].to_broadcast([P, NT, D]), ALU.mult))
                v.tensor_tensor(ob[:, :, :], tmp[:, :, :], sq[:, :, :], ALU.add).then_inc(s_ob, 1)
                dve.wait_ge(s_ob, b + 1)
                v.nop().then_inc(s_dve_end, 1)
                assert count[0] == CHAIN, count[0]


def _rope(width, t):
    import numpy as np
    inv = (1.0 / (np.float32(10000.0) ** (np.arange(0, width, 2, dtype=np.float32) / np.float32(width))))
    ang = np.arange(t, dtype=np.float32)[:, None] * inv.astype(np.float32)[None, :]
    ang = np.concatenate([ang, ang], axis=1)
    sign = np.concatenate([-np.ones(width // 2), np.ones(width // 2)]).astype(np.float32)
    cos, sin = np.cos(ang), np.sin(ang) * sign
    return np.tile(cos.T, (P // width, 1)), np.tile(sin.T, (P // width, 1))


def constants():
    import numpy as np
    i = np.arange(P)
    c = {}
    c["ident"] = np.eye(P)
    c["mask_qk"] = np.where(i[None, :] > i[:, None], -1e30, 0.0)
    c["mask_kq"] = c["mask_qk"].T
    c["upto"] = (i[None, :] >= i[:, None]) * 1.0
    c["ones"] = np.ones((P, P))
    c["quad"] = ((i[:, None] // LD) % G == np.arange(G)[None, :]) * 1.0
    c["diag"] = (i[:, None] // LD == (np.arange(LH * LV) // LV)[None, :]) * 1.0
    c["iota"] = np.tile(np.arange(E), (P, 1))
    c["less"] = c["iota"] - E
    c["cos_l"], c["sin_l"] = _rope(LD, T)
    c["cos_s"], c["sin_s"] = _rope(HD, T)
    return np.ascontiguousarray(np.concatenate([c[n] for n, _ in CONST], axis=1).astype(np.float32))


def kernel(**inputs):
    import numpy as np
    import concourse.bacc as bacc
    from concourse.bass_utils import run_bass_kernel_spmd

    g = {k: np.asarray(v) for k, v in inputs.items()}

    def exchanged(w, width):
        w = w.reshape(w.shape[0], -1, 2, width // 2)
        return w[:, :, ::-1, :].reshape(w.shape[0], -1)

    wq, wk = g["L0_attn_Wq"].T, g["L0_attn_Wk"].T
    w_lin = np.concatenate([wq, exchanged(wq, LD), wk, exchanged(wk, LD), g["L0_attn_Wv"].T, g["L0_attn_Wb"].T], axis=1)
    fq = g["L0_ffn_wq"].reshape(D, G, HKV, HD).transpose(0, 2, 1, 3).reshape(D, HQ * HD)
    fk = np.repeat(g["L0_ffn_wk"].reshape(D, HKV, 1, HD), 2, axis=2).reshape(D, 2 * HKV * HD)
    w_att = np.concatenate([fq, exchanged(fq, HD), fk, exchanged(fk, HD), g["L0_ffn_wv"]], axis=1)
    w_out = g["L0_ffn_wo"].reshape(G, HKV, HD, D).transpose(1, 0, 2, 3).reshape(HQ * HD, D)
    w_up = np.concatenate([g["L0_ffn_w1"], g["L0_ffn_w2"]], axis=2).transpose(1, 0, 2)
    rows = np.concatenate([g["L0_attn_bb"], g["L0_attn_bo"], g["L0_attn_scale"], g["L0_ffn_g2"], g["L0_ffn_router_b"]])
    arrays = {
        "x": g["L0_attn_x"], "w_lin": w_lin, "w_lout": g["L0_attn_Wo"].T, "w_att": w_att, "w_out": w_out,
        "w_up": w_up, "w_down": g["L0_ffn_w3"], "w_router": g["L0_ffn_router_w"],
        "g1": g["L0_ffn_g1"].reshape(D, 1), "rows": np.tile(rows[None, :], (P, 1)), "consts": constants(),
    }
    arrays = {k: np.ascontiguousarray(v) for k, v in arrays.items()}
    nc = bacc.Bacc("TRN2", target_bir_lowering=False, num_devices=1)
    args = [nc.dram_tensor(k, v.shape, mybir.dt.from_np(v.dtype), kind="ExternalInput").ap() for k, v in arrays.items()]
    args.append(nc.dram_tensor("out", (B, T, D), F32, kind="ExternalOutput").ap())
    attention_kernel(nc, *args)
    return run_bass_kernel_spmd(nc, [arrays], core_ids=[0]).results[0]["out"]
```

```python
import concourse.bass as bass
from concourse import mybir
from contextlib import ExitStack

F32 = mybir.dt.float32
F32R = mybir.dt.float32r
I32 = mybir.dt.int32
BF16 = mybir.dt.bfloat16
U32 = mybir.dt.uint32
ALU = mybir.AluOpType
ACT = mybir.ActivationFunctionType
AX = mybir.AxisListType

B, T, D = 8, 512, 128
P = 128
NT = T // P
LH, LD = 16, 8
LV = LD + 1
HQ, HKV, HD = 16, 4, 64
G = HQ // HKV
E, HID = 8, 256
CAP = (B * T) // 8
SG = 4
NS = -(-(B * NT + E - 1) // SG) * SG
EPS = 1e-6
LN_EPS = 1e-5

CONST = [("ident", P), ("mask_qk", P), ("mask_kq", P), ("upto", P), ("ones", P), ("quad", G),
         ("diag", LH * LV), ("iota", E), ("less", E), ("steps", B * NT), ("tiles", NS),
         ("cos_l", T), ("sin_l", T), ("cos_s", T), ("sin_s", T)]
COFF = {}
_at = 0
for _n, _w in CONST:
    COFF[_n] = (_at, _w)
    _at += _w
NCONST = _at
ROWS = [("bb", LH), ("bo", D), ("scale", D), ("g2", D), ("router_b", E)]
ROFF = {}
_at = 0
for _n, _w in ROWS:
    ROFF[_n] = (_at, _w)
    _at += _w
NROWS = _at


def body_steps():
    side = {n: [] for n in range(HQ)}

    def put(n, at, *steps):
        side[n] += [(at, st) for st in steps]

    def project(n, at, kind, rel, i):
        put(n, at, (kind, rel, (i, 0)))
        put(n, at + 1, (kind, rel, (i, 1)))
        put(n, at + 2, (kind + "H", rel, i))
        put(n, at + 4, (kind + "L", rel, i))

    for n, rel, i in [(1, -1, 7)] + [(2 * i + 3, 0, i) for i in range(7)]:
        for part in range(NT):
            put(n, part, ("RC", rel, (i, part)))
        put(n, NT, ("RM", rel, i))
    project(0, 0, "Q", 0, 6)
    project(0, 2, "K", 0, 3)
    project(0, 4, "Q", 0, 7)
    put(0, 9, ("VP", 0, 0), ("VP", 0, 1))
    put(1, 6, ("WO", -1, 7))
    put(1, 8, ("H1", -1, 0), ("XR", 0, 0))
    put(2, 0, ("LN", 1, 0))
    put(2, 4, ("LM", 1, 0))
    put(3, 0, ("XN", 1, 0))
    put(3, 2, ("XG", 1, 0))
    put(3, 3, ("XH", 1, 0))
    put(3, 6, ("WO", 0, 0))
    put(3, 4, ("XL", 1, 0))
    put(3, 5, ("BL", 1, 0))
    put(3, 6, ("XF", -1, 0))
    put(4, 1, ("BX", 1, 0))
    project(4, 0, "Q", 1, 0)
    project(4, 2, "K", 1, 0)
    put(4, 6, ("BE", 1, 0), ("LG", -1, 0))
    for n, i in ((5, 1), (7, 2), (9, 3), (11, 4), (13, 5), (15, 6)):
        put(n, 6, ("WO", 0, i))
    put(5, 1, ("LP", 1, 0))
    put(5, 2, ("LP", 1, 1))
    put(5, 4, ("EE", 1, 0))
    put(5, 5, ("LP", 1, 2))
    put(5, 6, ("LP", 1, 3))
    put(6, 1, ("EE", 1, 1), ("DX", -1, 0))
    project(6, 0, "Q", 1, 1)
    put(6, 3, ("PC", -1, 0))
    put(7, 1, ("LE", 1, 0), ("LE", 1, 1))
    put(7, 2, ("LB", 1, 0))
    put(7, 4, ("LB", 1, 1))
    put(7, 5, ("LV", 1, 0), ("LQ", 1, 0))
    project(8, 0, "Q", 1, 2)
    project(8, 2, "K", 1, 1)
    put(9, 5, ("RK", -1, 0))
    project(10, 0, "Q", 1, 3)
    for n, at, c in ((9, 1, 0), (11, 1, 1), (13, 1, 2), (14, 3, 3)):
        put(n - 1, 6, ("CQ", 1, c))
        put(n, at, ("CK", 1, c))
        for q in range(4):
            put(n, at + 1 + q, ("CS", 1, (c, q)))
        put(n + 1, 1, ("CO", 1, c))
        put(n + 1, 2, ("CU", 1, c))
    project(12, 0, "Q", 1, 4)
    project(12, 2, "K", 1, 2)
    project(14, 0, "Q", 1, 5)
    put(14, 6, ("YC", 0, 0))
    put(15, 4, ("LT", 1, 0))
    put(15, 6, ("LY", 1, 0))
    steps = []
    for n in range(HQ):
        m, r = (n + 4, 0) if n + 4 < HQ else (n + 4 - HQ, 1)
        main = [("M", r, (m, 0)), ("S", 0, (n, 0)), ("M", r, (m, 1)), ("S", 0, (n, 1)), ("M", r, (m, 2)),
                ("S", 0, (n, 2)), ("M", r, (m, 3)), ("V", 0, n - 1) if n else ("V", -1, HQ - 1)]
        for at, st in enumerate(main):
            steps += [x for a, x in side[n] if a == at]
            steps.append(st)
        steps += [x for a, x in side[n] if a > len(main) - 1]
        if n % G == G - 1:
            steps.append(("T", 0, (n + 1) // G) if n + 1 < HQ else ("T", 1, 0))
    return steps


SIDE_DVE = ("Q", "K", "XN", "XG", "BL", "LP", "LB", "CS", "CO", "CU", "LY", "LG", "PC", "RK")
SIDE_ACT = ("T", "VP", "LV", "CK", "LT", "XF")
COUNTED = {
    "fill": SIDE_DVE + SIDE_ACT, "ed": SIDE_DVE, "ea": SIDE_ACT, "sc": ("M",), "mx": ("M",),
    "ex": ("S",), "p": ("S",), "pv": ("V",), "o": ("V",), "rec": ("RC",), "nrm": ("RM",), "wo": ("WO",),
    "hi": ("XN", "XH", "QH", "KH"), "xl": ("XL",), "rot": ("QH", "KH"), "low": ("QL", "KL"),
    "var": ("LN", "LM", "H1", "LY"), "rstd": ("LN", "LM", "H1", "LY"), "norm": ("LN", "LM"),
    "xf": ("H1",), "res": ("XR",), "elu": ("EE",), "eluexp": ("EE",), "lphi": ("LE",), "zbe": ("BX",),
    "beta": ("BE",), "lin": ("LQ",), "qm": ("CQ",), "st": ("CU",), "ylp": ("YC",), "la": ("LY",),
    "oh": ("LG",), "dif": ("DX",), "dexp": ("DX",), "pick": ("PC",), "rk": ("RK",),
}


class Order:

    def __init__(self):
        full = body_steps()
        self.steps, self.at, self.total = {}, {}, {}
        for b in (-1, 0, 1, B - 1, B):
            mine = [st for st in full if 0 <= b + st[1] < B]
            self.steps[b] = mine
            self.at[b], self.total[b] = {}, {}
            for name, kinds in COUNTED.items():
                count = 0
                for kind, rel, i in mine:
                    if kind in kinds or f"{kind}{i}" in kinds:
                        count += 1
                        self.at[b][name, kind, rel, i] = count
                self.total[b][name] = count

    def base(self, b, body, name):
        t = {k: v[name] for k, v in self.total.items()}
        if body == -1:
            return 0
        if body == 0:
            return t[-1]
        if body == 1:
            return b * t[1] + (t[-1] + t[0] - t[1])
        done = t[-1] + t[0] + (B - 2) * t[1]
        return done if body == B - 1 else done + t[B - 1]

    def value(self, b, body, name, kind, rel, i):
        own = self.at[body].get((name, kind, rel, i))
        if own is not None:
            return self.base(b, body, name) + own
        before = {0: (-1,), 1: (0, 1), B - 1: (1,), B: (B - 1,), -1: ()}[body]
        back = [self.total[q][name] - self.at[q][name, kind, rel + 1, i] for q in before
                if (name, kind, rel + 1, i) in self.at[q]]
        if not back:
            return None
        assert len(back) == len(before), (name, kind, rel, i)
        return self.base(b, body, name) - min(back)

    def last(self, body, name, steps):
        b = 2 if body == 1 else body
        counts = [(self.value(b, body, name, *st), st) for st in steps if st is not None and st[0] in COUNTED[name]]
        counts = [c for c in counts if c[0] is not None]
        return max(counts, key=lambda c: c[0])[1] if counts else None

    def ring(self, body):
        fills = {b: [st for st in self.steps[b] if st[0] in SIDE_DVE + SIDE_ACT] for b in self.steps}
        assert len(fills[1]) % 2 == 0, {b: len(f) for b, f in fills.items()}
        before = {0: -1, 1: 1, B - 1: 1, B: B - 1}.get(body)
        start = self.base(1, body, "fill") % 2 if body != 1 else (len(fills[-1]) + len(fills[0])) % 2
        lead = [(k, r - 1, i) for k, r, i in fills[before][-2:]] if before is not None else [None, None]
        both = lead + fills[body]
        return {st: ((start + n) % 2, both[n]) for n, st in enumerate(fills[body])}


def attention_kernel(nc, x, w_lin, w_lout, w_att, w_out, w_up, w_down, w_router, g1, rows, consts, out):
    ctx = ExitStack()
    with ctx:
        def sb(name, shape, dt=F32):
            return ctx.enter_context(nc.sbuf_tensor(name, shape, dt))

        def sem(name):
            return ctx.enter_context(nc.semaphore(name))

        c_all = sb("c_all", [P, NCONST])
        rows_sb = sb("rows_sb", [P, NROWS])
        g1_sb = sb("g1_sb", [P, 1])
        wlout = sb("wlout", [P, D])
        wout = sb("wout", [P, HQ * HD // P, D])
        wrt = sb("wrt", [P, E])

        def const(name):
            a, w = COFF[name]
            return c_all[:, a:a + w]

        def row(name):
            a, w = ROFF[name]
            return rows_sb[:, a:a + w]

        ident_r = sb("ident_r", [P, G], F32R)
        cb = sb("cb", [P, 3 * P], BF16)
        ident_b, mask_qk_b, mask_kq_b = cb[:, 0:P], cb[:, P:2 * P], cb[:, 2 * P:3 * P]

        def pick_row(n, r):
            return ident_r[0:n, r:r + 1].to_broadcast([n, P])

        NW = 2 * HQ * HD + 4 * HKV * HD + HKV * HD
        watt_h = sb("watt_h", [P, NW], F32R)
        watt_l = sb("watt_l", [P, NW], F32R)
        wlin_h = sb("wlin_h", [P, 5 * D + LH], F32R)
        wlin_l = sb("wlin_l", [P, 5 * D + LH], F32R)

        xt = sb("xt", [P, NT, D])
        xn = sb("xn", [P, NT, D])
        xres = sb("xres", [P, NT, D])
        xg = sb("xg", [P, NT, D])
        sq = sb("sq", [P, NT, D])
        st = sb("st", [P, 10, NT])
        xgt = sq[:, :, :].rearrange("p n d -> p (n d)")
        xn_h = sb("xn_h", [P, T], F32R)
        xn_l = sb("xn_l", [P, T], F32R)
        xg_h = sb("xg_h", [P, T], F32R)
        xg_l = sb("xg_l", [P, T], F32R)
        lin_area = sb("lin_area", [P, 8 * T])
        am_area = lin_area[:, 0:4 * T]
        r_a, rot = (lin_area[:, i * 2 * T:(i + 1) * 2 * T].rearrange("p (a t) -> p a t", a=2) for i in (2, 3))
        r_sin = sb("r_sin", [P, T])
        qk_l = sb("qk_l", [P, 2, T])
        ql, kl = qk_l[:, 0, :], qk_l[:, 1, :]
        dec = sb("dec", [P, 2, T])
        zb = sb("zb", [P, 4, NT, LH])
        qm = sb("qm", [P, 2, G, P])
        v9 = sb("v9", [P, NT, LH, LV])
        kt = sb("kt", [P, D])
        state = sb("state", [P, LH * LV])
        stt = sb("stt", [P, LH * LV])
        rden_l = sb("rden_l", [P, LH])
        h1 = sb("h1", [P, NT, D])
        at_l = h1
        atT = sb("atT", [P, T])
        yl = sb("yl", [P, NT, D])
        ylp = sb("ylp", [P, NT, D])
        r_m = am_area[:, 0:2 * T].rearrange("p (a t) -> p a t", a=2)
        bet = [am_area[:, i * T:(i + 1) * T].rearrange("p (n h d) -> p n h d", n=NT, h=LH) for i in (2, 3)]
        am = am_area[:, :].rearrange("p (h t) -> p h t", h=LH)
        kh = sb("kh", [P, HKV, T], F32R)
        klo = sb("klo", [P, HKV, T], F32R)
        qs = sb("qs", [P, HQ, T], F32R)
        v1 = sb("v1", [P, NT * HKV // 2, 3, HD])
        negm = sb("negm", [P, 2, NT, G])
        half = sb("half", [P, NT])
        negmT = sb("negmT", [G, 2, T], F32R)
        NPT = P * (NT * (NT + 1) // 2)
        pt = sb("pt", [P, 2, NPT])
        rden = sb("rden", [P, T])
        oT = sb("oT", [P, 2, T])
        xf = sb("xf", [P, NT, D])
        xfT = atT
        lg = sb("lg", [P, 2, NT, E])
        mx = sb("mx", [P, 2, NT])
        mi = sb("mi", [P, NT])
        eq = sb("eq", [P, NT, E])
        oh = sb("oh", [P, NT, 2, E])
        ohc = sb("ohc", [P, NT, 2, E])
        carry = sb("carry", [P, 2, E])
        pos = sb("pos", [P, NT, 2, E])
        em = sb("em", [P, NT, 2, E])
        emi = sb("emi", [P, NT, 2, E])
        tk = sb("tk", [P, 10, NT, 2])
        pick = sb("pick", [P, NT, E])
        pickc = sb("pickc", [P, NT, E])
        pcarry = sb("pcarry", [P, E])
        ob = ylp
        xf_all = sb("xf_all", [P, B * NT, D])
        pick_all = sb("pick_all", [P, B * NT, E])
        rank_all = sb("rank_all", [P, B * NT])
        share_all = sb("share_all", [P, B * NT])
        total = sb("total", [P, 4, E])
        slot_f = sb("slot_f", [P, B * NT])
        slot = sb("slot", [P, B * NT], U32)
        expert_f = sb("expert_f", [P, NS])
        expert = sb("expert", [P, NS], I32)
        stage = xf_all[:, :, :].rearrange("p n d -> p (n d)")
        watt, wlin = stage[:, 0:NW], stage[:, NW:NW + 5 * D + LH]
        wup = lin_area[:, :].rearrange("p (e n) -> p e n", e=E)
        wdown = pt[:, :, :].rearrange("p a n -> p (a n)")[:, 0:E * 2 * D].rearrange("p (e c n) -> p e c n", e=E, c=2)
        cmp = oT[:, :, :].rearrange("p a t -> p (a t)")
        ob_zero = sb("ob_zero", [P, D])
        xs, ys = xt, yl
        xsT = h1
        eht = [xgt, atT[:, :]]
        yg = [xn, xres]
        ehc = dec[:, :, :].rearrange("p a (k n) -> p (a k) n", n=HID)
        ehp = qm[:, :, :, :].rearrange("p a (k g) n -> p (a k) (g n)", g=2)
        ehg = qk_l[:, :, :].rearrange("p a (k n) -> p (a k) n", n=HID)

        sorted_x = nc.dram_tensor("sorted_x", (NS * P, D), F32).ap()
        sorted_y = nc.dram_tensor("sorted_y", (NS * P, D), F32).ap()
        partial = nc.dram_tensor("partial", (B, P, NT * D), F32).ap()
        bank = [ctx.enter_context(nc.psum_tensor(f"bank{i}", [P, 512], F32)) for i in range(8)]

        s_load = sem("s_load")
        s_x = sem("s_x")
        s_out = sem("s_out")
        s_obfree = sem("s_obfree")
        s_wsplit = sem("s_wsplit")
        s_const = sem("s_const")
        s_fill = sem("s_fill")
        s_ed = sem("s_ed")
        s_ea = sem("s_ea")
        s_var = sem("s_var")
        s_rstd = sem("s_rstd")
        s_norm = sem("s_norm")
        s_res = sem("s_res")
        s_hi = sem("s_hi")
        s_xl = sem("s_xl")
        s_rot = sem("s_rot")
        s_low = sem("s_low")
        s_zbe = sem("s_zbe")
        s_beta = sem("s_beta")
        s_elu = sem("s_elu")
        s_eluexp = sem("s_eluexp")
        s_lphi = sem("s_lphi")
        s_lin = sem("s_lin")
        s_qm = sem("s_qm")
        s_st = sem("s_st")
        s_ylp = sem("s_ylp")
        s_la = sem("s_la")
        s_sc = sem("s_sc")
        s_mx = sem("s_mx")
        s_ex = sem("s_ex")
        s_p = sem("s_p")
        s_pv = sem("s_pv")
        s_o = sem("s_o")
        s_rec = sem("s_rec")
        s_nrm = sem("s_nrm")
        s_wo = sem("s_wo")
        s_xf = sem("s_xf")
        s_oh = sem("s_oh")
        s_dif = sem("s_dif")
        s_dexp = sem("s_dexp")
        s_pick = sem("s_pick")
        s_rk = sem("s_rk")
        s_chain = sem("s_chain")
        s_half = sem("s_half")
        s_setup = sem("s_setup")
        s_pe_end = sem("s_pe_end")
        s_act_end = sem("s_act_end")
        s_dve_end = sem("s_dve_end")
        s_zero = sem("s_zero")
        s_tot = sem("s_tot")
        s_slot = sem("s_slot")
        s_expert = sem("s_expert")
        s_scat = sem("s_scat")
        s_wexp = sem("s_wexp")
        s_xs = sem("s_xs")
        s_xst = sem("s_xst")
        s_xstc = sem("s_xstc")
        s_eup = sem("s_eup")
        s_ehc = sem("s_ehc")
        s_ehp = sem("s_ehp")
        s_ehg = sem("s_ehg")
        s_eht = sem("s_eht")
        s_ehtc = sem("s_ehtc")
        s_ey = sem("s_ey")
        s_ys = sem("s_ys")
        s_yst = sem("s_yst")
        s_ysfree = sem("s_ysfree")
        s_yg = [sem("s_yg0"), sem("s_yg1")]
        s_pin = sem("s_pin")
        s_fin = sem("s_fin")
        s_done = sem("s_done")

        block = ctx.enter_context(nc.Block())
        xv = x.rearrange("b (n p) d -> b p n d", p=P)
        sxv = sorted_x.rearrange("(i k p) d -> i p k d", k=SG, p=P)
        syv = sorted_y.rearrange("(i k p) d -> i p k d", k=SG, p=P)
        ov = out.rearrange("b (n p) d -> b p n d", p=P)
        NLOAD = 8
        CHAIN = 66
        order = Order()

        WQ, WQX, WK, WKX, WV = 0, 1024, 2048, 2560, 3072
        POFF = [sum(T - P * i for i in range(j)) for j in range(NT)]
        PIECES = [[0], [1], [2, 3]]
        PROJ = ["Q0", "K0", "Q1", "Q2", "K1", "Q3", "Q4", "K2", "Q5", "Q6", "K3", "Q7"]
        score_bank, exp_bank, out_bank, wo_bank, side_bank = bank[0:2], bank[2:4], bank[4], bank[5], bank[6:8]

        def bcast(ap, n):
            return ap.unsqueeze(2).to_broadcast([ap.shape[0], ap.shape[1], n])

        def tile(ap, n):
            return ap[:, n * P:(n + 1) * P]

        def when(eng, semaphore, value):
            if value is not None:
                eng.wait_ge(semaphore, value)

        def before(step, n, per_batch):
            k = step - n
            return (0, k) if k >= 0 else (-1, k + per_batch)

        def run_bodies(eng, body):
            body(-1, -1)
            body(0, 0)
            with eng.Fori(1, B - 1) as b:
                body(b, 1)
            body(B - 1, B - 1)
            body(B, B)

        @block.sync
        def _(sp):
            sp.dma_start(xt[:, :, :], xv[0]).then_inc(s_x, 16)
            sp.dma_start(c_all[:, :], consts).then_inc(s_load, 16)
            sp.dma_start(wlin[:, :], w_lin).then_inc(s_load, 16)
            sp.dma_start(watt[:, :], w_att).then_inc(s_load, 16)
            sp.dma_start(rows_sb[:, :], rows).then_inc(s_load, 16)
            sp.dma_start(g1_sb[:, :], g1).then_inc(s_load, 16)
            sp.dma_start(wlout[:, :], w_lout).then_inc(s_load, 16)
            sp.dma_start(wout[:, :, :], w_out.rearrange("(c p) n -> p c n", p=P)).then_inc(s_load, 16)
            sp.dma_start(wrt[:, :], w_router).then_inc(s_load, 16)
            for b in (1, 2):
                sp.wait_ge(s_la, b)
                sp.dma_start(xt[:, :, :], xv[b]).then_inc(s_x, 16)
            with sp.Fori(1, B - 2) as b:
                sp.wait_ge(s_rk, b)
                sp.dma_start(partial[b - 1], ob[:, :, :].rearrange("p n d -> p (n d)")).then_inc(s_out, 16)
                sp.wait_ge(s_out, 16 * b)
                sp.nop().then_inc(s_obfree, 1)
                sp.wait_ge(s_la, b + 2)
                sp.dma_start(xt[:, :, :], xv[b + 2]).then_inc(s_x, 16)
            for b in range(B - 2, B + 1):
                sp.wait_ge(s_rk, b)
                sp.dma_start(partial[b - 1], ob[:, :, :].rearrange("p n d -> p (n d)")).then_inc(s_out, 16)
                sp.wait_ge(s_out, 16 * b)
                sp.nop().then_inc(s_obfree, 1)
                if b == B - 2:
                    sp.wait_ge(s_la, B)
                    sp.wait_ge(s_low, B * (HKV + HQ // 2))
                    sp.dma_start(wup[:, :, :], w_up).then_inc(s_wexp, 16)
            sp.wait_ge(s_pe_end, 1)
            sp.dma_start(wdown[:, :, :, :], w_down.rearrange("e (c p) n -> p e c n", p=P)).then_inc(s_wexp, 16)
            sp.nop().then_inc(s_ysfree, 1)
            sp.wait_ge(s_scat, 16 * B * NT)
            sp.dma_start(xs[:, :, :], sxv[0]).then_inc(s_xs, 16)
            with sp.Fori(1, NS // SG) as i:
                sp.wait_ge(s_xst, i)
                sp.dma_start(xs[:, :, :], sxv[i]).then_inc(s_xs, 16)
                sp.wait_ge(s_ys, i)
                sp.dma_start(syv[i - 1], ys[:, :, :]).then_inc(s_yst, 16)
                sp.wait_ge(s_yst, 16 * i)
                sp.nop().then_inc(s_ysfree, 1)
            sp.wait_ge(s_ys, NS // SG)
            sp.dma_start(syv[NS // SG - 1], ys[:, :, :]).then_inc(s_yst, 16)
            sp.dma_start(ob[:, :, :].rearrange("p n d -> p (n d)"), partial[0]).then_inc(s_pin, 16)
            with sp.Fori(1, B) as i:
                sp.wait_ge(s_fin, i)
                sp.dma_start(ov[i - 1], ob[:, :, :]).then_inc(s_done, 16)
                sp.wait_ge(s_done, 16 * i)
                sp.dma_start(ob[:, :, :].rearrange("p n d -> p (n d)"), partial[i]).then_inc(s_pin, 16)
            sp.wait_ge(s_fin, B)
            sp.dma_start(ov[B - 1], ob[:, :, :]).then_inc(s_done, 16)
            sp.wait_ge(s_done, 16 * B)

        ROOTS = {"LN": (2, 3), "LM": (4, 5), "H1": (6, 7), "LY": (8, 9)}

        @block.gpsimd
        def _(pool):
            nc.gpsimd.memset(half[:, :], -0.5).then_inc(s_half, 1)
            pool.wait_ge(s_half, 1)
            nc.gpsimd.memset(ob_zero[:, :], 0.0).then_inc(s_half, 1)
            pool.wait_ge(s_half, 2)
            for i in range(NS // SG):
                pool.dma_start(sxv[i].rearrange("p k d -> p k d"),
                               ob_zero[:, :].unsqueeze(1).to_broadcast([P, SG, D])).then_inc(s_zero, 16)

            def body(b, which):
                for kind, rel, i in order.steps[which]:
                    if kind in ROOTS:
                        pool.wait_ge(s_var, order.value(b, which, "var", kind, rel, i))
                        a, o = ROOTS[kind]
                        nc.gpsimd.tensor_tensor(st[:, o, :], st[:, a, :], half[:, :], ALU.pow).then_inc(s_rstd, 1)

            run_bodies(pool, body)
            pool.wait_ge(s_zero, 16 * (NS // SG))
            pool.wait_ge(s_slot, 1)
            pool.wait_ge(s_act_end, 1)
            for t in range(B * NT):
                pool.indirect_dma_start(sorted_x[:, :], bass.IndirectOffsetOnAxis(ap=slot[:, t:t + 1], axis=0),
                                        xf_all[:, t, :], None).then_inc(s_scat, 16)
            pool.wait_ge(s_yst, 16 * (NS // SG))
            for i in range(B):
                if i >= 2:
                    pool.wait_ge(s_fin, i - 1)
                for n in range(NT):
                    t = i * NT + n
                    pool.indirect_dma_start(yg[i % 2][:, n, :], None, sorted_y[:, :],
                                            bass.IndirectOffsetOnAxis(ap=slot[:, t:t + 1], axis=0))\
                        .then_inc(s_yg[i % 2], 16)

        @block.tensor
        def _(pe):
            pe.wait_ge(s_const, 1)
            pe.wait_ge(s_load, 16 * NLOAD)

            def split_product(out_, lh, ll, rh, rl):
                nc.tensor.matmul(out_, lh, rh, start=True, stop=False)
                nc.tensor.matmul(out_, lh, rl, start=False, stop=False)
                return nc.tensor.matmul(out_, ll, rh, start=False, stop=True)

            def body(b, which):
                ring = order.ring(which)

                def at(name, kind, rel, i):
                    return order.value(b, which, name, kind, rel, i)

                for kind, rel, i in order.steps[which]:
                    if (kind, rel, i) in ring:
                        k, old = ring[kind, rel, i]
                        bk = side_bank[k]
                        by_dve = {"BL": ("XN", rel, 0), "LT": ("CO", rel, NT - 1)}.get(kind)
                        by_act = {"CO": ("LV", rel, 0), "CU": ("CK", rel, i), "LY": ("LT", rel, 0),
                                  "LG": ("XF", rel, 0)}.get(kind)
                        read = order.last(which, "ed", [by_dve, old])
                        if read is not None:
                            pe.wait_ge(s_ed, at("ed", *read))
                        read = order.last(which, "ea", [by_act, old])
                        if read is not None:
                            pe.wait_ge(s_ea, at("ea", *read))
                    if kind == "M":
                        n, qt = i
                        r, k = before(n * NT + qt, 2, HQ * NT)
                        when(pe, s_mx, at("mx", "M", rel + r, (k // NT, k % NT)))
                        if qt == 0:
                            parts = [("QL", rel, n // 2), ("KL", rel, n // G)]
                            pe.wait_ge(s_low, at("low", *order.last(which, "low", parts)))
                        w = (qt + 1) * P
                        bk = score_bank[qt % 2]
                        nc.tensor.matmul(bk[:, 0:w], tile(qs[:, n, :], qt), kh[:, n // G, 0:w], start=True, stop=False)
                        nc.tensor.matmul(bk[:, w - P:w], ident_b, mask_qk_b, start=False, stop=True).then_inc(s_sc, 1)
                    elif kind == "T":
                        pe.wait_ge(s_mx, at("mx", "M", rel, (i * G + G - 1, NT - 1)))
                        for qt in range(NT):
                            last = nc.tensor.transpose(tile(bk[0:G, :], qt), negm[:, i % 2, qt, :], const("ident"))
                        last.then_inc(s_fill, 1)
                    elif kind == "S":
                        n, piece = i
                        h = n // G
                        if n % G == 0 and piece == 0:
                            pe.wait_ge(s_ea, at("ea", "T", rel, h))
                        r, k = before(n * 3 + piece, 2, HQ * 3)
                        when(pe, s_p, at("p", "S", rel + r, (k // 3, k % 3)))
                        js = PIECES[piece]
                        bk = exp_bank[(n * 3 + piece) % 2]
                        for j in js:
                            o = POFF[j] - POFF[js[0]]
                            dst = bk[:, o:o + T - P * j]
                            nc.tensor.matmul(dst, tile(kh[:, h, :], j), qs[:, n, j * P:], start=True, stop=False)
                            nc.tensor.matmul(dst, tile(klo[:, h, :], j), qs[:, n, j * P:], start=False, stop=False)
                            nc.tensor.matmul(dst, pick_row(G, n % G), negmT[:, h % 2, j * P:], start=False, stop=False)
                            last = nc.tensor.matmul(bk[:, o:o + P], ident_b, mask_kq_b, start=False, stop=True)
                        last.then_inc(s_ex, 1)
                    elif kind == "V":
                        pe.wait_ge(s_p, at("p", "S", rel, (i, 2)))
                        if i == 0:
                            pe.wait_ge(s_ea, at("ea", "VP", rel, 1))
                        r, k = before(i, 1, HQ)
                        when(pe, s_o, at("o", "V", rel + r, k))
                        h = i // G
                        for j in range(NT):
                            block = v1[:, 2 * j + h // 2, h % 2:h % 2 + 2, :].rearrange("p a d -> p (a d)")
                            last = nc.tensor.matmul(out_bank[:, j * P:], block, pt[:, i % 2, POFF[j]:POFF[j] + T - P * j],
                                                    start=(j == 0), stop=(j == NT - 1), skip_group_check=True)
                        last.then_inc(s_pv, 1)
                    elif kind == "WO":
                        pe.wait_ge(s_nrm, at("nrm", "RM", rel, i))
                        if i == 0:
                            when(pe, s_xf, at("xf", "H1", rel - 1, 0))
                        for qt in range(NT):
                            last = nc.tensor.matmul(tile(wo_bank, qt), tile(oT[:, i % 2, :], qt), wout[:, i, :],
                                                    start=(i == 0 and qt == 0), stop=True, skip_group_check=True)
                        last.then_inc(s_wo, 1)
                    elif kind in ("XN", "XG"):
                        pe.wait_ge(s_norm, at("norm", {"XN": "LN", "XG": "LM"}[kind], rel, 0))
                        src = {"XN": xn, "XG": xg}[kind]
                        for n in range(NT):
                            last = nc.tensor.transpose(tile(bk, n), src[:, n, :], const("ident"))
                        last.then_inc(s_fill, 1)
                    elif kind == "BL":
                        for n in range(NT):
                            last = split_product(bk[:, n * LH:(n + 1) * LH], tile(xn_h, n), tile(xn_l, n),
                                                 wlin_h[:, 5 * D:], wlin_l[:, 5 * D:])
                        last.then_inc(s_fill, 1)
                    elif kind == "LP":
                        w = slice(i * D, (i + 1) * D)
                        split_product(bk[:, :], wlin_h[:, w], wlin_l[:, w], xn_h[:, :], xn_l[:, :]).then_inc(s_fill, 1)
                    elif kind == "LV":
                        for n in range(NT):
                            last = split_product(tile(bk, n), tile(xn_h, n), tile(xn_l, n),
                                                 wlin_h[:, 4 * D:5 * D], wlin_l[:, 4 * D:5 * D])
                        last.then_inc(s_fill, 1)
                    elif kind == "VP":
                        for k in range(2):
                            n = 2 * i + k
                            last = split_product(bk[:, k * 256:(k + 1) * 256], tile(xg_h, n), tile(xg_l, n),
                                                 watt_h[:, WV:WV + 256], watt_l[:, WV:WV + 256])
                        last.then_inc(s_fill, 1)
                    elif kind in ("Q", "K"):
                        pe.wait_ge(s_xl, at("xl", "XL", rel, 0))
                        k, x_ = i
                        o = {"Q": (WQ, WQX), "K": (WK, WKX)}[kind][x_] + k * P
                        split_product(bk[:, :], watt_h[:, o:o + P], watt_l[:, o:o + P], xg_h[:, :], xg_l[:, :])\
                            .then_inc(s_fill, 1)
                    elif kind == "LB":
                        pe.wait_ge(s_beta, at("beta", "BE", rel, 0))
                        for n in range(NT):
                            last = nc.tensor.matmul(tile(bk, n), bet[i][:, n, :, :].rearrange("p h d -> p (h d)"),
                                                    const("ident"), start=True, stop=True)
                        last.then_inc(s_fill, 1)
                    elif kind == "CK":
                        pe.wait_ge(s_lin, at("lin", "LQ", rel, 0))
                        nc.tensor.transpose(bk[:, 0:P], tile(kl, i), const("ident")).then_inc(s_fill, 1)
                    elif kind == "CS":
                        c, q = i
                        pe.wait_ge(s_qm, at("qm", "CQ", rel, c))
                        r = slice(32 * q, 32 * q + 32)
                        nc.tensor.matmul(bk[:, :], kl[r, c * P:(c + 1) * P],
                                         qm[r, c % 2, :, :].rearrange("p g t -> p (g t)"),
                                         start=True, stop=True).then_inc(s_fill, 1)
                    elif kind == "CO":
                        if i >= 1:
                            pe.wait_ge(s_st, at("st", "CU", rel, i - 1))
                        nc.tensor.matmul(bk[:, 0:LH * LV], tile(ql, i), state[:, :], start=True, stop=False,
                                         skip_group_check=True)
                        pe.wait_ge(s_ed, at("ed", "CS", rel, (i, 3)))
                        for hd in range(LH):
                            last = nc.tensor.matmul(bk[:, hd * LV:(hd + 1) * LV], am[:, hd, :],
                                                    v9[:, i, hd, :], start=False, stop=True, skip_group_check=True)
                        last.then_inc(s_fill, 1)
                    elif kind == "CU":
                        nc.tensor.matmul(bk[:, 0:LH * LV], kt[:, :], v9[:, i, :, :].rearrange("p h e -> p (h e)"),
                                         start=True, stop=True).then_inc(s_fill, 1)
                    elif kind == "LT":
                        for n in range(NT):
                            last = nc.tensor.transpose(tile(bk, n), at_l[:, n, :], const("ident"))
                        last.then_inc(s_fill, 1)
                    elif kind == "LY":
                        for n in range(NT):
                            last = nc.tensor.matmul(tile(bk, n), tile(atT, n), wlout[:, :], start=True, stop=True)
                        last.then_inc(s_fill, 1)
                    elif kind == "XF":
                        pe.wait_ge(s_xf, at("xf", "H1", rel, 0))
                        for n in range(NT):
                            last = nc.tensor.transpose(tile(bk, n), xf[:, n, :], const("ident"))
                        last.then_inc(s_fill, 1)
                    elif kind == "LG":
                        for n in range(NT):
                            last = nc.tensor.matmul(bk[:, n * E:(n + 1) * E], tile(xfT, n), wrt[:, :],
                                                    start=True, stop=True)
                        last.then_inc(s_fill, 1)
                    elif kind == "PC":
                        pe.wait_ge(s_oh, at("oh", "LG", rel, 0))
                        for n in range(NT):
                            dst = bk[:, n * 2 * E:(n + 1) * 2 * E]
                            nc.tensor.matmul(dst, const("upto"), oh[:, n, :, :].rearrange("p k e -> p (k e)"),
                                             start=True, stop=False)
                            last = nc.tensor.matmul(dst, const("ones"), ohc[:, n, :, :].rearrange("p k e -> p (k e)"),
                                                    start=False, stop=True)
                        last.then_inc(s_fill, 1)
                    elif kind == "RK":
                        pe.wait_ge(s_pick, at("pick", "PC", rel, 0))
                        for n in range(NT):
                            dst = bk[:, n * E:(n + 1) * E]
                            nc.tensor.matmul(dst, const("upto"), pick[:, n, :], start=True, stop=False)
                            last = nc.tensor.matmul(dst, const("ones"), pickc[:, n, :], start=False, stop=True)
                        last.then_inc(s_fill, 1)

            run_bodies(pe, body)
            pe.nop().then_inc(s_pe_end, 1)
            pe.wait_ge(s_act_end, 1)
            pe.wait_ge(s_dve_end, 1)
            nc.tensor.matmul(bank[0][:, 0:E], const("ones"), pcarry[:, :], start=True, stop=True).then_inc(s_tot, 1)
            pe.wait_ge(s_wexp, 32)
            pe.wait_ge(s_expert, 1)
            with pe.Fori(0, NS // SG) as i:
                pe.wait_ge(s_xs, 16 * i + 16)
                for k in range(SG):
                    last = nc.tensor.transpose(tile(bank[0], k), xs[:, k, :], const("ident"))
                last.then_inc(s_xst, 1)
                pe.wait_ge(s_xstc, i + 1)
                es = []
                for k in range(SG):
                    es.append(pe.value_load(expert[0:1, bass.ds(i * SG + k, 1)], min_val=0, max_val=E - 1))
                    nc.tensor.matmul(bank[1 + k][:, :], xsT[:, k, :],
                                     wup[:, bass.ds(es[k], 1), :].rearrange("p e n -> p (e n)"),
                                     start=True, stop=True).then_inc(s_eup, 1)
                for k in range(SG):
                    pe.wait_ge(s_ehg, i * SG + k + 1)
                    for c in range(2):
                        last = nc.tensor.transpose(bank[5 + k // 2][:, (k % 2) * HID + c * P:(k % 2) * HID + (c + 1) * P],
                                                   ehg[:, k, c * P:(c + 1) * P], const("ident"))
                    if k % 2 == 1:
                        last.then_inc(s_eht, 1)
                for k in range(SG):
                    pe.wait_ge(s_ehtc, i * 2 + k // 2 + 1)
                    for c in range(2):
                        o = (k % 2) * HID + c * P
                        last = nc.tensor.matmul(tile(bank[7], k), eht[k // 2][:, o:o + P],
                                                wdown[:, bass.ds(es[k], 1), c, :].rearrange("p e n -> p (e n)"),
                                                start=(c == 0), stop=(c == 1))
                last.then_inc(s_ey, 1)

        @block.scalar
        def _(act):
            act.wait_ge(s_load, 16 * NLOAD)
            nc.scalar.activation(watt_h[:, :], watt[:, :], ACT.Copy)
            nc.scalar.activation(wlin_h[:, :], wlin[:, :], ACT.Copy).then_inc(s_wsplit, 1)

            def body(b, which):
                ring = order.ring(which)

                def at(name, kind, rel, i):
                    return order.value(b, which, name, kind, rel, i)

                def empty(dst, src, step):
                    act.wait_ge(s_fill, at("fill", *step))
                    nc.scalar.activation(dst, src, ACT.Copy).then_inc(s_ea, 1)

                for step in order.steps[which]:
                    kind, rel, i = step
                    bk = side_bank[ring[step][0]] if step in ring else None
                    if kind == "V":
                        if i % 2 == 0:
                            r, k = before(i // 2, 2, HQ // 2)
                            when(act, s_wo, at("wo", "WO", rel + r, k))
                            r, k = before(i // 2, 1, HQ // 2)
                            when(act, s_nrm, at("nrm", "RM", rel + r, k))
                        act.wait_ge(s_pv, at("pv", *step))
                        num, den = (slice(0, HD), slice(HD, P)) if (i // G) % 2 == 0 else (slice(HD, P), slice(0, HD))
                        mine = slice((i % 2) * HD, (i % 2 + 1) * HD)
                        nc.scalar.activation(rden[mine, :], out_bank[den, :], ACT.Copy)
                        nc.scalar.activation(oT[mine, (i // 2) % 2, :], out_bank[num, :], ACT.Copy).then_inc(s_o, 1)
                    elif kind == "S":
                        n, piece = i
                        if piece == 0:
                            r, k = before(n, 2, HQ)
                            when(act, s_pv, at("pv", "V", rel + r, k))
                        act.wait_ge(s_ex, at("ex", *step))
                        js = PIECES[piece]
                        w = sum(T - P * j for j in js)
                        nc.scalar.activation(pt[:, n % 2, POFF[js[0]]:POFF[js[0]] + w],
                                             exp_bank[(n * 3 + piece) % 2][:, 0:w], ACT.Exp,
                                             scale=HD ** -0.5).then_inc(s_p, 1)
                    elif kind == "T":
                        empty(negmT[:, i % 2, :], bk[0:G, :], step)
                    elif kind == "VP":
                        empty(v1[:, 4 * i:4 * i + 4, 0:3:2, :], bk[:, :].rearrange("p (m h d) -> p m h d", m=4, h=2), step)
                    elif kind == "LV":
                        empty(v9[:, :, :, 0:LD], bk[:, :].rearrange("p (n h d) -> p n h d", n=NT, h=LH), step)
                    elif kind == "CK":
                        empty(kt[:, :], bk[:, 0:P], step)
                    elif kind == "LT":
                        empty(atT[:, :], bk[:, :], step)
                    elif kind == "XF":
                        act.wait_ge(s_fill, at("fill", *step))
                        nc.scalar.activation(xfT[:, :], bk[:, :], ACT.Copy)
                        nc.scalar.activation(xf_all[:, bass.ds(b * NT - NT, NT), :], xf[:, :, :], ACT.Copy)\
                            .then_inc(s_ea, 1)
                    elif kind == "XN":
                        act.wait_ge(s_fill, at("fill", *step))
                        nc.scalar.activation(xn_h[:, :], bk[:, :], ACT.Copy).then_inc(s_hi, 1)
                    elif kind == "XH":
                        act.wait_ge(s_ed, at("ed", "XG", rel, 0))
                        nc.scalar.activation(xg_h[:, :], xgt[:, :], ACT.Copy).then_inc(s_hi, 1)
                    elif kind == "KH":
                        act.wait_ge(s_rot, at("rot", *step))
                        nc.scalar.activation(kh[:, i, :], rot[:, PROJ.index(f"K{i}") % 2, :], ACT.Copy).then_inc(s_hi, 1)
                    elif kind == "QH":
                        act.wait_ge(s_rot, at("rot", *step))
                        src = rot[:, PROJ.index(f"Q{i}") % 2, :]
                        nc.scalar.activation(qs[0:HD, 2 * i, :], src[0:HD, :], ACT.Copy)
                        nc.scalar.activation(qs[HD:P, 2 * i + 1, :], src[HD:P, :], ACT.Copy).then_inc(s_hi, 1)
                    elif kind == "BX":
                        act.wait_ge(s_ed, at("ed", "BL", rel, 0))
                        nc.scalar.activation(zb[:, 1], zb[:, 0], ACT.Exp, scale=-1.0).then_inc(s_zbe, 1)
                    elif kind == "EE":
                        act.wait_ge(s_elu, at("elu", *step))
                        nc.scalar.activation(r_m[:, i, :], r_m[:, i, :], ACT.Exp).then_inc(s_eluexp, 1)
                    elif kind == "DX":
                        act.wait_ge(s_dif, at("dif", *step))
                        nc.scalar.activation(tk[:, 0, :, 1], tk[:, 0, :, 0], ACT.Exp).then_inc(s_dexp, 1)

            run_bodies(act, body)
            act.nop().then_inc(s_act_end, 1)
            with act.Fori(0, NS // SG) as i:
                act.wait_ge(s_xst, i + 1)
                nc.scalar.activation(xsT[:, :, :], bank[0][:, :].rearrange("p (k t) -> p k t", k=SG), ACT.Copy)\
                    .then_inc(s_xstc, 1)
                for k in range(SG):
                    act.wait_ge(s_eup, i * SG + k + 1)
                    nc.scalar.activation(ehc[:, k, :], bank[1 + k][:, 0:HID], ACT.Copy).then_inc(s_ehc, 1)
                for k in range(SG):
                    act.wait_ge(s_ehp, i * SG + k + 1)
                    nc.scalar.activation(ehg[:, k, :], ehp[:, k, :], ACT.Gelu).then_inc(s_ehg, 1)
                act.wait_ge(s_ey, i + 1)
                act.wait_ge(s_ysfree, i + 1)
                nc.scalar.activation(ys[:, :, :], bank[7][:, :].rearrange("p (k d) -> p k d", k=SG), ACT.Copy)\
                    .then_inc(s_ys, 1)

        @block.vector
        def _(dve):
            v = nc.vector
            links = [0]

            def setup(ins):
                links[0] += 1
                ins.then_inc(s_setup, 1)
                dve.wait_ge(s_setup, links[0])

            dve.wait_ge(s_load, 16 * NLOAD)
            v.memset(v9[:, :, :, LD:LV], 1.0)
            v.memset(v1[:, :, 1, :], 1.0)
            v.memset(carry[:, :, :], 0.0)
            v.memset(pcarry[:, :], 0.0)
            v.tensor_copy(ident_r[:, :], const("ident")[:, 0:G])
            setup(v.tensor_copy(cb[:, :], c_all[:, 0:3 * P]))
            dve.wait_ge(s_wsplit, 1)
            v.tensor_tensor(watt_l[:, :], watt[:, :], watt_h[:, :], ALU.subtract)
            v.tensor_tensor(wlin_l[:, :], wlin[:, :], wlin_h[:, :], ALU.subtract).then_inc(s_const, 1)
            chain_before = {-1: 0}

            def body(b, which):
                ring = order.ring(which)
                count = [0]
                base = b * CHAIN + chain_before[which] - CHAIN if which == 1 else chain_before[which]

                def at(name, kind, rel, i):
                    return order.value(b, which, name, kind, rel, i)

                def link(ins):
                    count[0] += 1
                    ins.then_inc(s_chain, 1)
                    dve.wait_ge(s_chain, base + count[0])

                def filled(step):
                    dve.wait_ge(s_fill, at("fill", *step))

                def emptied(ins, step):
                    ins.then_inc(s_ed, 1)
                    dve.wait_ge(s_ed, at("ed", *step))

                def mean_square(src, step, eps):
                    link(v.tensor_tensor(sq[:, :, :], src, src, ALU.mult))
                    link(v.tensor_reduce(st[:, 0, :], sq[:, :, :], AX.X, ALU.add))
                    v.tensor_scalar(st[:, ROOTS[step[0]][0], :], st[:, 0, :], 1.0 / D, eps, ALU.mult, ALU.add)\
                        .then_inc(s_var, 1)
                    dve.wait_ge(s_rstd, at("rstd", *step))
                    return bcast(st[:, ROOTS[step[0]][1], :], D)

                own = (s_la, at("la", "LY", 0, 0))
                if own[1] is None:
                    own = (s_nrm, at("nrm", "RM", -1, HQ // 2 - 2))
                if own[1] is None:
                    own = (s_setup, 1)

                for step in order.steps[which]:
                    kind, rel, i = step
                    bk = side_bank[ring[step][0]] if step in ring else None
                    if kind == "M":
                        n, qt = i
                        h = n // G
                        if n % G == 0 and qt == 0:
                            r, k = before(h, 2, HKV)
                            when(dve, s_fill, at("fill", "T", rel + r, k))
                        dve.wait_ge(s_sc, at("sc", *step))
                        v.tensor_reduce(negm[:, h % 2, qt, n % G:n % G + 1], score_bank[qt % 2][:, 0:(qt + 1) * P],
                                        AX.X, ALU.max, negate=True).then_inc(s_mx, 1)
                        continue
                    if kind in ("RC", "RM", "H1", "XR", "LN", "LM", "XN", "XG", "XL", "BL", "BE", "LP", "LE", "LB", "LQ", "CQ",
                                "CS", "CO", "CU", "YC", "LY", "LG", "PC", "RK", "Q", "QL", "K", "KL"):
                        dve.wait_ge(*own)
                    if kind == "RC":
                        k, part = i
                        dve.wait_ge(s_o, at("o", "V", rel, 2 * k + 1))
                        v.reciprocal(rden[:, part * P:(part + 1) * P], rden[:, part * P:(part + 1) * P]).then_inc(s_rec, 1)
                        own = (s_rec, at("rec", *step))
                    elif kind == "RM":
                        v.tensor_tensor(oT[:, i % 2, :], oT[:, i % 2, :], rden[:, :], ALU.mult).then_inc(s_nrm, 1)
                        own = (s_nrm, at("nrm", *step))
                    elif kind == "LN":
                        dve.wait_ge(s_x, 16 * b + 16 * (rel + 1))
                        link(v.tensor_reduce(st[:, 0, :], xt[:, :, :], AX.X, ALU.add))
                        link(v.tensor_scalar(st[:, 1, :], st[:, 0, :], 1.0 / D, None, ALU.mult))
                        link(v.tensor_tensor(xn[:, :, :], xt[:, :, :], bcast(st[:, 1, :], D), ALU.subtract))
                        root = mean_square(xn[:, :, :], step, LN_EPS)
                        v.tensor_tensor(xn[:, :, :], xn[:, :, :], root, ALU.mult).then_inc(s_norm, 1)
                        own = (s_norm, at("norm", *step))
                    elif kind == "LM":
                        root = mean_square(xn[:, :, :], step, EPS)
                        v.tensor_tensor(xg[:, :, :], xn[:, :, :], root, ALU.mult).then_inc(s_norm, 1)
                        own = (s_norm, at("norm", *step))
                    elif kind == "XR":
                        v.tensor_copy(xres[:, :, :], xn[:, :, :]).then_inc(s_res, 1)
                        own = (s_res, at("res", *step))
                    elif kind == "XN":
                        filled(step)
                        dve.wait_ge(s_hi, at("hi", *step))
                        v.tensor_tensor(xn_l[:, :], bk[:, :], xn_h[:, :], ALU.subtract).then_inc(s_ed, 1)
                        own = (s_ed, at("ed", *step))
                    elif kind == "XG":
                        filled(step)
                        v.tensor_scalar(xgt[:, :], bk[:, :], g1_sb[:, :], None, ALU.mult).then_inc(s_ed, 1)
                        own = (s_ed, at("ed", *step))
                    elif kind == "XL":
                        dve.wait_ge(s_hi, at("hi", "XH", rel, 0))
                        v.tensor_tensor(xg_l[:, :], xgt[:, :], xg_h[:, :], ALU.subtract).then_inc(s_xl, 1)
                        own = (s_xl, at("xl", *step))
                    elif kind == "BL":
                        filled(step)
                        v.tensor_tensor(zb[:, 0], bk[:, 0:NT * LH].rearrange("p (n h) -> p n h", n=NT),
                                        row("bb").unsqueeze(1).to_broadcast([P, NT, LH]), ALU.add).then_inc(s_ed, 1)
                        own = (s_ed, at("ed", *step))
                    elif kind == "BE":
                        dve.wait_ge(s_zbe, at("zbe", "BX", rel, 0))
                        link(v.tensor_scalar(zb[:, 2], zb[:, 1], 1.0, None, ALU.add))
                        link(v.reciprocal(zb[:, 3], zb[:, 2]))
                        link(v.tensor_scalar(zb[:, 0], zb[:, 3], 0.8, 0.999, ALU.max, ALU.min))
                        link(v.reciprocal(zb[:, 1], zb[:, 0]))
                        for k in range(2):
                            last = v.tensor_copy(bet[k], zb[:, k].unsqueeze(3).to_broadcast([P, NT, LH, LD]))
                        last.then_inc(s_beta, 1)
                        own = (s_beta, at("beta", *step))
                    elif kind == "LP":
                        filled(step)
                        k = i // 2
                        if i % 2 == 0:
                            v.tensor_tensor(r_a[:, k, :], bk[:, :], const("cos_l"), ALU.mult).then_inc(s_ed, 1)
                            own = (s_ed, at("ed", *step))
                        else:
                            emptied(v.tensor_tensor(r_sin[:, :], bk[:, :], const("sin_l"), ALU.mult), step)
                            link(v.tensor_tensor(r_a[:, k, :], r_a[:, k, :], r_sin[:, :], ALU.add))
                            v.tensor_scalar(r_m[:, k, :], r_a[:, k, :], 0.0, None, ALU.min).then_inc(s_elu, 1)
                            own = (s_elu, at("elu", "EE", rel, k))
                    elif kind == "LE":
                        dve.wait_ge(s_eluexp, at("eluexp", "EE", rel, i))
                        v.scalar_tensor_tensor(qk_l[:, i, :], r_a[:, i, :], 0.0, r_m[:, i, :], ALU.max, ALU.add)\
                            .then_inc(s_lphi, 1)
                        own = (s_lphi, at("lphi", *step))
                    elif kind == "LB":
                        filled(step)
                        for c in range(NT):
                            t = slice(c * P, (c + 1) * P)
                            last = v.tensor_tensor_scan(dec[:, i, t], bk[:, t], const("ones"), 1.0, ALU.mult, ALU.mult)
                        last.then_inc(s_ed, 1)
                        own = (s_ed, at("ed", *step))
                    elif kind == "LQ":
                        v.tensor_tensor(ql[:, :], ql[:, :], dec[:, 0, :], ALU.mult)
                        v.tensor_tensor(kl[:, :], kl[:, :], dec[:, 1, :], ALU.mult)
                        v.memset(state[:, :], 0.0).then_inc(s_lin, 1)
                        own = (s_lin, at("lin", *step))
                    elif kind == "CQ":
                        for g in range(G):
                            last = v.tensor_scalar(qm[:, i % 2, g, :], ql[:, i * P:(i + 1) * P],
                                                   const("quad")[:, g:g + 1], None, ALU.mult)
                        last.then_inc(s_qm, 1)
                        own = (s_qm, at("qm", *step))
                    elif kind == "CS":
                        filled(step)
                        c, q = i
                        v.tensor_tensor(am[:, 4 * q:4 * q + 4, :], bk[:, :].rearrange("p (g t) -> p g t", g=4),
                                        const("upto").unsqueeze(1).to_broadcast([P, G, P]), ALU.mult).then_inc(s_ed, 1)
                        own = (s_ed, at("ed", *step))
                    elif kind == "CO":
                        filled(step)
                        acc = bk[:, 0:LH * LV].rearrange("p (h e) -> p h e", h=LH)
                        link(v.tensor_scalar(rden_l[:, :], acc[:, :, LD:LV].rearrange("p h e -> p (h e)"), EPS, None,
                                             ALU.add))
                        link(v.reciprocal(rden_l[:, :], rden_l[:, :]))
                        v.tensor_tensor(at_l[:, i, :].rearrange("p (h d) -> p h d", h=LH), acc[:, :, 0:LD],
                                        bcast(rden_l[:, :], LD), ALU.mult).then_inc(s_ed, 1)
                        own = (s_ed, at("ed", *step))
                    elif kind == "CU":
                        filled(step)
                        emptied(v.tensor_tensor(stt[:, :], bk[:, 0:LH * LV], const("diag"), ALU.mult), step)
                        link(v.tensor_tensor(stt[:, :], stt[:, :], state[:, :], ALU.add))
                        v.tensor_scalar(state[:, :], stt[:, :], dec[:, 0, (i + 1) * P - 1:(i + 1) * P], None, ALU.mult)\
                            .then_inc(s_st, 1)
                        own = (s_st, at("st", *step))
                    elif kind == "YC":
                        if which != 0:
                            dve.wait_ge(s_obfree, b)
                        v.tensor_copy(ylp[:, :, :], yl[:, :, :]).then_inc(s_ylp, 1)
                        own = (s_ylp, at("ylp", *step))
                    elif kind == "LY":
                        filled(step)
                        emptied(v.tensor_tensor(yl[:, :, :], xn[:, :, :], bk[:, :].rearrange("p (n d) -> p n d", n=NT),
                                                ALU.add), step)
                        link(v.tensor_tensor(yl[:, :, :], yl[:, :, :],
                                             row("bo").unsqueeze(1).to_broadcast([P, NT, D]), ALU.add))
                        root = mean_square(yl[:, :, :], step, EPS)
                        link(v.tensor_tensor(yl[:, :, :], yl[:, :, :], root, ALU.mult))
                        link(v.tensor_tensor(yl[:, :, :], yl[:, :, :],
                                             row("scale").unsqueeze(1).to_broadcast([P, NT, D]), ALU.mult))
                        v.tensor_tensor(yl[:, :, :], yl[:, :, :], xt[:, :, :], ALU.add).then_inc(s_la, 1)
                        own = (s_la, at("la", *step))
                    elif kind == "H1":
                        dve.wait_ge(s_wo, at("wo", "WO", rel, HQ // 2 - 1))
                        link(v.tensor_tensor(h1[:, :, :], xres[:, :, :],
                                             wo_bank[:, :].rearrange("p (n d) -> p n d", n=NT), ALU.add))
                        root = mean_square(h1[:, :, :], step, EPS)
                        link(v.tensor_tensor(xf[:, :, :], h1[:, :, :], root, ALU.mult))
                        v.tensor_tensor(xf[:, :, :], xf[:, :, :], row("g2").unsqueeze(1).to_broadcast([P, NT, D]),
                                        ALU.mult).then_inc(s_xf, 1)
                        own = (s_xf, at("xf", *step))
                    elif kind in ("Q", "K"):
                        filled(step)
                        k, x_ = i
                        r = PROJ.index(f"{kind}{k}") % 2
                        if x_ == 0:
                            v.tensor_tensor(rot[:, r, :], bk[:, :], const("cos_s"), ALU.mult).then_inc(s_ed, 1)
                            own = (s_ed, at("ed", *step))
                        else:
                            emptied(v.tensor_tensor(r_sin[:, :], bk[:, :], const("sin_s"), ALU.mult), step)
                            v.tensor_tensor(rot[:, r, :], rot[:, r, :], r_sin[:, :], ALU.add).then_inc(s_rot, 1)
                            own = (s_rot, at("rot", kind + "H", rel, k))
                    elif kind == "KL":
                        dve.wait_ge(s_hi, at("hi", "KH", rel, i))
                        v.tensor_tensor(klo[:, i, :], rot[:, PROJ.index(f"K{i}") % 2, :], kh[:, i, :], ALU.subtract)\
                            .then_inc(s_low, 1)
                        own = (s_low, at("low", *step))
                    elif kind == "QL":
                        dve.wait_ge(s_hi, at("hi", "QH", rel, i))
                        src = rot[:, PROJ.index(f"Q{i}") % 2, :]
                        v.tensor_tensor(qs[HD:P, 2 * i, :], src[0:HD, :], qs[0:HD, 2 * i, :], ALU.subtract)
                        v.tensor_tensor(qs[0:HD, 2 * i + 1, :], src[HD:P, :], qs[HD:P, 2 * i + 1, :], ALU.subtract)\
                            .then_inc(s_low, 1)
                        own = (s_low, at("low", *step))
                    elif kind == "LG":
                        filled(step)
                        emptied(v.tensor_tensor(lg[:, 0], bk[:, 0:NT * E].rearrange("p (n e) -> p n e", n=NT),
                                                row("router_b").unsqueeze(1).to_broadcast([P, NT, E]), ALU.add), step)
                        less = const("less").unsqueeze(1).to_broadcast([P, NT, E])
                        for k in range(2):
                            link(v.tensor_reduce(mx[:, k, :], lg[:, k], AX.X, ALU.max))
                            link(v.tensor_tensor(eq[:, :, :], lg[:, k], bcast(mx[:, k, :], E), ALU.is_equal))
                            link(v.tensor_tensor(eq[:, :, :], eq[:, :, :], less, ALU.mult))
                            link(v.tensor_reduce(mi[:, :], eq[:, :, :], AX.X, ALU.min))
                            link(v.tensor_tensor(oh[:, :, k, :], less, bcast(mi[:, :], E), ALU.is_equal))
                            if k == 0:
                                link(v.scalar_tensor_tensor(lg[:, 1], oh[:, :, 0, :], -3.0e38, lg[:, 0], ALU.mult,
                                                            ALU.add))
                        v.tensor_copy(ohc[:, 0], carry[:, :, :])
                        link(v.tensor_tensor(ohc[:, 1], carry[:, :, :], oh[:, 0], ALU.add))
                        for n in range(2, NT):
                            link(v.tensor_tensor(ohc[:, n], ohc[:, n - 1], oh[:, n - 1], ALU.add))
                        v.tensor_tensor(carry[:, :, :], ohc[:, NT - 1], oh[:, NT - 1], ALU.add).then_inc(s_oh, 1)
                        v.tensor_tensor(tk[:, 0, :, 0], mx[:, 1, :], mx[:, 0, :], ALU.subtract).then_inc(s_dif, 1)
                        own = (s_dif, at("dif", "DX", rel, 0))
                    elif kind == "PC":
                        filled(step)
                        iota = const("iota").unsqueeze(1).to_broadcast([P, NT, E])
                        cnt = bk[:, 0:NT * 2 * E].rearrange("p (n k e) -> p n k e", n=NT, k=2)
                        link(v.tensor_copy(pos[:, :, 0, :], cnt[:, :, 0, :]))
                        emptied(v.tensor_tensor(pos[:, :, 1, :], cnt[:, :, 1, :], pos[:, :, 0, :], ALU.add), step)
                        link(v.scalar_tensor_tensor(em[:, :, :, :].rearrange("p n k e -> p (n k e)"),
                                                    pos[:, :, :, :].rearrange("p n k e -> p (n k e)"), float(CAP),
                                                    oh[:, :, :, :].rearrange("p n k e -> p (n k e)"), ALU.is_lt, ALU.mult))
                        fit = tk[:, 1]
                        link(v.tensor_reduce(fit, em[:, :, :, :], AX.X, ALU.add))
                        for k in range(2):
                            last = v.tensor_tensor(emi[:, :, k, :], em[:, :, k, :], iota, ALU.mult)
                        link(last)
                        link(v.tensor_reduce(tk[:, 2], emi[:, :, :, :], AX.X, ALU.add))
                        link(v.tensor_tensor(tk[:, 3, :, 0], tk[:, 2, :, 0], tk[:, 2, :, 1], ALU.max))
                        v.tensor_copy(pickc[:, 0], pcarry[:, :])
                        link(v.tensor_tensor(pick[:, :, :], iota, tk[:, 3, :, 0:1].to_broadcast([P, NT, E]), ALU.is_equal))
                        link(v.tensor_tensor(pickc[:, 1], pcarry[:, :], pick[:, 0], ALU.add))
                        for n in range(2, NT):
                            link(v.tensor_tensor(pickc[:, n], pickc[:, n - 1], pick[:, n - 1], ALU.add))
                        v.tensor_tensor(pick_all[:, bass.ds(b * NT - NT, NT), :], pick[:, :, :], pick[:, :, :], ALU.max)
                        v.tensor_tensor(pcarry[:, :], pickc[:, NT - 1], pick[:, NT - 1], ALU.add).then_inc(s_pick, 1)
                        own = (s_pick, at("pick", *step))
                    elif kind == "RK":
                        fit = tk[:, 1]
                        dve.wait_ge(s_dexp, at("dexp", "DX", rel, 0))
                        link(v.tensor_scalar(tk[:, 5, :, 0], tk[:, 0, :, 1], 1.0, None, ALU.add))
                        link(v.reciprocal(tk[:, 6, :, 0], tk[:, 5, :, 0]))
                        link(v.tensor_tensor(tk[:, 6, :, 1], tk[:, 6, :, 0], tk[:, 0, :, 1], ALU.mult))
                        link(v.tensor_tensor(tk[:, 7], tk[:, 6], fit, ALU.mult))
                        link(v.tensor_tensor(tk[:, 8], tk[:, 6], tk[:, 7], ALU.subtract))
                        v.tensor_tensor(tk[:, 9, :, 0], tk[:, 7, :, 0], tk[:, 7, :, 1], ALU.add)
                        link(v.tensor_tensor(tk[:, 9, :, 1], tk[:, 8, :, 0], tk[:, 8, :, 1], ALU.add))
                        filled(step)
                        emptied(v.tensor_tensor(eq[:, :, :], bk[:, 0:NT * E].rearrange("p (n e) -> p n e", n=NT),
                                                pick[:, :, :], ALU.mult), step)
                        v.tensor_reduce(rank_all[:, bass.ds(b * NT - NT, NT)], eq[:, :, :], AX.X, ALU.add)
                        v.tensor_tensor(share_all[:, bass.ds(b * NT - NT, NT)], tk[:, 9, :, 0], tk[:, 9, :, 0], ALU.max)
                        link(v.tensor_tensor(xf[:, :, :], xf[:, :, :], tk[:, 9, :, 1:2].to_broadcast([P, NT, D]), ALU.mult))
                        link(v.tensor_tensor(h1[:, :, :], xf[:, :, :], h1[:, :, :], ALU.add))
                        v.tensor_tensor(ob[:, :, :], ylp[:, :, :], h1[:, :, :], ALU.add)\
                            .then_inc(s_rk, 1)
                        own = (s_rk, at("rk", *step))
                if which == 1:
                    assert count[0] == CHAIN, count[0]
                    chain_before[B - 1] = chain_before[1] + (B - 2) * CHAIN
                else:
                    chain_before[{-1: 0, 0: 1, B - 1: B, B: None}[which]] = chain_before[which] + count[0]

            run_bodies(dve, body)
            dve.wait_ge(s_rk, B)
            v.nop().then_inc(s_dve_end, 1)
            step = setup
            dve.wait_ge(s_tot, 1)
            step(v.tensor_copy(total[:, 0], bank[0][:, 0:E]))
            c3 = cmp[:, 0:E * B * NT].rearrange("p (e k) -> p e k", e=E)
            step(v.tensor_tensor(c3, bcast(total[:, 0], B * NT),
                                 const("steps").unsqueeze(1).to_broadcast([P, E, B * NT]), ALU.is_gt))
            step(v.tensor_reduce(total[:, 1], c3, AX.X, ALU.add))
            step(v.tensor_tensor_scan(total[:, 2], const("ones")[:, 0:E], total[:, 1], 0.0, ALU.mult, ALU.add))
            step(v.tensor_tensor(total[:, 3], total[:, 2], total[:, 1], ALU.subtract))
            step(v.tensor_scalar(total[:, 3], total[:, 3], float(P), -1.0, ALU.mult, ALU.add))
            c3 = cmp[:, 0:E * B * NT].rearrange("p (t e) -> p t e", e=E)
            step(v.tensor_tensor(c3, pick_all[:, :, :], total[:, 3].unsqueeze(1).to_broadcast([P, B * NT, E]), ALU.mult))
            step(v.tensor_reduce(slot_f[:, :], c3, AX.X, ALU.add))
            step(v.tensor_tensor(slot_f[:, :], slot_f[:, :], rank_all[:, :], ALU.add))
            v.tensor_copy(slot[:, :], slot_f[:, :]).then_inc(s_slot, 1)
            dve.wait_ge(s_slot, 1)
            c3 = cmp[:, 0:E * NS].rearrange("p (t e) -> p t e", e=E)
            step(v.tensor_tensor(c3, bcast(const("tiles"), E), total[:, 2].unsqueeze(1).to_broadcast([P, NS, E]), ALU.is_ge))
            step(v.tensor_reduce(expert_f[:, :], c3, AX.X, ALU.add))
            v.tensor_scalar(expert[:, :], expert_f[:, :], float(E - 1), None, ALU.min).then_inc(s_expert, 1)
            with dve.Fori(0, NS // SG) as i:
                for k in range(SG):
                    dve.wait_ge(s_ehc, i * SG + k + 1)
                    v.tensor_tensor(ehp[:, k, :], bank[1 + k][:, HID:2 * HID], ehc[:, k, :], ALU.mult).then_inc(s_ehp, 1)
                for k in range(SG // 2):
                    dve.wait_ge(s_eht, i * 2 + k + 1)
                    v.tensor_copy(eht[k], bank[5 + k][:, :]).then_inc(s_ehtc, 1)
            for i in range(B):
                dve.wait_ge(s_yg[i % 2], 16 * NT * (i // 2 + 1))
                step(v.tensor_tensor(yg[i % 2][:, :, :], yg[i % 2][:, :, :],
                                     bcast(share_all[:, i * NT:(i + 1) * NT], D), ALU.mult))
                dve.wait_ge(s_pin, 16 * (i + 1))
                v.tensor_tensor(ob[:, :, :], ob[:, :, :], yg[i % 2][:, :, :], ALU.add).then_inc(s_fin, 1)


def _rope(width, t):
    import numpy as np
    inv = (1.0 / (np.float32(10000.0) ** (np.arange(0, width, 2, dtype=np.float32) / np.float32(width))))
    ang = np.arange(t, dtype=np.float32)[:, None] * inv.astype(np.float32)[None, :]
    ang = np.concatenate([ang, ang], axis=1)
    sign = np.concatenate([-np.ones(width // 2), np.ones(width // 2)]).astype(np.float32)
    cos, sin = np.cos(ang), np.sin(ang) * sign
    return np.tile(cos.T, (P // width, 1)), np.tile(sin.T, (P // width, 1))


def constants():
    import numpy as np
    i = np.arange(P)
    c = {}
    c["ident"] = np.eye(P)
    c["mask_qk"] = np.where(i[None, :] > i[:, None], -1e30, 0.0)
    c["mask_kq"] = c["mask_qk"].T
    c["upto"] = (i[None, :] >= i[:, None]) * 1.0
    c["ones"] = np.ones((P, P))
    c["quad"] = ((i[:, None] // LD) % G == np.arange(G)[None, :]) * 1.0
    c["diag"] = (i[:, None] // LD == (np.arange(LH * LV) // LV)[None, :]) * 1.0
    c["iota"] = np.tile(np.arange(E), (P, 1))
    c["less"] = c["iota"] - E
    c["steps"] = np.tile(np.arange(B * NT) * P, (P, 1))
    c["tiles"] = np.tile(np.arange(NS), (P, 1))
    c["cos_l"], c["sin_l"] = _rope(LD, T)
    c["cos_s"], c["sin_s"] = _rope(HD, T)
    return np.ascontiguousarray(np.concatenate([c[n] for n, _ in CONST], axis=1).astype(np.float32))


def kernel(**inputs):
    import numpy as np
    import concourse.bacc as bacc
    from concourse.bass_utils import run_bass_kernel_spmd

    g = {k: np.asarray(v) for k, v in inputs.items()}

    def exchanged(w, width):
        w = w.reshape(w.shape[0], -1, 2, width // 2)
        return w[:, :, ::-1, :].reshape(w.shape[0], -1)

    wq, wk = g["L0_attn_Wq"].T, g["L0_attn_Wk"].T
    w_lin = np.concatenate([wq, exchanged(wq, LD), wk, exchanged(wk, LD), g["L0_attn_Wv"].T, g["L0_attn_Wb"].T], axis=1)
    fq = g["L0_ffn_wq"].reshape(D, G, HKV, HD).transpose(0, 2, 1, 3).reshape(D, HQ * HD)
    fk = np.repeat(g["L0_ffn_wk"].reshape(D, HKV, 1, HD), 2, axis=2).reshape(D, 2 * HKV * HD)
    w_att = np.concatenate([fq, exchanged(fq, HD), fk, exchanged(fk, HD), g["L0_ffn_wv"]], axis=1)
    w_out = g["L0_ffn_wo"].reshape(G, HKV, HD, D).transpose(1, 0, 2, 3).reshape(HQ * HD, D)
    w_up = np.concatenate([g["L0_ffn_w1"], g["L0_ffn_w2"]], axis=2).transpose(1, 0, 2)
    rows = np.concatenate([g["L0_attn_bb"], g["L0_attn_bo"], g["L0_attn_scale"], g["L0_ffn_g2"], g["L0_ffn_router_b"]])
    arrays = {
        "x": g["L0_attn_x"], "w_lin": w_lin, "w_lout": g["L0_attn_Wo"].T, "w_att": w_att, "w_out": w_out,
        "w_up": w_up, "w_down": g["L0_ffn_w3"], "w_router": g["L0_ffn_router_w"],
        "g1": g["L0_ffn_g1"].reshape(D, 1), "rows": np.tile(rows[None, :], (P, 1)), "consts": constants(),
    }
    arrays = {k: np.ascontiguousarray(v) for k, v in arrays.items()}
    nc = bacc.Bacc("TRN2", target_bir_lowering=False, num_devices=1)
    args = [nc.dram_tensor(k, v.shape, mybir.dt.from_np(v.dtype), kind="ExternalInput").ap() for k, v in arrays.items()]
    args.append(nc.dram_tensor("out", (B, T, D), F32, kind="ExternalOutput").ap())
    attention_kernel(nc, *args)
    return run_bass_kernel_spmd(nc, [arrays], core_ids=[0]).results[0]["out"]
```

```python
import concourse.bass as bass
from concourse import mybir
from contextlib import ExitStack

F32 = mybir.dt.float32
F32R = mybir.dt.float32r
I32 = mybir.dt.int32
BF16 = mybir.dt.bfloat16
U32 = mybir.dt.uint32
ALU = mybir.AluOpType
ACT = mybir.ActivationFunctionType
AX = mybir.AxisListType

B, T, D = 8, 512, 128
P = 128
NT = T // P
LH, LD = 16, 8
LV = LD + 1
HQ, HKV, HD = 16, 4, 64
G = HQ // HKV
E, HID = 8, 256
CAP = (B * T) // 8
SG = 4
NS = -(-(B * NT + E - 1) // SG) * SG
NG = NS // SG
EPS = 1e-6
LN_EPS = 1e-5

CONST = [("ident", P), ("mask_qk", P), ("mask_kq", P), ("upto", P), ("ones", P), ("quad", G),
         ("diag", LH * LV), ("iota", E), ("less", E), ("steps", B * NT), ("tiles", NS),
         ("cos_l", T), ("sin_l", T), ("cos_s", T), ("sin_s", T)]
COFF = {}
_at = 0
for _n, _w in CONST:
    COFF[_n] = (_at, _w)
    _at += _w
NCONST = _at
ROWS = [("bb", LH), ("bo", D), ("scale", D), ("g2", D), ("router_b", E)]
ROFF = {}
_at = 0
for _n, _w in ROWS:
    ROFF[_n] = (_at, _w)
    _at += _w
NROWS = _at


def body_steps():
    side = {n: [] for n in range(HQ)}

    def put(n, at, *steps):
        side[n] += [(at, st) for st in steps]

    def project(n, at, kind, rel, i):
        put(n, at, (kind, rel, (i, 0)))
        put(n, at + 2, (kind, rel, (i, 1)))
        put(n, at + 2, (kind + "H", rel, i))
        put(n, at + 4, (kind + "L", rel, i))

    for n, rel, i in [(1, -1, 7)] + [(2 * i + 3, 0, i) for i in range(7)]:
        for part in range(NT):
            put(n, part + 1, ("RC", rel, (i, part)))
        put(n, NT + 1, ("RM", rel, i))
    put(0, 2, ("WO", -1, 6))
    project(0, 0, "Q", 0, 6)
    project(0, 1, "K", 0, 3)
    put(0, 9, ("VP", 0, 0), ("VP", 0, 1))
    project(1, 1, "Q", 0, 7)
    put(1, 9, ("WO", -1, 7))
    put(2, 1, ("H1", -1, 0))
    put(2, 3, ("XR", 0, 0))
    put(2, 3, ("H1R", -1, 0))
    put(2, 5, ("LN", 1, 0))
    put(3, 0, ("LNR", 1, 0), ("LM", 1, 0))
    put(3, 2, ("XF", -1, 0))
    put(3, 3, ("LMR", 1, 0), ("XN", 1, 0))
    put(3, 7, ("XG", 1, 0))
    put(4, 0, ("XH", 1, 0))
    put(4, 1, ("XL", 1, 0), ("BL", 1, 0))
    put(4, 3, ("LG", -1, 0), ("BX", 1, 0))
    put(4, 5, ("G2", -1, 0))
    project(4, 3, "Q", 1, 0)
    put(4, 8, ("BE", 1, 0))
    for i in range(HQ // 2 - 2):
        put(2 * i + 4, 2, ("WO", 0, i))
    put(5, 1, ("LP", 1, 0))
    put(5, 2, ("LP", 1, 1))
    put(5, 4, ("EE", 1, 0))
    put(5, 5, ("LP", 1, 2))
    put(5, 6, ("LP", 1, 3))
    put(6, 1, ("EE", 1, 1), ("DX", -1, 0))
    project(6, 0, "Q", 1, 1)
    project(6, 2, "K", 1, 0)
    put(6, 6, ("PC", -1, 0))
    put(6, 6, ("P2", -1, 0))
    put(7, 1, ("LE", 1, 0), ("LE", 1, 1))
    put(7, 2, ("LB", 1, 0))
    put(7, 6, ("LB", 1, 1))
    put(7, 7, ("LV", 1, 0), ("LQ", 1, 0))
    project(8, 0, "Q", 1, 2)
    put(8, 2, ("RK", -1, 0))
    put(8, 6, ("R2", -1, 0))
    project(10, 0, "K", 1, 1)
    project(10, 3, "Q", 1, 3)
    project(12, 0, "K", 1, 2)
    project(12, 3, "Q", 1, 4)
    project(14, 0, "Q", 1, 5)
    put(14, 7, ("YC", 0, 0))
    for c in range(NT):
        n = 8 + 2 * c
        put(n - 1, 7, ("CQ", 1, c))
        if c < NT - 1:
            put(n, 1, ("CK", 1, c))
        for q in range(4):
            put(n, 1 + 2 * q, ("CS", 1, (c, q)))
        for q in range(3):
            put(n + 1, q, ("CP", 1, (c, q)))
        put(n + 1, 3, ("CO", 1, c))
        if c < NT - 1:
            put(n + 1, 5, ("CU", 1, c))
    put(15, 5, ("LT", 1, 0))
    put(15, 7, ("LY", 1, 0))
    put(15, 9, ("LYR", 1, 0))
    steps = []
    for n in range(HQ):
        m, r = (n + 4, 0) if n + 4 < HQ else (n + 4 - HQ, 1)
        main = [("M", r, (m, 0)), ("S", 0, (n, 0)), ("M", r, (m, 1)), ("S", 0, (n, 1)), ("M", r, (m, 2)),
                ("S", 0, (n, 2)), ("M", r, (m, 3)), ("V", 0, n - 1) if n else ("V", -1, HQ - 1)]
        for at, st in enumerate(main):
            steps += [x for a, x in side[n] if a == at]
            steps.append(st)
        steps += [x for a, x in side[n] if a > len(main) - 1]
        if n % G == G - 1:
            steps.append(("T", 0, (n + 1) // G) if n + 1 < HQ else ("T", 1, 0))
    return steps


SIDE_DVE = ("Q", "K", "XN", "BL", "LP", "LB", "CS", "CO", "CU", "LY", "LG", "PC", "RK")
SIDE_ACT = ("T", "XG", "VP", "LV", "CK", "LT", "XF")
COUNTED = {
    "fill": SIDE_DVE + SIDE_ACT, "ed": SIDE_DVE, "ea": SIDE_ACT, "sc": ("M",), "mx": ("M",),
    "ex": ("S",), "p": ("S",), "pv": ("V",), "o": ("V",), "rec": ("RC",), "nrm": ("RM",), "wo": ("WO",),
    "hi": ("XN", "XH", "QH", "KH"), "xl": ("XL",), "rot": ("QH", "KH"), "low": ("QL", "KL"),
    "var": ("LN", "LM", "H1", "LY"), "rstd": ("LN", "LM", "H1", "LY"), "norm": ("LNR", "LMR"),
    "xf": ("H1R",), "res": ("XR",), "elu": ("EE",), "eluexp": ("EE",), "lphi": ("LE",), "zbe": ("BX",),
    "beta": ("BE",), "lin": ("LQ",), "qm": ("CQ",), "st": ("CU",), "ylp": ("YC",), "la": ("LYR",),
    "oh": ("G2",), "share": ("RK",), "top": ("LG",), "dif": ("DX",), "dexp": ("DX",), "pick": ("P2",), "rk": ("R2",),
}


class Order:

    def __init__(self):
        full = body_steps()
        self.steps, self.at, self.total = {}, {}, {}
        for b in (-1, 0, 1, B - 1, B):
            mine = [st for st in full if 0 <= b + st[1] < B]
            self.steps[b] = mine
            self.at[b], self.total[b] = {}, {}
            for name, kinds in COUNTED.items():
                count = 0
                for kind, rel, i in mine:
                    if kind in kinds or f"{kind}{i}" in kinds:
                        count += 1
                        self.at[b][name, kind, rel, i] = count
                self.total[b][name] = count

    def base(self, b, body, name):
        t = {k: v[name] for k, v in self.total.items()}
        if body == -1:
            return 0
        if body == 0:
            return t[-1]
        if body == 1:
            return b * t[1] + (t[-1] + t[0] - t[1])
        done = t[-1] + t[0] + (B - 2) * t[1]
        return done if body == B - 1 else done + t[B - 1]

    def value(self, b, body, name, kind, rel, i):
        own = self.at[body].get((name, kind, rel, i))
        if own is not None:
            return self.base(b, body, name) + own
        before = {0: (-1,), 1: (0, 1), B - 1: (1,), B: (B - 1,), -1: ()}[body]
        back = [self.total[q][name] - self.at[q][name, kind, rel + 1, i] for q in before
                if (name, kind, rel + 1, i) in self.at[q]]
        if not back:
            return None
        assert len(back) == len(before), (name, kind, rel, i)
        return self.base(b, body, name) - min(back)

    def last(self, body, name, steps):
        b = 2 if body == 1 else body
        counts = [(self.value(b, body, name, *st), st) for st in steps if st is not None and st[0] in COUNTED[name]]
        counts = [c for c in counts if c[0] is not None]
        return max(counts, key=lambda c: c[0])[1] if counts else None

    def ring(self, body):
        fills = {b: [st for st in self.steps[b] if st[0] in SIDE_DVE + SIDE_ACT] for b in self.steps}
        assert len(fills[1]) % 2 == 0, {b: len(f) for b, f in fills.items()}
        before = {0: -1, 1: 1, B - 1: 1, B: B - 1}.get(body)
        start = self.base(1, body, "fill") % 2 if body != 1 else (len(fills[-1]) + len(fills[0])) % 2
        lead = [(k, r - 1, i) for k, r, i in fills[before][-2:]] if before is not None else [None, None]
        both = lead + fills[body]
        return {st: ((start + n) % 2, both[n]) for n, st in enumerate(fills[body])}


def attention_kernel(nc, x, w_lin, w_lout, w_att, w_out, w_up, w_down, w_router, g1, rows, consts, out):
    ctx = ExitStack()
    with ctx:
        def sb(name, shape, dt=F32):
            return ctx.enter_context(nc.sbuf_tensor(name, shape, dt))

        def sem(name):
            return ctx.enter_context(nc.semaphore(name))

        c_all = sb("c_all", [P, NCONST])
        rows_sb = sb("rows_sb", [P, NROWS])
        g1_sb = sb("g1_sb", [P, 1])
        wlout = sb("wlout", [P, D])
        wout = sb("wout", [P, HQ * HD // P, D])
        wrt = sb("wrt", [P, E])

        def const(name):
            a, w = COFF[name]
            return c_all[:, a:a + w]

        def row(name):
            a, w = ROFF[name]
            return rows_sb[:, a:a + w]

        ident_r = sb("ident_r", [P, G], F32R)
        cb = sb("cb", [P, 3 * P], BF16)
        ident_b, mask_qk_b, mask_kq_b = cb[:, 0:P], cb[:, P:2 * P], cb[:, 2 * P:3 * P]

        def pick_row(n, r):
            return ident_r[0:n, r:r + 1].to_broadcast([n, P])

        NW = 2 * HQ * HD + 4 * HKV * HD + HKV * HD
        watt_h = sb("watt_h", [P, NW], F32R)
        watt_l = sb("watt_l", [P, NW], F32R)
        wlin_h = sb("wlin_h", [P, 5 * D + LH], F32R)
        wlin_l = sb("wlin_l", [P, 5 * D + LH], F32R)

        xt = sb("xt", [P, NT, D])
        xn = sb("xn", [P, NT, D])
        xres = sb("xres", [P, NT, D])
        xg = sb("xg", [P, NT, D])
        sq = sb("sq", [P, NT, D])
        st = sb("st", [P, 10, NT])
        xgt = sq[:, :, :].rearrange("p n d -> p (n d)")
        xn_h = sb("xn_h", [P, T], F32R)
        xn_l = sb("xn_l", [P, T], F32R)
        xg_h = sb("xg_h", [P, T], F32R)
        xg_l = sb("xg_l", [P, T], F32R)
        lin_area = sb("lin_area", [P, 8 * T])
        am_area = lin_area[:, 0:4 * T]
        r_a, rot = (lin_area[:, i * 2 * T:(i + 1) * 2 * T].rearrange("p (a t) -> p a t", a=2) for i in (2, 3))
        r_sin = sb("r_sin", [P, T])
        qk_l = sb("qk_l", [P, 2, T])
        ql, kl = qk_l[:, 0, :], qk_l[:, 1, :]
        dec = sb("dec", [P, 2, T])
        zb = sb("zb", [P, 4, NT, LH])
        qm = sb("qm", [P, 2, G, P])
        v9 = sb("v9", [P, NT, LH, LV])
        kt = sb("kt", [P, D])
        state = sb("state", [P, LH * LV])
        stt = sb("stt", [P, LH * LV])
        rden_l = sb("rden_l", [P, LH])
        h1 = sb("h1", [P, NT, D])
        at_l = h1
        atT = sb("atT", [P, T])
        yl = sb("yl", [P, NT, D])
        ylp = sb("ylp", [P, NT, D])
        r_m = am_area[:, 0:2 * T].rearrange("p (a t) -> p a t", a=2)
        bet = [am_area[:, i * T:(i + 1) * T].rearrange("p (n h d) -> p n h d", n=NT, h=LH) for i in (2, 3)]
        am = am_area[:, :].rearrange("p (h t) -> p h t", h=LH)
        kh = sb("kh", [P, HKV, T], F32R)
        klo = sb("klo", [P, HKV, T], F32R)
        qs = sb("qs", [P, HQ, T], F32R)
        v1 = sb("v1", [P, NT * HKV // 2, 3, HD])
        negm = sb("negm", [P, 2, NT, G])
        half = sb("half", [P, NT])
        negmT = sb("negmT", [G, 2, T], F32R)
        NPT = P * (NT * (NT + 1) // 2)
        pt = sb("pt", [P, 2, NPT])
        rden = sb("rden", [P, T])
        oT = sb("oT", [P, 2, T])
        xf = sb("xf", [P, NT, D])
        xfT = atT
        lg = sb("lg", [P, 2, NT, E])
        mx = sb("mx", [P, 2, NT])
        mi = sb("mi", [P, NT])
        eq = sb("eq", [P, NT, E])
        oh = sb("oh", [P, NT, 2, E])
        ohc = sb("ohc", [P, NT, 2, E])
        carry = sb("carry", [P, 2, E])
        pos = sb("pos", [P, NT, 2, E])
        em = sb("em", [P, NT, 2, E])
        emi = sb("emi", [P, NT, 2, E])
        tk = sb("tk", [P, 10, NT, 2])
        pick = sb("pick", [P, NT, E])
        pickc = sb("pickc", [P, NT, E])
        pcarry = sb("pcarry", [P, E])
        ob = ylp
        xf_all = sb("xf_all", [P, B * NT, D])
        pick_all = sb("pick_all", [P, B * NT, E])
        rank_all = sb("rank_all", [P, B * NT])
        share_all = sb("share_all", [P, B * NT])
        total = sb("total", [P, 4, E])
        slot_f = sb("slot_f", [P, B * NT])
        slot = sb("slot", [P, B * NT], U32)
        expert_f = sb("expert_f", [P, NS])
        expert = sb("expert", [P, NS], I32)
        stage = xf_all[:, :, :].rearrange("p n d -> p (n d)")
        watt, wlin = stage[:, 0:NW], stage[:, NW:NW + 5 * D + LH]
        wup = lin_area[:, :].rearrange("p (e n) -> p e n", e=E)
        wdown = pt[:, :, :].rearrange("p a n -> p (a n)")[:, 0:E * 2 * D].rearrange("p (e c n) -> p e c n", e=E, c=2)
        cmp = oT[:, :, :].rearrange("p a t -> p (a t)")
        ob_zero = sb("ob_zero", [P, D])
        xs, ys = xt, yl
        xsT = h1
        eht = [xgt, atT[:, :]]
        yg = [xn, xres]
        ehc = dec[:, :, :].rearrange("p a (k n) -> p (a k) n", n=HID)
        ehp = qm[:, :, :, :].rearrange("p a (k g) n -> p (a k) (g n)", g=2)
        ehg = qk_l[:, :, :].rearrange("p a (k n) -> p (a k) n", n=HID)

        sorted_x = nc.dram_tensor("sorted_x", (NS * P, D), F32).ap()
        sorted_y = nc.dram_tensor("sorted_y", (NS * P, D), F32).ap()
        partial = nc.dram_tensor("partial", (B, P, NT * D), F32).ap()
        bank = [ctx.enter_context(nc.psum_tensor(f"bank{i}", [P, 512], F32)) for i in range(8)]

        s_load = sem("s_load")
        s_late = sem("s_late")
        s_x = sem("s_x")
        s_out = sem("s_out")
        s_obfree = sem("s_obfree")
        s_wsplit = sem("s_wsplit")
        s_const = sem("s_const")
        s_fill = sem("s_fill")
        s_ed = sem("s_ed")
        s_ea = sem("s_ea")
        s_var = sem("s_var")
        s_rstd = sem("s_rstd")
        s_norm = sem("s_norm")
        s_res = sem("s_res")
        s_hi = sem("s_hi")
        s_xl = sem("s_xl")
        s_rot = sem("s_rot")
        s_low = sem("s_low")
        s_zbe = sem("s_zbe")
        s_beta = sem("s_beta")
        s_elu = sem("s_elu")
        s_eluexp = sem("s_eluexp")
        s_lphi = sem("s_lphi")
        s_lin = sem("s_lin")
        s_qm = sem("s_qm")
        s_st = sem("s_st")
        s_ylp = sem("s_ylp")
        s_la = sem("s_la")
        s_sc = sem("s_sc")
        s_mx = sem("s_mx")
        s_ex = sem("s_ex")
        s_p = sem("s_p")
        s_pv = sem("s_pv")
        s_o = sem("s_o")
        s_rec = sem("s_rec")
        s_nrm = sem("s_nrm")
        s_wo = sem("s_wo")
        s_xf = sem("s_xf")
        s_oh = sem("s_oh")
        s_dif = sem("s_dif")
        s_dexp = sem("s_dexp")
        s_top = sem("s_top")
        s_share = sem("s_share")
        s_pick = sem("s_pick")
        s_rk = sem("s_rk")
        s_chain = sem("s_chain")
        s_half = sem("s_half")
        s_setup = sem("s_setup")
        s_pe_end = sem("s_pe_end")
        s_act_end = sem("s_act_end")
        s_dve_end = sem("s_dve_end")
        s_zero = sem("s_zero")
        s_tot = sem("s_tot")
        s_slot = sem("s_slot")
        s_expert = sem("s_expert")
        s_scat = sem("s_scat")
        s_wexp = sem("s_wexp")
        s_xs = sem("s_xs")
        s_xst = sem("s_xst")
        s_xstc = sem("s_xstc")
        s_eup = sem("s_eup")
        s_ehc = sem("s_ehc")
        s_ehp = sem("s_ehp")
        s_ehg = sem("s_ehg")
        s_eht = sem("s_eht")
        s_ehtc = sem("s_ehtc")
        s_ey = sem("s_ey")
        s_ys = sem("s_ys")
        s_yst = sem("s_yst")
        s_ysfree = sem("s_ysfree")
        s_yg = [sem("s_yg0"), sem("s_yg1")]
        s_pin = sem("s_pin")
        s_fin = sem("s_fin")
        s_done = sem("s_done")

        block = ctx.enter_context(nc.Block())
        xv = x.rearrange("b (n p) d -> b p n d", p=P)
        sxv = sorted_x.rearrange("(i k p) d -> i p k d", k=SG, p=P)
        syv = sorted_y.rearrange("(i k p) d -> i p k d", k=SG, p=P)
        ov = out.rearrange("b (n p) d -> b p n d", p=P)
        NLOAD, NLATE = 5, 3
        CHAIN = 64
        order = Order()

        WQ, WQX, WK, WKX, WV = 0, 1024, 2048, 2560, 3072
        POFF = [sum(T - P * i for i in range(j)) for j in range(NT)]
        PIECES = [[0], [1], [2, 3]]
        PROJ = ["Q0", "Q1", "K0", "Q2", "K1", "Q3", "K2", "Q4", "Q5", "Q6", "K3", "Q7"]
        score_bank, exp_bank, out_bank, wo_bank, side_bank = bank[0:2], bank[2:4], bank[4], bank[5], bank[6:8]

        def bcast(ap, n):
            return ap.unsqueeze(2).to_broadcast([ap.shape[0], ap.shape[1], n])

        def tile(ap, n):
            return ap[:, n * P:(n + 1) * P]

        def when(eng, semaphore, value):
            if value is not None:
                eng.wait_ge(semaphore, value)

        def before(step, n, per_batch):
            k = step - n
            return (0, k) if k >= 0 else (-1, k + per_batch)

        def run_bodies(eng, body):
            body(-1, -1)
            body(0, 0)
            with eng.Fori(1, B - 1) as b:
                body(b, 1)
            body(B - 1, B - 1)
            body(B, B)

        @block.sync
        def _(sp):
            sp.dma_start(xt[:, :, :], xv[0]).then_inc(s_x, 16)
            sp.dma_start(c_all[:, :], consts).then_inc(s_load, 16)
            sp.dma_start(wlin[:, :], w_lin).then_inc(s_load, 16)
            sp.dma_start(watt[:, :], w_att).then_inc(s_load, 16)
            sp.dma_start(rows_sb[:, :], rows).then_inc(s_load, 16)
            sp.dma_start(g1_sb[:, :], g1).then_inc(s_load, 16)
            sp.dma_start(wlout[:, :], w_lout).then_inc(s_late, 16)
            sp.dma_start(wout[:, :, :], w_out.rearrange("(c p) n -> p c n", p=P)).then_inc(s_late, 16)
            sp.dma_start(wrt[:, :], w_router).then_inc(s_late, 16)
            for b in (1, 2):
                sp.wait_ge(s_la, b)
                sp.dma_start(xt[:, :, :], xv[b]).then_inc(s_x, 16)
            with sp.Fori(1, B - 2) as b:
                sp.wait_ge(s_rk, b)
                sp.dma_start(partial[b - 1], ob[:, :, :].rearrange("p n d -> p (n d)")).then_inc(s_out, 16)
                sp.wait_ge(s_out, 16 * b)
                sp.nop().then_inc(s_obfree, 1)
                sp.wait_ge(s_la, b + 2)
                sp.dma_start(xt[:, :, :], xv[b + 2]).then_inc(s_x, 16)
            for b in range(B - 2, B + 1):
                sp.wait_ge(s_rk, b)
                sp.dma_start(partial[b - 1], ob[:, :, :].rearrange("p n d -> p (n d)")).then_inc(s_out, 16)
                sp.wait_ge(s_out, 16 * b)
                sp.nop().then_inc(s_obfree, 1)
                if b == B - 2:
                    sp.wait_ge(s_la, B)
                    sp.wait_ge(s_low, B * (HKV + HQ // 2))
                    sp.dma_start(wup[:, :, :], w_up).then_inc(s_wexp, 16)
            sp.wait_ge(s_pe_end, 1)
            sp.dma_start(wdown[:, :, :, :], w_down.rearrange("e (c p) n -> p e c n", p=P)).then_inc(s_wexp, 16)
            sp.nop().then_inc(s_ysfree, 1)
            sp.wait_ge(s_scat, 16 * B * NT)
            sp.dma_start(xs[:, :, :], sxv[0]).then_inc(s_xs, 16)
            sp.wait_ge(s_xst, 1)
            sp.dma_start(xs[:, :, :], sxv[1]).then_inc(s_xs, 16)
            with sp.Fori(1, NG - 1) as i:
                sp.wait_ge(s_xst, i + 1)
                sp.dma_start(xs[:, :, :], sxv[i + 1]).then_inc(s_xs, 16)
                sp.wait_ge(s_ys, i)
                sp.dma_start(syv[i - 1], ys[:, :, :]).then_inc(s_yst, 16)
                sp.wait_ge(s_yst, 16 * i)
                sp.nop().then_inc(s_ysfree, 1)
            for i in (NG - 1, NG):
                sp.wait_ge(s_ys, i)
                sp.dma_start(syv[i - 1], ys[:, :, :]).then_inc(s_yst, 16)
                if i < NG:
                    sp.wait_ge(s_yst, 16 * i)
                    sp.nop().then_inc(s_ysfree, 1)
            sp.dma_start(ob[:, :, :].rearrange("p n d -> p (n d)"), partial[0]).then_inc(s_pin, 16)
            with sp.Fori(1, B) as i:
                sp.wait_ge(s_fin, i)
                sp.dma_start(ov[i - 1], ob[:, :, :]).then_inc(s_done, 16)
                sp.wait_ge(s_done, 16 * i)
                sp.dma_start(ob[:, :, :].rearrange("p n d -> p (n d)"), partial[i]).then_inc(s_pin, 16)
            sp.wait_ge(s_fin, B)
            sp.dma_start(ov[B - 1], ob[:, :, :]).then_inc(s_done, 16)
            sp.wait_ge(s_done, 16 * B)

        ROOTS = {"LN": (2, 3), "LM": (4, 5), "H1": (6, 7), "LY": (8, 9)}

        @block.gpsimd
        def _(pool):
            nc.gpsimd.memset(half[:, :], -0.5).then_inc(s_half, 1)
            pool.wait_ge(s_half, 1)
            nc.gpsimd.memset(ob_zero[:, :], 0.0).then_inc(s_half, 1)
            pool.wait_ge(s_half, 2)
            for i in range(NS // SG):
                pool.dma_start(sxv[i].rearrange("p k d -> p k d"),
                               ob_zero[:, :].unsqueeze(1).to_broadcast([P, SG, D])).then_inc(s_zero, 16)

            def body(b, which):
                def at(name, kind, rel, i):
                    return order.value(b, which, name, kind, rel, i)

                own = (s_rstd, at("rstd", "LY", 0, 0))
                for kind, rel, i in order.steps[which]:
                    if kind in ("Q", "K") and i[1] == 1:
                        when(pool, *own)
                        own = (s_rot, at("rot", kind + "H", rel, i[0]))
                        pool.wait_ge(s_ed, at("ed", kind, rel, i))
                        r = PROJ.index(f"{kind}{i[0]}") % 2
                        nc.gpsimd.tensor_tensor(rot[:, r, :], rot[:, r, :], r_sin[:, :], ALU.add).then_inc(s_rot, 1)
                    if kind in ROOTS:
                        when(pool, *own)
                        own = (s_rstd, at("rstd", kind, rel, i))
                        pool.wait_ge(s_var, at("var", kind, rel, i))
                        a, o = ROOTS[kind]
                        nc.gpsimd.tensor_tensor(st[:, o, :], st[:, a, :], half[:, :], ALU.pow).then_inc(s_rstd, 1)

            run_bodies(pool, body)
            pool.wait_ge(s_zero, 16 * (NS // SG))
            pool.wait_ge(s_slot, 1)
            pool.wait_ge(s_act_end, 1)
            for t in range(B * NT):
                pool.indirect_dma_start(sorted_x[:, :], bass.IndirectOffsetOnAxis(ap=slot[:, t:t + 1], axis=0),
                                        xf_all[:, t, :], None).then_inc(s_scat, 16)
            pool.wait_ge(s_yst, 16 * (NS // SG))
            for i in range(B):
                if i >= 2:
                    pool.wait_ge(s_fin, i - 1)
                for n in range(NT):
                    t = i * NT + n
                    pool.indirect_dma_start(yg[i % 2][:, n, :], None, sorted_y[:, :],
                                            bass.IndirectOffsetOnAxis(ap=slot[:, t:t + 1], axis=0))\
                        .then_inc(s_yg[i % 2], 16)

        @block.tensor
        def _(pe):
            pe.wait_ge(s_load, 16 * NLOAD)

            def split_product(out_, lh, ll, rh, rl):
                nc.tensor.matmul(out_, lh, rh, start=True, stop=False)
                nc.tensor.matmul(out_, lh, rl, start=False, stop=False)
                return nc.tensor.matmul(out_, ll, rh, start=False, stop=True)

            def body(b, which):
                ring = order.ring(which)

                def at(name, kind, rel, i):
                    return order.value(b, which, name, kind, rel, i)

                for kind, rel, i in order.steps[which]:
                    if kind == "CP" or (kind, rel, i) in ring:
                        k, old = ring["CO", rel, i[0]] if kind == "CP" else ring[kind, rel, i]
                        bk = side_bank[k]
                        if kind == "CO" or (kind == "CP" and i[1] > 0):
                            old = None
                        by_dve = {"BL": ("XN", rel, 0), "LT": ("CO", rel, NT - 1)}.get(kind)
                        by_act = {"CU": ("CK", rel, i), "LY": ("LT", rel, 0),
                                  "LG": ("XF", rel, 0)}.get(kind)
                        read = order.last(which, "ed", [by_dve, old])
                        if read is not None:
                            pe.wait_ge(s_ed, at("ed", *read))
                        read = order.last(which, "ea", [by_act, old])
                        if read is not None:
                            pe.wait_ge(s_ea, at("ea", *read))
                    if which == -1 and kind == "BL":
                        pe.wait_ge(s_const, 1)
                    if which == -1 and kind == "LY":
                        pe.wait_ge(s_late, 16 * NLATE)
                    if kind == "M":
                        n, qt = i
                        r, k = before(n * NT + qt, 2, HQ * NT)
                        when(pe, s_mx, at("mx", "M", rel + r, (k // NT, k % NT)))
                        if qt == 0:
                            parts = [("QL", rel, n // 2), ("KL", rel, n // G)]
                            pe.wait_ge(s_low, at("low", *order.last(which, "low", parts)))
                        w = (qt + 1) * P
                        bk = score_bank[qt % 2]
                        nc.tensor.matmul(bk[:, 0:w], tile(qs[:, n, :], qt), kh[:, n // G, 0:w], start=True, stop=False)
                        nc.tensor.matmul(bk[:, w - P:w], ident_b, mask_qk_b, start=False, stop=True).then_inc(s_sc, 1)
                    elif kind == "T":
                        pe.wait_ge(s_mx, at("mx", "M", rel, (i * G + G - 1, NT - 1)))
                        for qt in range(NT):
                            last = nc.tensor.transpose(tile(bk[0:G, :], qt), negm[:, i % 2, qt, :], const("ident"))
                        last.then_inc(s_fill, 1)
                    elif kind == "S":
                        n, piece = i
                        h = n // G
                        if n % G == 0 and piece == 0:
                            pe.wait_ge(s_ea, at("ea", "T", rel, h))
                        r, k = before(n * 3 + piece, 2, HQ * 3)
                        when(pe, s_p, at("p", "S", rel + r, (k // 3, k % 3)))
                        js = PIECES[piece]
                        bk = exp_bank[(n * 3 + piece) % 2]
                        for j in js:
                            o = POFF[j] - POFF[js[0]]
                            dst = bk[:, o:o + T - P * j]
                            nc.tensor.matmul(dst, tile(kh[:, h, :], j), qs[:, n, j * P:], start=True, stop=False)
                            nc.tensor.matmul(dst, tile(klo[:, h, :], j), qs[:, n, j * P:], start=False, stop=False)
                            nc.tensor.matmul(dst, pick_row(G, n % G), negmT[:, h % 2, j * P:], start=False, stop=False)
                            last = nc.tensor.matmul(bk[:, o:o + P], ident_b, mask_kq_b, start=False, stop=True)
                        last.then_inc(s_ex, 1)
                    elif kind == "V":
                        pe.wait_ge(s_p, at("p", "S", rel, (i, 2)))
                        if i == 0:
                            pe.wait_ge(s_ea, at("ea", "VP", rel, 1))
                        r, k = before(i, 1, HQ)
                        when(pe, s_o, at("o", "V", rel + r, k))
                        h = i // G
                        for j in range(NT):
                            block = v1[:, 2 * j + h // 2, h % 2:h % 2 + 2, :].rearrange("p a d -> p (a d)")
                            last = nc.tensor.matmul(out_bank[:, j * P:], block, pt[:, i % 2, POFF[j]:POFF[j] + T - P * j],
                                                    start=(j == 0), stop=(j == NT - 1), skip_group_check=True)
                        last.then_inc(s_pv, 1)
                    elif kind == "WO":
                        pe.wait_ge(s_nrm, at("nrm", "RM", rel, i))
                        if i == 0:
                            when(pe, s_xf, at("xf", "H1R", rel - 1, 0))
                        for qt in range(NT):
                            last = nc.tensor.matmul(tile(wo_bank, qt), tile(oT[:, i % 2, :], qt), wout[:, i, :],
                                                    start=(i == 0 and qt == 0), stop=True, skip_group_check=True)
                        last.then_inc(s_wo, 1)
                    elif kind in ("XN", "XG"):
                        pe.wait_ge(s_norm, at("norm", {"XN": "LNR", "XG": "LMR"}[kind], rel, 0))
                        src = {"XN": xn, "XG": xg}[kind]
                        for n in range(NT):
                            last = nc.tensor.transpose(tile(bk, n), src[:, n, :], const("ident"))
                        last.then_inc(s_fill, 1)
                    elif kind == "BL":
                        for n in range(NT):
                            last = split_product(bk[:, n * LH:(n + 1) * LH], tile(xn_h, n), tile(xn_l, n),
                                                 wlin_h[:, 5 * D:], wlin_l[:, 5 * D:])
                        last.then_inc(s_fill, 1)
                    elif kind == "LP":
                        w = slice(i * D, (i + 1) * D)
                        split_product(bk[:, :], wlin_h[:, w], wlin_l[:, w], xn_h[:, :], xn_l[:, :]).then_inc(s_fill, 1)
                    elif kind == "LV":
                        for n in range(NT):
                            last = split_product(tile(bk, n), tile(xn_h, n), tile(xn_l, n),
                                                 wlin_h[:, 4 * D:5 * D], wlin_l[:, 4 * D:5 * D])
                        last.then_inc(s_fill, 1)
                    elif kind == "VP":
                        for k in range(2):
                            n = 2 * i + k
                            last = split_product(bk[:, k * 256:(k + 1) * 256], tile(xg_h, n), tile(xg_l, n),
                                                 watt_h[:, WV:WV + 256], watt_l[:, WV:WV + 256])
                        last.then_inc(s_fill, 1)
                    elif kind in ("Q", "K"):
                        pe.wait_ge(s_xl, at("xl", "XL", rel, 0))
                        k, x_ = i
                        o = {"Q": (WQ, WQX), "K": (WK, WKX)}[kind][x_] + k * P
                        split_product(bk[:, :], watt_h[:, o:o + P], watt_l[:, o:o + P], xg_h[:, :], xg_l[:, :])\
                            .then_inc(s_fill, 1)
                    elif kind == "LB":
                        pe.wait_ge(s_beta, at("beta", "BE", rel, 0))
                        for n in range(NT):
                            last = nc.tensor.matmul(tile(bk, n), bet[i][:, n, :, :].rearrange("p h d -> p (h d)"),
                                                    const("ident"), start=True, stop=True)
                        last.then_inc(s_fill, 1)
                    elif kind == "CK":
                        pe.wait_ge(s_lin, at("lin", "LQ", rel, 0))
                        nc.tensor.transpose(bk[:, 0:P], tile(kl, i), const("ident")).then_inc(s_fill, 1)
                    elif kind == "CS":
                        c, q = i
                        pe.wait_ge(s_qm, at("qm", "CQ", rel, c))
                        r = slice(32 * q, 32 * q + 32)
                        nc.tensor.matmul(bk[:, :], kl[r, c * P:(c + 1) * P],
                                         qm[r, c % 2, :, :].rearrange("p g t -> p (g t)"),
                                         start=True, stop=True).then_inc(s_fill, 1)
                    elif kind in ("CP", "CO"):
                        c, q = i if kind == "CP" else (i, 3)
                        if q == 0:
                            if c >= 1:
                                pe.wait_ge(s_st, at("st", "CU", rel, c - 1))
                            nc.tensor.matmul(bk[:, 0:LH * LV], tile(ql, c), state[:, :], start=True, stop=False,
                                             skip_group_check=True)
                            pe.wait_ge(s_ea, at("ea", "LV", rel, 0))
                        pe.wait_ge(s_ed, at("ed", "CS", rel, (c, q)))
                        for hd in range(4 * q, 4 * q + 4):
                            last = nc.tensor.matmul(bk[:, hd * LV:(hd + 1) * LV], am[:, hd, :],
                                                    v9[:, c, hd, :], start=False, stop=True, skip_group_check=True)
                        if kind == "CO":
                            last.then_inc(s_fill, 1)
                    elif kind == "CU":
                        nc.tensor.matmul(bk[:, 0:LH * LV], kt[:, :], v9[:, i, :, :].rearrange("p h e -> p (h e)"),
                                         start=True, stop=True).then_inc(s_fill, 1)
                    elif kind == "LT":
                        for n in range(NT):
                            last = nc.tensor.transpose(tile(bk, n), at_l[:, n, :], const("ident"))
                        last.then_inc(s_fill, 1)
                    elif kind == "LY":
                        for n in range(NT):
                            last = nc.tensor.matmul(tile(bk, n), tile(atT, n), wlout[:, :], start=True, stop=True)
                        last.then_inc(s_fill, 1)
                    elif kind == "XF":
                        pe.wait_ge(s_xf, at("xf", "H1R", rel, 0))
                        for n in range(NT):
                            last = nc.tensor.transpose(tile(bk, n), xf[:, n, :], const("ident"))
                        last.then_inc(s_fill, 1)
                    elif kind == "LG":
                        for n in range(NT):
                            last = nc.tensor.matmul(bk[:, n * E:(n + 1) * E], tile(xfT, n), wrt[:, :],
                                                    start=True, stop=True)
                        last.then_inc(s_fill, 1)
                    elif kind == "PC":
                        pe.wait_ge(s_oh, at("oh", "G2", rel, 0))
                        for n in range(NT):
                            dst = bk[:, n * 2 * E:(n + 1) * 2 * E]
                            nc.tensor.matmul(dst, const("upto"), oh[:, n, :, :].rearrange("p k e -> p (k e)"),
                                             start=True, stop=False)
                            last = nc.tensor.matmul(dst, const("ones"), ohc[:, n, :, :].rearrange("p k e -> p (k e)"),
                                                    start=False, stop=True)
                        last.then_inc(s_fill, 1)
                    elif kind == "RK":
                        pe.wait_ge(s_pick, at("pick", "P2", rel, 0))
                        for n in range(NT):
                            dst = bk[:, n * E:(n + 1) * E]
                            nc.tensor.matmul(dst, const("upto"), pick[:, n, :], start=True, stop=False)
                            last = nc.tensor.matmul(dst, const("ones"), pickc[:, n, :], start=False, stop=True)
                        last.then_inc(s_fill, 1)

            run_bodies(pe, body)
            pe.nop().then_inc(s_pe_end, 1)
            pe.wait_ge(s_act_end, 1)
            pe.wait_ge(s_dve_end, 1)
            nc.tensor.matmul(bank[0][:, 0:E], const("ones"), pcarry[:, :], start=True, stop=True).then_inc(s_tot, 1)
            pe.wait_ge(s_wexp, 32)
            pe.wait_ge(s_expert, 1)

            def turn_tokens(i):
                pe.wait_ge(s_xs, 16 * i + 16)
                for k in range(SG):
                    last = nc.tensor.transpose(tile(bank[0], k), xs[:, k, :], const("ident"))
                last.then_inc(s_xst, 1)

            def factors(i):
                pe.wait_ge(s_xstc, i + 1)
                for k in range(SG):
                    e = pe.value_load(expert[0:1, bass.ds(i * SG + k, 1)], min_val=0, max_val=E - 1)
                    nc.tensor.matmul(bank[1 + k][:, :], xsT[:, k, :],
                                     wup[:, bass.ds(e, 1), :].rearrange("p e n -> p (e n)"),
                                     start=True, stop=True).then_inc(s_eup, 1)

            def turn_hidden(i):
                for k in range(SG):
                    pe.wait_ge(s_ehg, i * SG + k + 1)
                    for c in range(2):
                        last = nc.tensor.transpose(bank[5 + k // 2][:, (k % 2) * HID + c * P:(k % 2) * HID + (c + 1) * P],
                                                   ehg[:, k, c * P:(c + 1) * P], const("ident"))
                    if k % 2 == 1:
                        last.then_inc(s_eht, 1)

            def outputs(i):
                for k in range(SG):
                    e = pe.value_load(expert[0:1, bass.ds(i * SG + k, 1)], min_val=0, max_val=E - 1)
                    pe.wait_ge(s_ehtc, i * 2 + k // 2 + 1)
                    for c in range(2):
                        o = (k % 2) * HID + c * P
                        last = nc.tensor.matmul(tile(bank[7], k), eht[k // 2][:, o:o + P],
                                                wdown[:, bass.ds(e, 1), c, :].rearrange("p e n -> p (e n)"),
                                                start=(c == 0), stop=(c == 1))
                last.then_inc(s_ey, 1)

            turn_tokens(0)
            factors(0)
            with pe.Fori(1, NG) as i:
                turn_tokens(i)
                turn_hidden(i - 1)
                factors(i)
                outputs(i - 1)
            turn_hidden(NG - 1)
            pe.wait_ge(s_ys, NG - 1)
            outputs(NG - 1)

        @block.scalar
        def _(act):
            act.wait_ge(s_load, 16 * NLOAD)
            nc.scalar.activation(watt_h[:, :], watt[:, :], ACT.Copy)
            nc.scalar.activation(wlin_h[:, :], wlin[:, :], ACT.Copy).then_inc(s_wsplit, 1)

            def body(b, which):
                ring = order.ring(which)

                def at(name, kind, rel, i):
                    return order.value(b, which, name, kind, rel, i)

                def empty(dst, src, step):
                    act.wait_ge(s_fill, at("fill", *step))
                    nc.scalar.activation(dst, src, ACT.Copy).then_inc(s_ea, 1)

                for step in order.steps[which]:
                    kind, rel, i = step
                    bk = side_bank[ring[step][0]] if step in ring else None
                    if kind == "V":
                        if i % 2 == 0:
                            r, k = before(i // 2, 2, HQ // 2)
                            when(act, s_wo, at("wo", "WO", rel + r, k))
                            r, k = before(i // 2, 1, HQ // 2)
                            when(act, s_nrm, at("nrm", "RM", rel + r, k))
                        act.wait_ge(s_pv, at("pv", *step))
                        num, den = (slice(0, HD), slice(HD, P)) if (i // G) % 2 == 0 else (slice(HD, P), slice(0, HD))
                        mine = slice((i % 2) * HD, (i % 2 + 1) * HD)
                        nc.scalar.activation(rden[mine, :], out_bank[den, :], ACT.Copy)
                        nc.scalar.activation(oT[mine, (i // 2) % 2, :], out_bank[num, :], ACT.Copy).then_inc(s_o, 1)
                    elif kind == "S":
                        n, piece = i
                        if piece == 0:
                            r, k = before(n, 2, HQ)
                            when(act, s_pv, at("pv", "V", rel + r, k))
                        act.wait_ge(s_ex, at("ex", *step))
                        js = PIECES[piece]
                        w = sum(T - P * j for j in js)
                        nc.scalar.activation(pt[:, n % 2, POFF[js[0]]:POFF[js[0]] + w],
                                             exp_bank[(n * 3 + piece) % 2][:, 0:w], ACT.Exp,
                                             scale=HD ** -0.5).then_inc(s_p, 1)
                    elif kind == "T":
                        empty(negmT[:, i % 2, :], bk[0:G, :], step)
                    elif kind == "VP":
                        empty(v1[:, 4 * i:4 * i + 4, 0:3:2, :], bk[:, :].rearrange("p (m h d) -> p m h d", m=4, h=2), step)
                    elif kind == "LV":
                        empty(v9[:, :, :, 0:LD], bk[:, :].rearrange("p (n h d) -> p n h d", n=NT, h=LH), step)
                    elif kind == "CK":
                        empty(kt[:, :], bk[:, 0:P], step)
                    elif kind == "LT":
                        empty(atT[:, :], bk[:, :], step)
                    elif kind == "XF":
                        act.wait_ge(s_fill, at("fill", *step))
                        nc.scalar.activation(xfT[:, :], bk[:, :], ACT.Copy)
                        nc.scalar.activation(xf_all[:, bass.ds(b * NT - NT, NT), :], xf[:, :, :], ACT.Copy)\
                            .then_inc(s_ea, 1)
                    elif kind == "XN":
                        act.wait_ge(s_fill, at("fill", *step))
                        nc.scalar.activation(xn_h[:, :], bk[:, :], ACT.Copy).then_inc(s_hi, 1)
                    elif kind == "XH":
                        act.wait_ge(s_ea, at("ea", "XG", rel, 0))
                        nc.scalar.activation(xg_h[:, :], xgt[:, :], ACT.Copy).then_inc(s_hi, 1)
                    elif kind == "KH":
                        act.wait_ge(s_rot, at("rot", *step))
                        nc.scalar.activation(kh[:, i, :], rot[:, PROJ.index(f"K{i}") % 2, :], ACT.Copy).then_inc(s_hi, 1)
                    elif kind == "QH":
                        act.wait_ge(s_rot, at("rot", *step))
                        src = rot[:, PROJ.index(f"Q{i}") % 2, :]
                        nc.scalar.activation(qs[0:HD, 2 * i, :], src[0:HD, :], ACT.Copy)
                        nc.scalar.activation(qs[HD:P, 2 * i + 1, :], src[HD:P, :], ACT.Copy).then_inc(s_hi, 1)
                    elif kind == "XG":
                        act.wait_ge(s_fill, at("fill", *step))
                        nc.scalar.activation(xgt[:, :], bk[:, :], ACT.Copy, scale=g1_sb[:, :]).then_inc(s_ea, 1)
                    elif kind == "XR":
                        when(act, s_var, at("var", "H1", -1, 0))
                        act.wait_ge(s_norm, at("norm", "LNR", rel, 0))
                        nc.scalar.activation(xres[:, :, :], xn[:, :, :], ACT.Copy).then_inc(s_res, 1)
                    elif kind == "YC":
                        if which != 0:
                            act.wait_ge(s_obfree, b)
                        act.wait_ge(s_la, at("la", "LYR", rel, 0))
                        nc.scalar.activation(ylp[:, :, :], yl[:, :, :], ACT.Copy).then_inc(s_ylp, 1)
                    elif kind == "CQ":
                        r, k = before(i, 2, NT)
                        when(act, s_fill, at("fill", "CS", rel + r, (k, 3)))
                        act.wait_ge(s_lin, at("lin", "LQ", rel, 0))
                        for g in range(G):
                            last = nc.scalar.activation(qm[:, i % 2, g, :], ql[:, i * P:(i + 1) * P], ACT.Copy,
                                                        scale=const("quad")[:, g:g + 1])
                        last.then_inc(s_qm, 1)
                    elif kind == "BX":
                        act.wait_ge(s_ed, at("ed", "BL", rel, 0))
                        nc.scalar.activation(zb[:, 1], zb[:, 0], ACT.Exp, scale=-1.0).then_inc(s_zbe, 1)
                    elif kind == "EE":
                        act.wait_ge(s_elu, at("elu", *step))
                        nc.scalar.activation(r_m[:, i, :], r_m[:, i, :], ACT.Exp).then_inc(s_eluexp, 1)
                    elif kind == "DX":
                        act.wait_ge(s_dif, at("dif", *step))
                        nc.scalar.activation(tk[:, 0, :, 1], tk[:, 0, :, 0], ACT.Exp).then_inc(s_dexp, 1)

            run_bodies(act, body)
            act.nop().then_inc(s_act_end, 1)

            def tokens(i):
                act.wait_ge(s_xst, i + 1)
                nc.scalar.activation(xsT[:, :, :], bank[0][:, :].rearrange("p (k t) -> p k t", k=SG), ACT.Copy)\
                    .then_inc(s_xstc, 1)

            def gelus(i):
                for k in range(SG):
                    act.wait_ge(s_eup, i * SG + k + 1)
                    nc.scalar.activation(ehc[:, k, :], bank[1 + k][:, 0:HID], ACT.Copy).then_inc(s_ehc, 1)
                for k in range(SG):
                    act.wait_ge(s_ehp, i * SG + k + 1)
                    nc.scalar.activation(ehg[:, k, :], ehp[:, k, :], ACT.Gelu).then_inc(s_ehg, 1)

            def keep_outputs(i):
                act.wait_ge(s_ey, i + 1)
                act.wait_ge(s_ysfree, i + 1)
                nc.scalar.activation(ys[:, :, :], bank[7][:, :].rearrange("p (k d) -> p k d", k=SG), ACT.Copy)\
                    .then_inc(s_ys, 1)

            tokens(0)
            gelus(0)
            with act.Fori(1, NG) as i:
                tokens(i)
                gelus(i)
                keep_outputs(i - 1)
            keep_outputs(NG - 1)

        @block.vector
        def _(dve):
            v = nc.vector
            links = [0]

            def setup(ins):
                links[0] += 1
                ins.then_inc(s_setup, 1)
                dve.wait_ge(s_setup, links[0])

            v.memset(v9[:, :, :, LD:LV], 1.0)
            v.memset(v1[:, :, 1, :], 1.0)
            v.memset(carry[:, :, :], 0.0)
            setup(v.memset(pcarry[:, :], 0.0))
            chain_before = {-1: 0}

            def body(b, which):
                ring = order.ring(which)
                count = [0]
                base = b * CHAIN + chain_before[which] - CHAIN if which == 1 else chain_before[which]

                def at(name, kind, rel, i):
                    return order.value(b, which, name, kind, rel, i)

                def link(ins):
                    count[0] += 1
                    ins.then_inc(s_chain, 1)
                    dve.wait_ge(s_chain, base + count[0])

                def filled(step):
                    dve.wait_ge(s_fill, at("fill", *step))

                def emptied(ins, step):
                    ins.then_inc(s_ed, 1)
                    dve.wait_ge(s_ed, at("ed", *step))

                def mean_square(src, step, eps):
                    link(v.tensor_tensor(sq[:, :, :], src, src, ALU.mult))
                    link(v.tensor_reduce(st[:, 0, :], sq[:, :, :], AX.X, ALU.add))
                    v.tensor_scalar(st[:, ROOTS[step[0]][0], :], st[:, 0, :], 1.0 / D, eps, ALU.mult, ALU.add)\
                        .then_inc(s_var, 1)
                    return s_var, at("var", *step)

                def root(of, rel, i):
                    dve.wait_ge(s_rstd, at("rstd", of, rel, i))
                    return bcast(st[:, ROOTS[of][1], :], D)

                own = (s_la, at("la", "LYR", 0, 0))
                if own[1] is None:
                    own = (s_nrm, at("nrm", "RM", -1, HQ // 2 - 2))
                if own[1] is None:
                    own = (s_setup, 1)

                for step in order.steps[which]:
                    kind, rel, i = step
                    bk = side_bank[ring[step][0]] if step in ring else None
                    if kind == "M":
                        n, qt = i
                        h = n // G
                        if n % G == 0 and qt == 0:
                            r, k = before(h, 2, HKV)
                            when(dve, s_fill, at("fill", "T", rel + r, k))
                        dve.wait_ge(s_sc, at("sc", *step))
                        v.tensor_reduce(negm[:, h % 2, qt, n % G:n % G + 1], score_bank[qt % 2][:, 0:(qt + 1) * P],
                                        AX.X, ALU.max, negate=True).then_inc(s_mx, 1)
                        continue
                    if kind in ("RC", "RM", "LNR", "LMR", "H1R", "LYR", "G2", "P2", "R2", "H1", "LN", "LM", "XN", "XL", "BL", "BE", "LP", "LE", "LB", "LQ",
                                "CS", "CO", "CU", "LY", "LG", "PC", "RK", "Q", "QL", "K", "KL"):
                        dve.wait_ge(*own)
                    if kind == "RC":
                        k, part = i
                        dve.wait_ge(s_o, at("o", "V", rel, 2 * k + 1))
                        v.reciprocal(rden[:, part * P:(part + 1) * P], rden[:, part * P:(part + 1) * P]).then_inc(s_rec, 1)
                        own = (s_rec, at("rec", *step))
                    elif kind == "RM":
                        v.tensor_tensor(oT[:, i % 2, :], oT[:, i % 2, :], rden[:, :], ALU.mult).then_inc(s_nrm, 1)
                        own = (s_nrm, at("nrm", *step))
                    elif kind == "LN":
                        dve.wait_ge(s_x, 16 * b + 16 * (rel + 1))
                        when(dve, s_res, at("res", "XR", rel - 1, 0))
                        link(v.tensor_reduce(st[:, 0, :], xt[:, :, :], AX.X, ALU.add))
                        link(v.tensor_scalar(st[:, 1, :], st[:, 0, :], 1.0 / D, None, ALU.mult))
                        link(v.tensor_tensor(xn[:, :, :], xt[:, :, :], bcast(st[:, 1, :], D), ALU.subtract))
                        own = mean_square(xn[:, :, :], step, LN_EPS)
                    elif kind == "LNR":
                        v.tensor_tensor(xn[:, :, :], xn[:, :, :], root("LN", rel, i), ALU.mult).then_inc(s_norm, 1)
                        own = (s_norm, at("norm", *step))
                    elif kind == "LM":
                        own = mean_square(xn[:, :, :], step, EPS)
                    elif kind == "LMR":
                        v.tensor_tensor(xg[:, :, :], xn[:, :, :], root("LM", rel, i), ALU.mult).then_inc(s_norm, 1)
                        own = (s_norm, at("norm", *step))
                    elif kind == "XN":
                        if which == -1:
                            dve.wait_ge(s_load, 16 * NLOAD)
                            v.tensor_copy(ident_r[:, :], const("ident")[:, 0:G])
                            v.tensor_copy(cb[:, :], c_all[:, 0:3 * P])
                            dve.wait_ge(s_wsplit, 1)
                            v.tensor_tensor(watt_l[:, :], watt[:, :], watt_h[:, :], ALU.subtract)
                            v.tensor_tensor(wlin_l[:, :], wlin[:, :], wlin_h[:, :], ALU.subtract).then_inc(s_const, 1)
                        filled(step)
                        dve.wait_ge(s_hi, at("hi", *step))
                        v.tensor_tensor(xn_l[:, :], bk[:, :], xn_h[:, :], ALU.subtract).then_inc(s_ed, 1)
                        own = (s_ed, at("ed", *step))
                    elif kind == "XL":
                        dve.wait_ge(s_hi, at("hi", "XH", rel, 0))
                        v.tensor_tensor(xg_l[:, :], xgt[:, :], xg_h[:, :], ALU.subtract).then_inc(s_xl, 1)
                        own = (s_xl, at("xl", *step))
                    elif kind == "BL":
                        filled(step)
                        v.tensor_tensor(zb[:, 0], bk[:, 0:NT * LH].rearrange("p (n h) -> p n h", n=NT),
                                        row("bb").unsqueeze(1).to_broadcast([P, NT, LH]), ALU.add).then_inc(s_ed, 1)
                        own = (s_ed, at("ed", *step))
                    elif kind == "BE":
                        dve.wait_ge(s_zbe, at("zbe", "BX", rel, 0))
                        link(v.tensor_scalar(zb[:, 2], zb[:, 1], 1.0, None, ALU.add))
                        link(v.reciprocal(zb[:, 3], zb[:, 2]))
                        link(v.tensor_scalar(zb[:, 0], zb[:, 3], 0.8, 0.999, ALU.max, ALU.min))
                        link(v.reciprocal(zb[:, 1], zb[:, 0]))
                        for k in range(2):
                            last = v.tensor_copy(bet[k], zb[:, k].unsqueeze(3).to_broadcast([P, NT, LH, LD]))
                        last.then_inc(s_beta, 1)
                        own = (s_beta, at("beta", *step))
                    elif kind == "LP":
                        filled(step)
                        k = i // 2
                        if i % 2 == 0:
                            v.tensor_tensor(r_a[:, k, :], bk[:, :], const("cos_l"), ALU.mult).then_inc(s_ed, 1)
                            own = (s_ed, at("ed", *step))
                        else:
                            dve.wait_ge(s_rot, at("rot", "QH", rel, 0))
                            emptied(v.tensor_tensor(r_sin[:, :], bk[:, :], const("sin_l"), ALU.mult), step)
                            link(v.tensor_tensor(r_a[:, k, :], r_a[:, k, :], r_sin[:, :], ALU.add))
                            v.tensor_scalar(r_m[:, k, :], r_a[:, k, :], 0.0, None, ALU.min).then_inc(s_elu, 1)
                            own = (s_elu, at("elu", "EE", rel, k))
                    elif kind == "LE":
                        dve.wait_ge(s_eluexp, at("eluexp", "EE", rel, i))
                        v.scalar_tensor_tensor(qk_l[:, i, :], r_a[:, i, :], 0.0, r_m[:, i, :], ALU.max, ALU.add)\
                            .then_inc(s_lphi, 1)
                        own = (s_lphi, at("lphi", *step))
                    elif kind == "LB":
                        filled(step)
                        for c in range(NT):
                            t = slice(c * P, (c + 1) * P)
                            last = v.tensor_tensor_scan(dec[:, i, t], bk[:, t], const("ones"), 1.0, ALU.mult, ALU.mult)
                        last.then_inc(s_ed, 1)
                        own = (s_ed, at("ed", *step))
                    elif kind == "LQ":
                        v.tensor_tensor(ql[:, :], ql[:, :], dec[:, 0, :], ALU.mult)
                        v.tensor_tensor(kl[:, :], kl[:, :], dec[:, 1, :], ALU.mult)
                        v.memset(state[:, :], 0.0).then_inc(s_lin, 1)
                        own = (s_lin, at("lin", *step))
                    elif kind == "CS":
                        filled(step)
                        c, q = i
                        v.tensor_tensor(am[:, 4 * q:4 * q + 4, :], bk[:, :].rearrange("p (g t) -> p g t", g=4),
                                        const("upto").unsqueeze(1).to_broadcast([P, G, P]), ALU.mult).then_inc(s_ed, 1)
                        own = (s_ed, at("ed", *step))
                    elif kind == "CO":
                        filled(step)
                        acc = bk[:, 0:LH * LV].rearrange("p (h e) -> p h e", h=LH)
                        link(v.tensor_scalar(rden_l[:, :], acc[:, :, LD:LV].rearrange("p h e -> p (h e)"), EPS, None,
                                             ALU.add))
                        link(v.reciprocal(rden_l[:, :], rden_l[:, :]))
                        v.tensor_tensor(at_l[:, i, :].rearrange("p (h d) -> p h d", h=LH), acc[:, :, 0:LD],
                                        bcast(rden_l[:, :], LD), ALU.mult).then_inc(s_ed, 1)
                        own = (s_ed, at("ed", *step))
                    elif kind == "CU":
                        filled(step)
                        emptied(v.tensor_tensor(stt[:, :], bk[:, 0:LH * LV], const("diag"), ALU.mult), step)
                        link(v.tensor_tensor(stt[:, :], stt[:, :], state[:, :], ALU.add))
                        v.tensor_scalar(state[:, :], stt[:, :], dec[:, 0, (i + 1) * P - 1:(i + 1) * P], None, ALU.mult)\
                            .then_inc(s_st, 1)
                        own = (s_st, at("st", *step))
                    elif kind == "LY":
                        filled(step)
                        when(dve, s_ylp, at("ylp", "YC", rel - 1, 0))
                        emptied(v.tensor_tensor(yl[:, :, :], xn[:, :, :], bk[:, :].rearrange("p (n d) -> p n d", n=NT),
                                                ALU.add), step)
                        link(v.tensor_tensor(yl[:, :, :], yl[:, :, :],
                                             row("bo").unsqueeze(1).to_broadcast([P, NT, D]), ALU.add))
                        own = mean_square(yl[:, :, :], step, EPS)
                    elif kind == "LYR":
                        link(v.tensor_tensor(yl[:, :, :], yl[:, :, :], root("LY", rel, i), ALU.mult))
                        link(v.tensor_tensor(yl[:, :, :], yl[:, :, :],
                                             row("scale").unsqueeze(1).to_broadcast([P, NT, D]), ALU.mult))
                        v.tensor_tensor(yl[:, :, :], yl[:, :, :], xt[:, :, :], ALU.add).then_inc(s_la, 1)
                        own = (s_la, at("la", *step))
                    elif kind == "H1":
                        dve.wait_ge(s_wo, at("wo", "WO", rel, HQ // 2 - 1))
                        link(v.tensor_tensor(h1[:, :, :], xres[:, :, :],
                                             wo_bank[:, :].rearrange("p (n d) -> p n d", n=NT), ALU.add))
                        own = mean_square(h1[:, :, :], step, EPS)
                    elif kind == "H1R":
                        link(v.tensor_tensor(xf[:, :, :], h1[:, :, :], root("H1", rel, i), ALU.mult))
                        v.tensor_tensor(xf[:, :, :], xf[:, :, :], row("g2").unsqueeze(1).to_broadcast([P, NT, D]),
                                        ALU.mult).then_inc(s_xf, 1)
                        own = (s_xf, at("xf", *step))
                    elif kind in ("Q", "K"):
                        filled(step)
                        k, x_ = i
                        r = PROJ.index(f"{kind}{k}") % 2
                        if x_ == 0:
                            v.tensor_tensor(rot[:, r, :], bk[:, :], const("cos_s"), ALU.mult).then_inc(s_ed, 1)
                            own = (s_ed, at("ed", *step))
                        else:
                            turn, name = before(PROJ.index(f"{kind}{k}"), 1, len(PROJ))
                            name = PROJ[name]
                            when(dve, s_rot, at("rot", name[0] + "H", rel + turn, int(name[1])))
                            v.tensor_tensor(r_sin[:, :], bk[:, :], const("sin_s"), ALU.mult).then_inc(s_ed, 1)
                            own = (s_ed, at("ed", *step))
                    elif kind == "KL":
                        dve.wait_ge(s_hi, at("hi", "KH", rel, i))
                        v.tensor_tensor(klo[:, i, :], rot[:, PROJ.index(f"K{i}") % 2, :], kh[:, i, :], ALU.subtract)\
                            .then_inc(s_low, 1)
                        own = (s_low, at("low", *step))
                    elif kind == "QL":
                        dve.wait_ge(s_hi, at("hi", "QH", rel, i))
                        src = rot[:, PROJ.index(f"Q{i}") % 2, :]
                        v.tensor_tensor(qs[HD:P, 2 * i, :], src[0:HD, :], qs[0:HD, 2 * i, :], ALU.subtract)
                        v.tensor_tensor(qs[0:HD, 2 * i + 1, :], src[HD:P, :], qs[HD:P, 2 * i + 1, :], ALU.subtract)\
                            .then_inc(s_low, 1)
                        own = (s_low, at("low", *step))
                    elif kind == "LG":
                        filled(step)
                        emptied(v.tensor_tensor(lg[:, 0], bk[:, 0:NT * E].rearrange("p (n e) -> p n e", n=NT),
                                                row("router_b").unsqueeze(1).to_broadcast([P, NT, E]), ALU.add), step)
                    if kind in ("LG", "G2"):
                        less = const("less").unsqueeze(1).to_broadcast([P, NT, E])
                        for k in (0,) if kind == "LG" else (1,):
                            link(v.tensor_reduce(mx[:, k, :], lg[:, k], AX.X, ALU.max))
                            link(v.tensor_tensor(eq[:, :, :], lg[:, k], bcast(mx[:, k, :], E), ALU.is_equal))
                            link(v.tensor_tensor(eq[:, :, :], eq[:, :, :], less, ALU.mult))
                            link(v.tensor_reduce(mi[:, :], eq[:, :, :], AX.X, ALU.min))
                            link(v.tensor_tensor(oh[:, :, k, :], less, bcast(mi[:, :], E), ALU.is_equal))
                            if k == 0:
                                v.scalar_tensor_tensor(lg[:, 1], oh[:, :, 0, :], -3.0e38, lg[:, 0], ALU.mult,
                                                       ALU.add).then_inc(s_top, 1)
                                own = (s_top, at("top", *step))
                    if kind == "G2":
                        v.tensor_copy(ohc[:, 0], carry[:, :, :])
                        link(v.tensor_tensor(ohc[:, 1], carry[:, :, :], oh[:, 0], ALU.add))
                        for n in range(2, NT):
                            link(v.tensor_tensor(ohc[:, n], ohc[:, n - 1], oh[:, n - 1], ALU.add))
                        v.tensor_tensor(carry[:, :, :], ohc[:, NT - 1], oh[:, NT - 1], ALU.add).then_inc(s_oh, 1)
                        v.tensor_tensor(tk[:, 0, :, 0], mx[:, 1, :], mx[:, 0, :], ALU.subtract).then_inc(s_dif, 1)
                        own = (s_dif, at("dif", "DX", rel, 0))
                    if kind == "PC":
                        filled(step)
                        cnt = bk[:, 0:NT * 2 * E].rearrange("p (n k e) -> p n k e", n=NT, k=2)
                        link(v.tensor_copy(pos[:, :, 0, :], cnt[:, :, 0, :]))
                        v.tensor_tensor(pos[:, :, 1, :], cnt[:, :, 1, :], pos[:, :, 0, :], ALU.add).then_inc(s_ed, 1)
                        own = (s_ed, at("ed", *step))
                    elif kind == "P2":
                        link(v.scalar_tensor_tensor(em[:, :, :, :].rearrange("p n k e -> p (n k e)"),
                                                    pos[:, :, :, :].rearrange("p n k e -> p (n k e)"), float(CAP),
                                                    oh[:, :, :, :].rearrange("p n k e -> p (n k e)"), ALU.is_lt, ALU.mult))
                        fit = tk[:, 1]
                        link(v.tensor_reduce(fit, em[:, :, :, :], AX.X, ALU.add))
                        iota = const("iota").unsqueeze(1).to_broadcast([P, NT, E])
                        for k in range(2):
                            last = v.tensor_tensor(emi[:, :, k, :], em[:, :, k, :], iota, ALU.mult)
                        link(last)
                        link(v.tensor_reduce(tk[:, 2], emi[:, :, :, :], AX.X, ALU.add))
                        link(v.tensor_tensor(tk[:, 3, :, 0], tk[:, 2, :, 0], tk[:, 2, :, 1], ALU.max))
                        v.tensor_copy(pickc[:, 0], pcarry[:, :])
                        link(v.tensor_tensor(pick[:, :, :], iota, tk[:, 3, :, 0:1].to_broadcast([P, NT, E]), ALU.is_equal))
                        link(v.tensor_tensor(pickc[:, 1], pcarry[:, :], pick[:, 0], ALU.add))
                        for n in range(2, NT):
                            link(v.tensor_tensor(pickc[:, n], pickc[:, n - 1], pick[:, n - 1], ALU.add))
                        v.tensor_tensor(pick_all[:, bass.ds(b * NT - NT, NT), :], pick[:, :, :], pick[:, :, :], ALU.max)
                        v.tensor_tensor(pcarry[:, :], pickc[:, NT - 1], pick[:, NT - 1], ALU.add).then_inc(s_pick, 1)
                        own = (s_pick, at("pick", *step))
                    elif kind == "RK":
                        fit = tk[:, 1]
                        dve.wait_ge(s_dexp, at("dexp", "DX", rel, 0))
                        link(v.tensor_scalar(tk[:, 5, :, 0], tk[:, 0, :, 1], 1.0, None, ALU.add))
                        link(v.reciprocal(tk[:, 6, :, 0], tk[:, 5, :, 0]))
                        link(v.tensor_tensor(tk[:, 6, :, 1], tk[:, 6, :, 0], tk[:, 0, :, 1], ALU.mult))
                        link(v.tensor_tensor(tk[:, 7], tk[:, 6], fit, ALU.mult))
                        link(v.tensor_tensor(tk[:, 8], tk[:, 6], tk[:, 7], ALU.subtract))
                        v.tensor_tensor(tk[:, 9, :, 0], tk[:, 7, :, 0], tk[:, 7, :, 1], ALU.add)
                        link(v.tensor_tensor(tk[:, 9, :, 1], tk[:, 8, :, 0], tk[:, 8, :, 1], ALU.add))
                        filled(step)
                        emptied(v.tensor_tensor(eq[:, :, :], bk[:, 0:NT * E].rearrange("p (n e) -> p n e", n=NT),
                                                pick[:, :, :], ALU.mult), step)
                        v.tensor_reduce(rank_all[:, bass.ds(b * NT - NT, NT)], eq[:, :, :], AX.X, ALU.add)
                        v.tensor_tensor(share_all[:, bass.ds(b * NT - NT, NT)], tk[:, 9, :, 0], tk[:, 9, :, 0], ALU.max)\
                            .then_inc(s_share, 1)
                        own = (s_share, at("share", *step))
                    elif kind == "R2":
                        link(v.tensor_tensor(xf[:, :, :], xf[:, :, :], tk[:, 9, :, 1:2].to_broadcast([P, NT, D]), ALU.mult))
                        link(v.tensor_tensor(h1[:, :, :], xf[:, :, :], h1[:, :, :], ALU.add))
                        v.tensor_tensor(ob[:, :, :], ylp[:, :, :], h1[:, :, :], ALU.add)\
                            .then_inc(s_rk, 1)
                        own = (s_rk, at("rk", *step))
                if which == 1:
                    assert count[0] == CHAIN, count[0]
                    chain_before[B - 1] = chain_before[1] + (B - 2) * CHAIN
                else:
                    chain_before[{-1: 0, 0: 1, B - 1: B, B: None}[which]] = chain_before[which] + count[0]

            run_bodies(dve, body)
            dve.wait_ge(s_rk, B)
            v.nop().then_inc(s_dve_end, 1)
            step = setup
            dve.wait_ge(s_tot, 1)
            step(v.tensor_copy(total[:, 0], bank[0][:, 0:E]))
            c3 = cmp[:, 0:E * B * NT].rearrange("p (e k) -> p e k", e=E)
            step(v.tensor_tensor(c3, bcast(total[:, 0], B * NT),
                                 const("steps").unsqueeze(1).to_broadcast([P, E, B * NT]), ALU.is_gt))
            step(v.tensor_reduce(total[:, 1], c3, AX.X, ALU.add))
            step(v.tensor_tensor_scan(total[:, 2], const("ones")[:, 0:E], total[:, 1], 0.0, ALU.mult, ALU.add))
            step(v.tensor_tensor(total[:, 3], total[:, 2], total[:, 1], ALU.subtract))
            step(v.tensor_scalar(total[:, 3], total[:, 3], float(P), -1.0, ALU.mult, ALU.add))
            c3 = cmp[:, 0:E * B * NT].rearrange("p (t e) -> p t e", e=E)
            step(v.tensor_tensor(c3, pick_all[:, :, :], total[:, 3].unsqueeze(1).to_broadcast([P, B * NT, E]), ALU.mult))
            step(v.tensor_reduce(slot_f[:, :], c3, AX.X, ALU.add))
            step(v.tensor_tensor(slot_f[:, :], slot_f[:, :], rank_all[:, :], ALU.add))
            v.tensor_copy(slot[:, :], slot_f[:, :]).then_inc(s_slot, 1)
            dve.wait_ge(s_slot, 1)
            c3 = cmp[:, 0:E * NS].rearrange("p (t e) -> p t e", e=E)
            step(v.tensor_tensor(c3, bcast(const("tiles"), E), total[:, 2].unsqueeze(1).to_broadcast([P, NS, E]), ALU.is_ge))
            step(v.tensor_reduce(expert_f[:, :], c3, AX.X, ALU.add))
            v.tensor_scalar(expert[:, :], expert_f[:, :], float(E - 1), None, ALU.min).then_inc(s_expert, 1)

            def products(i):
                for k in range(SG):
                    dve.wait_ge(s_ehc, i * SG + k + 1)
                    v.tensor_tensor(ehp[:, k, :], bank[1 + k][:, HID:2 * HID], ehc[:, k, :], ALU.mult).then_inc(s_ehp, 1)

            def turned_hidden(i):
                for k in range(SG // 2):
                    dve.wait_ge(s_eht, i * 2 + k + 1)
                    v.tensor_copy(eht[k], bank[5 + k][:, :]).then_inc(s_ehtc, 1)

            products(0)
            with dve.Fori(1, NG) as i:
                turned_hidden(i - 1)
                products(i)
            turned_hidden(NG - 1)
            for i in range(B):
                dve.wait_ge(s_yg[i % 2], 16 * NT * (i // 2 + 1))
                step(v.tensor_tensor(yg[i % 2][:, :, :], yg[i % 2][:, :, :],
                                     bcast(share_all[:, i * NT:(i + 1) * NT], D), ALU.mult))
                dve.wait_ge(s_pin, 16 * (i + 1))
                v.tensor_tensor(ob[:, :, :], ob[:, :, :], yg[i % 2][:, :, :], ALU.add).then_inc(s_fin, 1)


def _rope(width, t):
    import numpy as np
    inv = (1.0 / (np.float32(10000.0) ** (np.arange(0, width, 2, dtype=np.float32) / np.float32(width))))
    ang = np.arange(t, dtype=np.float32)[:, None] * inv.astype(np.float32)[None, :]
    ang = np.concatenate([ang, ang], axis=1)
    sign = np.concatenate([-np.ones(width // 2), np.ones(width // 2)]).astype(np.float32)
    cos, sin = np.cos(ang), np.sin(ang) * sign
    return np.tile(cos.T, (P // width, 1)), np.tile(sin.T, (P // width, 1))


def constants():
    import numpy as np
    i = np.arange(P)
    c = {}
    c["ident"] = np.eye(P)
    c["mask_qk"] = np.where(i[None, :] > i[:, None], -1e30, 0.0)
    c["mask_kq"] = c["mask_qk"].T
    c["upto"] = (i[None, :] >= i[:, None]) * 1.0
    c["ones"] = np.ones((P, P))
    c["quad"] = ((i[:, None] // LD) % G == np.arange(G)[None, :]) * 1.0
    c["diag"] = (i[:, None] // LD == (np.arange(LH * LV) // LV)[None, :]) * 1.0
    c["iota"] = np.tile(np.arange(E), (P, 1))
    c["less"] = c["iota"] - E
    c["steps"] = np.tile(np.arange(B * NT) * P, (P, 1))
    c["tiles"] = np.tile(np.arange(NS), (P, 1))
    c["cos_l"], c["sin_l"] = _rope(LD, T)
    c["cos_s"], c["sin_s"] = _rope(HD, T)
    return np.ascontiguousarray(np.concatenate([c[n] for n, _ in CONST], axis=1).astype(np.float32))


def kernel(**inputs):
    import numpy as np
    import concourse.bacc as bacc
    from concourse.bass_utils import run_bass_kernel_spmd

    g = {k: np.asarray(v) for k, v in inputs.items()}

    def exchanged(w, width):
        w = w.reshape(w.shape[0], -1, 2, width // 2)
        return w[:, :, ::-1, :].reshape(w.shape[0], -1)

    wq, wk = g["L0_attn_Wq"].T, g["L0_attn_Wk"].T
    w_lin = np.concatenate([wq, exchanged(wq, LD), wk, exchanged(wk, LD), g["L0_attn_Wv"].T, g["L0_attn_Wb"].T], axis=1)
    fq = g["L0_ffn_wq"].reshape(D, G, HKV, HD).transpose(0, 2, 1, 3).reshape(D, HQ * HD)
    fk = np.repeat(g["L0_ffn_wk"].reshape(D, HKV, 1, HD), 2, axis=2).reshape(D, 2 * HKV * HD)
    w_att = np.concatenate([fq, exchanged(fq, HD), fk, exchanged(fk, HD), g["L0_ffn_wv"]], axis=1)
    w_out = g["L0_ffn_wo"].reshape(G, HKV, HD, D).transpose(1, 0, 2, 3).reshape(HQ * HD, D)
    w_up = np.concatenate([g["L0_ffn_w1"], g["L0_ffn_w2"]], axis=2).transpose(1, 0, 2)
    rows = np.concatenate([g["L0_attn_bb"], g["L0_attn_bo"], g["L0_attn_scale"], g["L0_ffn_g2"], g["L0_ffn_router_b"]])
    arrays = {
        "x": g["L0_attn_x"], "w_lin": w_lin, "w_lout": g["L0_attn_Wo"].T, "w_att": w_att, "w_out": w_out,
        "w_up": w_up, "w_down": g["L0_ffn_w3"], "w_router": g["L0_ffn_router_w"],
        "g1": g["L0_ffn_g1"].reshape(D, 1), "rows": np.tile(rows[None, :], (P, 1)), "consts": constants(),
    }
    arrays = {k: np.ascontiguousarray(v) for k, v in arrays.items()}
    nc = bacc.Bacc("TRN2", target_bir_lowering=False, num_devices=1)
    args = [nc.dram_tensor(k, v.shape, mybir.dt.from_np(v.dtype), kind="ExternalInput").ap() for k, v in arrays.items()]
    args.append(nc.dram_tensor("out", (B, T, D), F32, kind="ExternalOutput").ap())
    attention_kernel(nc, *args)
    return run_bass_kernel_spmd(nc, [arrays], core_ids=[0]).results[0]["out"]
```
